# Optimizing a Trainium2 kernel written in Bass

```python
import numpy as np
import jax
import jax.numpy as jnp

def _softmax(x, axis=-1):
    return jax.nn.softmax(x, axis=axis)

def _gelu(x):
    return jax.nn.gelu(x, approximate=True)

def _silu(x):
    return jax.nn.silu(x)

def _sigmoid(x):
    return jax.nn.sigmoid(x)

def _layernorm(x, axis=-1, eps=1e-05):
    m = jnp.mean(x, axis=axis, keepdims=True)
    v = jnp.var(x, axis=axis, keepdims=True)
    return (x - m) / jnp.sqrt(v + eps)

def _scatter_add(tgt, idx, src, axis=0):
    return tgt.at[idx].add(src)

def _segment_sum(src, seg, n):
    return jax.ops.segment_sum(src, seg, n)
kernel_name = 'mk_gnn_ffn_d4_gnn_r32_eb5dc8'

def setup_inputs(seed: int=0):
    np.random.seed(seed)
    _w = jnp.asarray

    def _rec_inputs():
        import jax
        import jax.numpy as jnp
        _gk = jax.random.key(seed)
        x = -8.776e-05 + 1 * jax.random.normal(jax.random.fold_in(_gk, 1), (625, 256), jnp.float32)
        _s = jax.random.randint(jax.random.fold_in(_gk, 2), (10000,), 0, 625, jnp.int32)
        _d = jax.random.randint(jax.random.fold_in(_gk, 3), (10000,), 0, 625, jnp.int32)
        _loop = jnp.arange(625, dtype=jnp.int32)
        src = jnp.concatenate([_s, _d, _loop])
        dst = jnp.concatenate([_d, _s, _loop])
        _o = jnp.argsort(dst, stable=True)
        src = src[_o]
        dst = dst[_o]
        edge_weight = jax.random.uniform(jax.random.fold_in(_gk, 13), (20625,), jnp.float32, 0.0, 1)
        return (x, src, dst, edge_weight)
    x, src, dst, edge_weight = _rec_inputs()

    def _L0_gnn_setup():
        import jax, jax.numpy as jnp
        import numpy as np
        N = 625
        E = 10000
        IN = 256
        HID = 512
        OUT = 256
        H = 4
        C1 = HID // 2 // H
        NEG_SLOPE = 0.2

        def gat_conv(x, src, dst, W, a_s, a_d, b, heads, ch):
            h = (x @ W).reshape(-1, heads, ch)
            al_s = jnp.einsum('nhc,hc->nh', h, a_s)
            al_d = jnp.einsum('nhc,hc->nh', h, a_d)
            e = jax.nn.leaky_relu(al_s[src] + al_d[dst], NEG_SLOPE)
            m = jax.ops.segment_max(e, dst, num_segments=N)
            ex = jnp.exp(e - m[dst])
            denom = jax.ops.segment_sum(ex, dst, num_segments=N)
            alpha = ex / denom[dst]
            out = jax.ops.segment_sum(alpha[:, :, None] * h[src], dst, num_segments=N)
            return out.reshape(-1, heads * ch) + b
        key = jax.random.key(seed)
        ks = jax.random.split(key, 10)
        s = 0.1
        return {'x': jax.random.normal(ks[0], (N, IN), jnp.float32), 'edge_index': jax.random.randint(ks[1], (2, E), 0, N, dtype=jnp.int64), 'W1': jax.random.normal(ks[2], (IN, H * C1), jnp.float32) * s, 'att_src1': jax.random.normal(ks[3], (H, C1), jnp.float32) * s, 'att_dst1': jax.random.normal(ks[4], (H, C1), jnp.float32) * s, 'b1': jax.random.normal(ks[5], (H * C1,), jnp.float32) * s, 'W2': jax.random.normal(ks[6], (H * C1, OUT), jnp.float32) * s, 'att_src2': jax.random.normal(ks[7], (1, OUT), jnp.float32) * s, 'att_dst2': jax.random.normal(ks[8], (1, OUT), jnp.float32) * s, 'b2': jax.random.normal(ks[9], (OUT,), jnp.float32) * s}
    _L0_gnn_all = _L0_gnn_setup()
    _L0_gnn_in = {k: v for k, v in _L0_gnn_all.items() if k in ('W1', 'att_src1', 'att_dst1', 'b1', 'W2', 'att_src2', 'att_dst2', 'b2')}
    del _L0_gnn_all

    def _L0_ffn_setup():
        import math
        import jax, jax.numpy as jnp
        import numpy as np
        CAPACITY_FACTOR = 1.25
        key = jax.random.key(seed)
        ks = jax.random.split(key, 5)
        B, L, D, F, E = (8, 256, 256, 1024, 8)
        h = jax.random.normal(ks[0], (B, L, D), dtype=jnp.float32)
        gate_w = jax.random.normal(ks[1], (D, E), dtype=jnp.float32) * 0.02
        gate_b = jnp.zeros((E,), dtype=jnp.float32)
        w1 = jax.random.normal(ks[2], (E, D, F), dtype=jnp.float32) * (1.0 / math.sqrt(D))
        b1 = jnp.zeros((E, F), dtype=jnp.float32)
        w2 = jax.random.normal(ks[3], (E, F, D), dtype=jnp.float32) * (1.0 / math.sqrt(F))
        b2 = jnp.zeros((E, D), dtype=jnp.float32)
        return {'h': h, 'gate_w': gate_w, 'gate_b': gate_b, 'w1': w1, 'b1': b1, 'w2': w2, 'b2': b2}
    _L0_ffn_all = _L0_ffn_setup()
    _L0_ffn_in = {k: v for k, v in _L0_ffn_all.items() if k in ('gate_w', 'gate_b', 'w1', 'b1', 'w2', 'b2')}
    del _L0_ffn_all

    def _L1_gnn_setup():
        import jax, jax.numpy as jnp
        import numpy as np
        N_NODES = 3125
        key = jax.random.key(seed)
        ks = jax.random.split(key, 5)
        features = jax.random.normal(ks[0], (N_NODES, 256), dtype=jnp.float32)
        src = jax.random.randint(ks[1], (50000,), 0, N_NODES, dtype=jnp.int32)
        dst = jax.random.randint(ks[2], (50000,), 0, N_NODES, dtype=jnp.int32)
        W_gcn = jax.random.normal(ks[3], (256, 64), dtype=jnp.float32) * (1.0 / np.sqrt(256))
        b_gcn = jnp.zeros((64,), dtype=jnp.float32)
        W_out = jax.random.normal(ks[4], (64, 256), dtype=jnp.float32) * (1.0 / np.sqrt(64))
        b_out = jnp.zeros((256,), dtype=jnp.float32)
        return {'features': features, 'src': src, 'dst': dst, 'W_gcn': W_gcn, 'b_gcn': b_gcn, 'W_out': W_out, 'b_out': b_out}
    _L1_gnn_all = _L1_gnn_setup()
    _L1_gnn_in = {k: v for k, v in _L1_gnn_all.items() if k in ('W_gcn', 'b_gcn', 'W_out', 'b_out')}
    del _L1_gnn_all

    def _L1_ffn_setup():
        import jax, jax.numpy as jnp
        import numpy as np
        D_IN, D_HID, D_OUT = (256, 512, 256)
        N_EXPERTS, TOP_K = (64, 2)
        B, S = (8, 128)
        key = jax.random.key(seed)
        ks = jax.random.split(key, 8)
        scale_in = 1.0 / np.sqrt(D_IN)
        scale_hid = 1.0 / np.sqrt(D_HID)
        return {'x': jax.random.normal(ks[0], (B, S, D_IN), dtype=jnp.float32), 'Wr': jax.random.uniform(ks[1], (D_IN, N_EXPERTS), jnp.float32, -scale_in, scale_in), 'br': jax.random.uniform(ks[2], (N_EXPERTS,), jnp.float32, -scale_in, scale_in), 'W1': jax.random.uniform(ks[3], (N_EXPERTS, D_IN, D_HID), jnp.float32, -scale_in, scale_in), 'b1': jax.random.uniform(ks[4], (N_EXPERTS, D_HID), jnp.float32, -scale_in, scale_in), 'W2': jax.random.uniform(ks[5], (N_EXPERTS, D_HID, D_OUT), jnp.float32, -scale_hid, scale_hid), 'b2': jax.random.uniform(ks[6], (N_EXPERTS, D_OUT), jnp.float32, -scale_hid, scale_hid)}
    _L1_ffn_all = _L1_ffn_setup()
    _L1_ffn_in = {k: v for k, v in _L1_ffn_all.items() if k in ('Wr', 'br', 'W1', 'b1', 'W2', 'b2')}
    del _L1_ffn_all

    def _L2_gnn_setup():
        import jax, jax.numpy as jnp
        import numpy as np
        N, F, H, C = (50000, 256, 4, 64)
        E = 25000
        NEG_SLOPE = 0.2
        LN_EPS = 1e-05
        key = jax.random.key(seed)
        ks = jax.random.split(key, 8)
        x = jax.random.normal(ks[0], (N, F), dtype=jnp.float32)
        edge_index = jax.random.randint(ks[1], (2, E), 0, N, dtype=jnp.int32)
        W = jax.random.normal(ks[2], (F, H * C), dtype=jnp.float32) / np.sqrt(F)
        att_src = jax.random.normal(ks[3], (H, C), dtype=jnp.float32) / np.sqrt(C)
        att_dst = jax.random.normal(ks[4], (H, C), dtype=jnp.float32) / np.sqrt(C)
        bias = jnp.zeros((H * C,), dtype=jnp.float32)
        gamma = jnp.ones((H * C,), dtype=jnp.float32)
        beta = jnp.zeros((H * C,), dtype=jnp.float32)
        return {'x': x, 'edge_index': edge_index, 'W': W, 'att_src': att_src, 'att_dst': att_dst, 'bias': bias, 'gamma': gamma, 'beta': beta}
    _L2_gnn_all = _L2_gnn_setup()
    _L2_gnn_in = {k: v for k, v in _L2_gnn_all.items() if k in ('W', 'att_src', 'att_dst', 'bias', 'gamma', 'beta')}
    del _L2_gnn_all

    def _L2_ffn_setup():
        import jax, jax.numpy as jnp
        import numpy as np
        BN_EPS = 0.001

        def _bn(h, g, b, m, v):
            return g * (h - m) * jax.lax.rsqrt(v + BN_EPS) + b
        key = jax.random.key(seed)
        ks = jax.random.split(key, 8)
        B, F, Df = (256, 64, 256)
        E, H, D = (8, 256, 256)
        s1 = 1.0 / np.sqrt(Df)
        s2 = 1.0 / np.sqrt(H)
        return {'x': jax.random.normal(ks[0], (B, F, Df), jnp.float32), 'Wr': jax.random.normal(ks[1], (Df, E), jnp.float32) * s1, 'br': jnp.zeros((E,), jnp.float32), 'W1': jax.random.normal(ks[2], (E, Df, H), jnp.float32) * s1, 'b1': jnp.zeros((E, H), jnp.float32), 'g1': jnp.ones((E, H), jnp.float32), 'be1': jnp.zeros((E, H), jnp.float32), 'm1': jnp.zeros((E, H), jnp.float32), 'v1': jnp.ones((E, H), jnp.float32), 'W2': jax.random.normal(ks[3], (E, H, H), jnp.float32) * s2, 'b2': jnp.zeros((E, H), jnp.float32), 'g2': jnp.ones((E, H), jnp.float32), 'be2': jnp.zeros((E, H), jnp.float32), 'm2': jnp.zeros((E, H), jnp.float32), 'v2': jnp.ones((E, H), jnp.float32), 'Wo': jax.random.normal(ks[4], (E, H, D), jnp.float32) * s2, 'bo': jnp.zeros((E, D), jnp.float32)}
    _L2_ffn_all = _L2_ffn_setup()
    _L2_ffn_in = {k: v for k, v in _L2_ffn_all.items() if k in ('Wr', 'br', 'W1', 'b1', 'g1', 'be1', 'm1', 'v1', 'W2', 'b2', 'g2', 'be2', 'm2', 'v2', 'Wo', 'bo')}
    del _L2_ffn_all

    def _L3_gnn_setup():
        import jax, jax.numpy as jnp
        import numpy as np
        N_NODES = 3125
        N_EDGES = 100000
        D_IN = 256
        D_OUT = 256
        key = jax.random.key(seed)
        k1, k2, k3, k4, k5 = jax.random.split(key, 5)
        inputs = jax.random.normal(k1, (N_NODES, D_IN), dtype=jnp.float32)
        init_range = np.sqrt(6.0 / (D_IN + D_OUT)).astype(np.float32)
        weight = jax.random.uniform(k2, (D_IN, D_OUT), dtype=jnp.float32, minval=-init_range, maxval=init_range)
        edge_src = jax.random.randint(k3, (N_EDGES,), 0, N_NODES, dtype=jnp.int32)
        edge_dst = jax.random.randint(k4, (N_EDGES,), 0, N_NODES, dtype=jnp.int32)
        edge_vals = jax.random.uniform(k5, (N_EDGES,), dtype=jnp.float32)
        return {'inputs': inputs, 'weight': weight, 'edge_src': edge_src, 'edge_dst': edge_dst, 'edge_vals': edge_vals}
    _L3_gnn_all = _L3_gnn_setup()
    _L3_gnn_in = {k: v for k, v in _L3_gnn_all.items() if k in ('weight',)}
    del _L3_gnn_all

    def _L3_ffn_setup():
        import jax, jax.numpy as jnp
        import numpy as np
        NUM_EXPERTS = 8
        TOP_K = 2
        B, S, D = (8, 256, 256)

        def _moe(tokens, router_w, w1, b1, w2, b2):
            N = tokens.shape[0]
            E = router_w.shape[0]
            logits = tokens.astype(jnp.float32) @ router_w.astype(jnp.float32).T
            probs = jax.nn.softmax(logits, axis=-1)
            rw, re = jax.lax.top_k(probs, TOP_K)
            if TOP_K > 1:
                rw = rw / jnp.maximum(rw.sum(-1, keepdims=True), 1e-12)
            rw = rw.astype(tokens.dtype)
            combine = jnp.zeros((N, E), tokens.dtype).at[jnp.arange(N)[:, None], re].set(rw)
            out = tokens
            for e in range(E):
                h = jax.nn.gelu(tokens @ w1[e] + b1[e], approximate=False)
                y = h @ w2[e] + b2[e]
                out = out + combine[:, e:e + 1] * y
            return out
        key = jax.random.key(seed)
        ks = jax.random.split(key, 4)
        scale = 1.0 / np.sqrt(D).astype(np.float32)
        return {'input_embeddings': jax.random.normal(ks[0], (B, S, D), jnp.float32), 'router_w': jax.random.normal(ks[1], (NUM_EXPERTS, D), jnp.float32) * scale, 'w1': jax.random.normal(ks[2], (NUM_EXPERTS, D, D), jnp.float32) * scale, 'b1': jnp.zeros((NUM_EXPERTS, D), jnp.float32), 'w2': jax.random.normal(ks[3], (NUM_EXPERTS, D, D), jnp.float32) * scale, 'b2': jnp.zeros((NUM_EXPERTS, D), jnp.float32)}
    _L3_ffn_all = _L3_ffn_setup()
    _L3_ffn_in = {k: v for k, v in _L3_ffn_all.items() if k in ('router_w', 'w1', 'b1', 'w2', 'b2')}
    del _L3_ffn_all
    return {'x': x, 'src': src, 'dst': dst, 'edge_weight': edge_weight, 'L0_gnn_W1': _L0_gnn_in['W1'], 'L0_gnn_att_src1': _L0_gnn_in['att_src1'], 'L0_gnn_att_dst1': _L0_gnn_in['att_dst1'], 'L0_gnn_b1': _L0_gnn_in['b1'], 'L0_gnn_W2': _L0_gnn_in['W2'], 'L0_gnn_att_src2': _L0_gnn_in['att_src2'], 'L0_gnn_att_dst2': _L0_gnn_in['att_dst2'], 'L0_gnn_b2': _L0_gnn_in['b2'], 'L0_ffn_gate_w': _L0_ffn_in['gate_w'], 'L0_ffn_gate_b': _L0_ffn_in['gate_b'], 'L0_ffn_w1': _L0_ffn_in['w1'], 'L0_ffn_b1': _L0_ffn_in['b1'], 'L0_ffn_w2': _L0_ffn_in['w2'], 'L0_ffn_b2': _L0_ffn_in['b2'], 'L1_gnn_W_gcn': _L1_gnn_in['W_gcn'], 'L1_gnn_b_gcn': _L1_gnn_in['b_gcn'], 'L1_gnn_W_out': _L1_gnn_in['W_out'], 'L1_gnn_b_out': _L1_gnn_in['b_out'], 'L1_ffn_Wr': _L1_ffn_in['Wr'], 'L1_ffn_br': _L1_ffn_in['br'], 'L1_ffn_W1': _L1_ffn_in['W1'], 'L1_ffn_b1': _L1_ffn_in['b1'], 'L1_ffn_W2': _L1_ffn_in['W2'], 'L1_ffn_b2': _L1_ffn_in['b2'], 'L2_gnn_W': _L2_gnn_in['W'], 'L2_gnn_att_src': _L2_gnn_in['att_src'], 'L2_gnn_att_dst': _L2_gnn_in['att_dst'], 'L2_gnn_bias': _L2_gnn_in['bias'], 'L2_gnn_gamma': _L2_gnn_in['gamma'], 'L2_gnn_beta': _L2_gnn_in['beta'], 'L2_ffn_Wr': _L2_ffn_in['Wr'], 'L2_ffn_br': _L2_ffn_in['br'], 'L2_ffn_W1': _L2_ffn_in['W1'], 'L2_ffn_b1': _L2_ffn_in['b1'], 'L2_ffn_g1': _L2_ffn_in['g1'], 'L2_ffn_be1': _L2_ffn_in['be1'], 'L2_ffn_m1': _L2_ffn_in['m1'], 'L2_ffn_v1': _L2_ffn_in['v1'], 'L2_ffn_W2': _L2_ffn_in['W2'], 'L2_ffn_b2': _L2_ffn_in['b2'], 'L2_ffn_g2': _L2_ffn_in['g2'], 'L2_ffn_be2': _L2_ffn_in['be2'], 'L2_ffn_m2': _L2_ffn_in['m2'], 'L2_ffn_v2': _L2_ffn_in['v2'], 'L2_ffn_Wo': _L2_ffn_in['Wo'], 'L2_ffn_bo': _L2_ffn_in['bo'], 'L3_gnn_weight': _L3_gnn_in['weight'], 'L3_ffn_router_w': _L3_ffn_in['router_w'], 'L3_ffn_w1': _L3_ffn_in['w1'], 'L3_ffn_b1': _L3_ffn_in['b1'], 'L3_ffn_w2': _L3_ffn_in['w2'], 'L3_ffn_b2': _L3_ffn_in['b2']}

def reference(x, src, dst, edge_weight, L0_gnn_W1, L0_gnn_att_src1, L0_gnn_att_dst1, L0_gnn_b1, L0_gnn_W2, L0_gnn_att_src2, L0_gnn_att_dst2, L0_gnn_b2, L0_ffn_gate_w, L0_ffn_gate_b, L0_ffn_w1, L0_ffn_b1, L0_ffn_w2, L0_ffn_b2, L1_gnn_W_gcn, L1_gnn_b_gcn, L1_gnn_W_out, L1_gnn_b_out, L1_ffn_Wr, L1_ffn_br, L1_ffn_W1, L1_ffn_b1, L1_ffn_W2, L1_ffn_b2, L2_gnn_W, L2_gnn_att_src, L2_gnn_att_dst, L2_gnn_bias, L2_gnn_gamma, L2_gnn_beta, L2_ffn_Wr, L2_ffn_br, L2_ffn_W1, L2_ffn_b1, L2_ffn_g1, L2_ffn_be1, L2_ffn_m1, L2_ffn_v1, L2_ffn_W2, L2_ffn_b2, L2_ffn_g2, L2_ffn_be2, L2_ffn_m2, L2_ffn_v2, L2_ffn_Wo, L2_ffn_bo, L3_gnn_weight, L3_ffn_router_w, L3_ffn_w1, L3_ffn_b1, L3_ffn_w2, L3_ffn_b2):
    import jax
    import jax.numpy as jnp

    def _L0_gnn_ref(x, edge_index, W1, att_src1, att_dst1, b1, W2, att_src2, att_dst2, b2):
        import jax, jax.numpy as jnp
        import numpy as np
        N = 625
        E = 10000
        IN = 256
        HID = 512
        OUT = 256
        H = 4
        C1 = HID // 2 // H
        NEG_SLOPE = 0.2

        def gat_conv(x, src, dst, W, a_s, a_d, b, heads, ch):
            h = (x @ W).reshape(-1, heads, ch)
            al_s = jnp.einsum('nhc,hc->nh', h, a_s)
            al_d = jnp.einsum('nhc,hc->nh', h, a_d)
            e = jax.nn.leaky_relu(al_s[src] + al_d[dst], NEG_SLOPE)
            m = jax.ops.segment_max(e, dst, num_segments=N)
            ex = jnp.exp(e - m[dst])
            denom = jax.ops.segment_sum(ex, dst, num_segments=N)
            alpha = ex / denom[dst]
            out = jax.ops.segment_sum(alpha[:, :, None] * h[src], dst, num_segments=N)
            return out.reshape(-1, heads * ch) + b
        loop = jnp.arange(N, dtype=edge_index.dtype)
        src = jnp.concatenate([edge_index[0], loop])
        dst = jnp.concatenate([edge_index[1], loop])
        h1 = jax.nn.relu(gat_conv(x, src, dst, W1, att_src1, att_dst1, b1, H, C1))
        return gat_conv(h1, src, dst, W2, att_src2, att_dst2, b2, 1, OUT)

    def _L0_ffn_ref(h, gate_w, gate_b, w1, b1, w2, b2):
        import math
        import jax, jax.numpy as jnp
        import numpy as np
        CAPACITY_FACTOR = 1.25
        B, L, D = h.shape
        E = gate_w.shape[1]
        T = B * L
        C = max(1, math.ceil(CAPACITY_FACTOR * T / E))
        x = h.reshape(T, D)
        logits = x @ gate_w + gate_b
        probs = jax.nn.softmax(logits, axis=-1)
        idx = jnp.argmax(probs, axis=-1)
        prb = jnp.take_along_axis(probs, idx[:, None], axis=1)[:, 0]
        one_hot = jax.nn.one_hot(idx, E, dtype=jnp.float32)
        pos = (jnp.cumsum(one_hot, axis=0) * one_hot).sum(-1).astype(jnp.int32) - 1
        kept = pos < C
        pos_safe = jnp.where(kept, pos, C)
        buf = jnp.zeros((E, C, D), dtype=h.dtype).at[idx, pos_safe].set(x, mode='drop')
        hmid = jax.nn.relu(jnp.einsum('ecd,edf->ecf', buf, w1) + b1[:, None, :])
        ybuf = jnp.einsum('ecf,efd->ecd', hmid, w2) + b2[:, None, :]
        pos_g = jnp.minimum(pos, C - 1)
        y_tok = ybuf[idx, pos_g] * (prb * kept)[:, None]
        y = y_tok.reshape(B, L, D)
        y = jnp.nan_to_num(y, nan=0.0, posinf=10000.0, neginf=-10000.0)
        return y

    def _L1_gnn_ref(features, src, dst, W_gcn, b_gcn, W_out, b_out):
        import jax, jax.numpy as jnp
        import numpy as np
        N_NODES = 3125
        n = features.shape[0]
        ones = jnp.ones(src.shape[0], dtype=features.dtype)
        out_deg = jax.ops.segment_sum(ones, src, num_segments=n)
        in_deg = jax.ops.segment_sum(ones, dst, num_segments=n)
        norm_src = jax.lax.rsqrt(jnp.maximum(out_deg, 1.0))[:, None]
        norm_dst = jax.lax.rsqrt(jnp.maximum(in_deg, 1.0))[:, None]
        x = features * norm_src @ W_gcn
        msg = x[src]
        agg = jax.ops.segment_sum(msg, dst, num_segments=n)
        h = agg * norm_dst + b_gcn
        h = jax.nn.relu(h)
        return h @ W_out + b_out

    def _L1_ffn_ref(x, Wr, br, W1, b1, W2, b2):
        import jax, jax.numpy as jnp
        import numpy as np
        D_IN, D_HID, D_OUT = (256, 512, 256)
        N_EXPERTS, TOP_K = (64, 2)
        B, S = (8, 128)
        Bx, Sx, D = x.shape
        xf = x.reshape(-1, D)
        T = xf.shape[0]
        E = Wr.shape[1]
        logits = xf @ Wr + br
        topk_logits, topk_idx = jax.lax.top_k(logits, TOP_K)
        gates = jax.nn.softmax(topk_logits, axis=1)
        combine = jnp.zeros((T, E), xf.dtype).at[jnp.arange(T)[:, None], topk_idx].add(gates)
        out = jnp.zeros((T, W2.shape[-1]), xf.dtype)
        for e in range(E):
            h = jax.nn.relu(xf @ W1[e] + b1[e])
            y = h @ W2[e] + b2[e]
            out = out + combine[:, e:e + 1] * y
        return out.reshape(Bx, Sx, -1)

    def _L2_gnn_ref(x, edge_index, W, att_src, att_dst, bias, gamma, beta):
        import jax, jax.numpy as jnp
        import numpy as np
        N, F, H, C = (50000, 256, 4, 64)
        E = 25000
        NEG_SLOPE = 0.2
        LN_EPS = 1e-05
        n = x.shape[0]
        loops = jnp.arange(n, dtype=edge_index.dtype)
        src = jnp.concatenate([edge_index[0], loops])
        dst = jnp.concatenate([edge_index[1], loops])
        h = (x @ W).reshape(n, H, C)
        a_src = jnp.einsum('nhc,hc->nh', h, att_src)
        a_dst = jnp.einsum('nhc,hc->nh', h, att_dst)
        alpha = a_src[src] + a_dst[dst]
        alpha = jnp.where(alpha >= 0, alpha, NEG_SLOPE * alpha)
        seg_max = jax.ops.segment_max(alpha, dst, num_segments=n)
        alpha = jnp.exp(alpha - seg_max[dst])
        seg_sum = jax.ops.segment_sum(alpha, dst, num_segments=n)
        alpha = alpha / (seg_sum[dst] + 1e-16)
        msg = h[src] * alpha[:, :, None]
        out = jax.ops.segment_sum(msg, dst, num_segments=n)
        out = out.reshape(n, H * C) + bias
        mu = jnp.mean(out, axis=-1, keepdims=True)
        var = jnp.var(out, axis=-1, keepdims=True)
        out = (out - mu) * jax.lax.rsqrt(var + LN_EPS) * gamma + beta
        return out

    def _L2_ffn_ref(x, Wr, br, W1, b1, g1, be1, m1, v1, W2, b2, g2, be2, m2, v2, Wo, bo):
        import jax, jax.numpy as jnp
        import numpy as np
        BN_EPS = 0.001

        def _bn(h, g, b, m, v):
            return g * (h - m) * jax.lax.rsqrt(v + BN_EPS) + b
        feat = jnp.mean(x, axis=0)
        w = jax.nn.softmax(feat @ Wr + br, axis=-1)
        h = jnp.einsum('bfd,edh->bfeh', x, W1) + b1
        h = jax.nn.relu(_bn(h, g1, be1, m1, v1))
        h = jnp.einsum('bfeh,ehk->bfek', h, W2) + b2
        h = jax.nn.relu(_bn(h, g2, be2, m2, v2))
        y = jnp.einsum('bfeh,ehd->bfed', h, Wo) + bo
        return jnp.einsum('bfed,fe->bfd', y, w)

    def _L3_gnn_ref(inputs, weight, edge_src, edge_dst, edge_vals):
        import jax, jax.numpy as jnp
        import numpy as np
        N_NODES = 3125
        N_EDGES = 100000
        D_IN = 256
        D_OUT = 256
        x = inputs @ weight
        msgs = edge_vals[:, None] * x[edge_src]
        out = jax.ops.segment_sum(msgs, edge_dst, num_segments=inputs.shape[0])
        return jax.nn.relu(out)

    def _L3_ffn_ref(input_embeddings, router_w, w1, b1, w2, b2):
        import jax, jax.numpy as jnp
        import numpy as np
        NUM_EXPERTS = 8
        TOP_K = 2
        B, S, D = (8, 256, 256)

        def _moe(tokens, router_w, w1, b1, w2, b2):
            N = tokens.shape[0]
            E = router_w.shape[0]
            logits = tokens.astype(jnp.float32) @ router_w.astype(jnp.float32).T
            probs = jax.nn.softmax(logits, axis=-1)
            rw, re = jax.lax.top_k(probs, TOP_K)
            if TOP_K > 1:
                rw = rw / jnp.maximum(rw.sum(-1, keepdims=True), 1e-12)
            rw = rw.astype(tokens.dtype)
            combine = jnp.zeros((N, E), tokens.dtype).at[jnp.arange(N)[:, None], re].set(rw)
            out = tokens
            for e in range(E):
                h = jax.nn.gelu(tokens @ w1[e] + b1[e], approximate=False)
                y = h @ w2[e] + b2[e]
                out = out + combine[:, e:e + 1] * y
            return out
        b, s, d = input_embeddings.shape
        tokens = input_embeddings.reshape(b * s, d)
        return _moe(tokens, router_w, w1, b1, w2, b2).reshape(b, s, d)
    edge_index = jnp.stack([src, dst])
    x = x + _L0_gnn_ref(_layernorm(x, axis=-1), edge_index, L0_gnn_W1, L0_gnn_att_src1, L0_gnn_att_dst1, L0_gnn_b1, L0_gnn_W2, L0_gnn_att_src2, L0_gnn_att_dst2, L0_gnn_b2)
    x = x + _L0_ffn_ref(_layernorm(x, axis=-1)[None], L0_ffn_gate_w, L0_ffn_gate_b, L0_ffn_w1, L0_ffn_b1, L0_ffn_w2, L0_ffn_b2)[0]
    x = x + _L1_gnn_ref(_layernorm(x, axis=-1), src, dst, L1_gnn_W_gcn, L1_gnn_b_gcn, L1_gnn_W_out, L1_gnn_b_out)
    x = x + _L1_ffn_ref(_layernorm(x, axis=-1)[None], L1_ffn_Wr, L1_ffn_br, L1_ffn_W1, L1_ffn_b1, L1_ffn_W2, L1_ffn_b2)[0]
    x = x + _L2_gnn_ref(_layernorm(x, axis=-1), edge_index, L2_gnn_W, L2_gnn_att_src, L2_gnn_att_dst, L2_gnn_bias, L2_gnn_gamma, L2_gnn_beta)
    x = x + _L2_ffn_ref(_layernorm(x, axis=-1)[None], L2_ffn_Wr, L2_ffn_br, L2_ffn_W1, L2_ffn_b1, L2_ffn_g1, L2_ffn_be1, L2_ffn_m1, L2_ffn_v1, L2_ffn_W2, L2_ffn_b2, L2_ffn_g2, L2_ffn_be2, L2_ffn_m2, L2_ffn_v2, L2_ffn_Wo, L2_ffn_bo)[0]
    x = x + _L3_gnn_ref(_layernorm(x, axis=-1), L3_gnn_weight, src, dst, edge_weight)
    x = x + _L3_ffn_ref(_layernorm(x, axis=-1)[None], L3_ffn_router_w, L3_ffn_w1, L3_ffn_b1, L3_ffn_w2, L3_ffn_b2)[0]
    return x

_drawn_inputs = setup_inputs


def setup_inputs(seed=0):
    import zlib

    import numpy as np

    out = dict(_drawn_inputs(seed))
    spreads = {'L0_ffn_gate_b': (0.0, 0.1),
     'L0_ffn_b1': (0.0, 0.707),
     'L0_ffn_b2': (0.0, 0.456),
     'L1_gnn_b_gcn': (0.0, 0.1),
     'L1_gnn_b_out': (0.0, 0.1),
     'L2_gnn_bias': (0.0, 0.1),
     'L2_gnn_gamma': (1.0, 0.2),
     'L2_gnn_beta': (0.0, 0.1),
     'L2_ffn_br': (0.0, 0.641),
     'L2_ffn_b1': (0.0, 0.517),
     'L2_ffn_g1': (1.0, 0.2),
     'L2_ffn_be1': (0.0, 0.579),
     'L2_ffn_m1': (0.0, 0.512),
     'L2_ffn_v1': (1.0, 0.6),
     'L2_ffn_b2': (0.0, 0.332),
     'L2_ffn_g2': (1.0, 0.2),
     'L2_ffn_be2': (0.0, 0.394),
     'L2_ffn_m2': (0.0, 0.319),
     'L2_ffn_v2': (1.0, 0.6),
     'L2_ffn_bo': (0.0, 0.1),
     'L3_ffn_b1': (0.0, 0.8),
     'L3_ffn_b2': (0.0, 0.8)}
    factors = {'L0_gnn_att_dst2': 2.903, 'L1_ffn_br': 3.501, 'L1_ffn_b1': 8.0, 'L1_ffn_b2': 5.362}
    for name, (base, spread) in spreads.items():
        noise = np.random.default_rng([zlib.crc32(name.encode()), seed]).standard_normal(out[name].shape)
        drawn = base * np.exp(spread * noise) if base else spread * noise
        out[name] = jnp.asarray(drawn.astype(out[name].dtype))
    for name, factor in factors.items():
        out[name] = (out[name] * factor).astype(out[name].dtype)
    return out
```

```python
from contextlib import ExitStack

import concourse.bass as bass
from concourse import mybir

F32 = mybir.dt.float32
I32 = mybir.dt.int32
U32 = mybir.dt.uint32
BF16 = mybir.dt.bfloat16
F16 = mybir.dt.float16
ALU = mybir.AluOpType
ACT = mybir.ActivationFunctionType
AX = mybir.AxisListType.X

N, D, E = 625, 256, 20625
P, NT = 125, 5
KD = D // 128
EPP = E // P
CH = 11
CHE = CH * P
NCHUNK = E // CHE
WB = 32
NBLK = (N + WB - 1) // WB
NPAD = NBLK * WB
LN_EPS, BN_EPS, SLOPE = 1e-5, 1e-3, 0.2
NEG = -1e30
E0, F0, CAP = 8, 1024, 98
E1, F1 = 64, 512
SLOTS = 2 * N
WIN = 96
ROUNDS = (N + WIN - 1) // WIN
E2 = 8
CHUNK = 2048
RING = 8
FLT_MAX = 3.4028235e38
PARAMS = 36


TAGS = ("l0g", "l0a", "l0m", "l0b", "l0f", "l1g", "l1f", "l2g", "l2a", "l2n", "l2f", "l3g", "l3f")
NORMS = ("l0g", "l0f", "l1g", "l1f", "l2g", "l2n", "l2f", "l3g", "l3f")
TURNS = ("l0g", "l0m", "l0f", "l1g", "l1f", "l2g", "l2f", "l3g", "l3f")
ATTS = ("l0a", "l0b", "l2a")
HEADS = {"l0a": 4, "l0b": 1, "l2a": 4}
RECURRING = {k: (NORMS, 1) for k in ("var", "rstd", "xln")}
RECURRING |= {k: (TURNS, 1) for k in ("turned0", "turned1", "xT0", "xT1")}
RECURRING |= {k: (ATTS, NT) for k in ("proj", "hs", "al")}
RECURRING |= {k: (ATTS, 1) for k in ("ones", "rows")}
RECURRING |= {k: (ATTS, HEADS) for k in ("bc", "r1", "r2", "u", "v", "max", "p")}
RECURRING |= {"masked": (ATTS, {t: n * NT for t, n in HEADS.items()})}
RECURRING |= {k: (ATTS, {"l0a": 4, "l0b": NT, "l2a": 4}) for k in ("agg", "out")}
RECURRING |= {"logits": (("l0f", "l1f", "l2f", "l3f"), 1), "onehot": (("l0f", "l1f"), 1)}
RECURRING |= {k: (("l0f", "l2f", "l3f"), 1) for k in ("wturned", "wT")}
RECURRING |= {k: (("l0f", "l2f", "l3f"), NT) for k in ("bias", "bias_out")}
RECURRING |= {k: (("l2f", "l3f"), 1) for k in ("shift", "exp", "w")}
RECURRING |= {"hidden": (("l2f", "l3f"), {"l2f": 2 * KD * E2, "l3f": KD * E2})}
RECURRING |= {"act": (("l2f", "l3f"), {"l2f": 2 * KD * E2 + 2, "l3f": KD * E2 + 2})}
RECURRING |= {"y": (("l2f", "l3f"), NT * E2), "y_free": (("l2f", "l3f"), NT * E2 + 2)}

ONCE = {
    "dve_stage": ("pack_ready", "base_ready", "bn_var_ready", "bn_ready", "params_used", "outdeg_ready", "flag_ready",
                  "graph_ready", "at_ready", "row_added", "l0a_done", "zrow_ready", "shift0_ready", "slots0_ready", "bufT1",
                  "ysb_ready", "deg_ready", "gcn_ones", "indeg_ready", "gcn_scaled", "shift1_ready", "cntcol_ready",
                  "slots1_ready", "flag2_ready", "yT_ready", "l1_experts_done", "ys_ready", "x_final"),
    "pe_stage": ("base_sum", "params_acc", "total_sum", "l0_ranks", "bufs_turned0", "bufs_turned1", "gcn_agg",
                 "gcn_turned", "l1_ranks", "l1_offsets"),
    "act_stage": ("params_turned", "at_copied", "exp0_ready", "bufT0", "gcn_hT", "exp1_ready"),
    "pool_stage": ("iota_ready", "consts_ready", "bn_pow_ready", "nsrc_ready", "ndst_ready"),
}
STAGE_OF = {name: (sem, n) for sem, names in ONCE.items() for n, name in enumerate(names)}


class Steps:

    def __init__(self, sem):
        self.sem, self.n = sem, 0

    def done(self, ins):
        ins.then_inc(self.sem, 1)
        self.n += 1

    def wait(self, eng):
        eng.wait_ge(self.sem, self.n)


def build(nc, a, out, stages=8):
    with ExitStack() as ctx:
        def sb(name, shape, dt=F32):
            return ctx.enter_context(nc.sbuf_tensor(name, shape, dt))

        def pb(name, shape, dt=F32):
            return ctx.enter_context(nc.psum_tensor(name, shape, dt))

        sems = {}

        def S(name):
            if name[:3] in TAGS and name[4:] in RECURRING:
                name = "each_" + name[4:]
            elif name in STAGE_OF:
                name = STAGE_OF[name][0]
            if name not in sems:
                sems[name] = ctx.enter_context(nc.semaphore(name))
            return sems[name]

        def reached(name, count):
            tag, kind = name[:3], name[4:]
            if tag in TAGS and kind in RECURRING:
                order, per = RECURRING[kind]
                for t in order[:order.index(tag)]:
                    count = count + (per[t] if isinstance(per, dict) else per)
            elif name in STAGE_OF:
                count = count + STAGE_OF[name][1]
            return S(name), count

        edges_d = nc.dram_tensor("edges_d", (E, 5), F32, kind="Internal").ap()
        buf_d = nc.dram_tensor("buf_d", (E0 * CAP + N, D), F32, kind="Internal").ap()
        ybuf_d = nc.dram_tensor("ybuf_d", (E0 * CAP, D), F32, kind="Internal").ap()
        xs_d = nc.dram_tensor("xs_d", (SLOTS, D), F32, kind="Internal").ap()
        ys_d = nc.dram_tensor("ys_d", (SLOTS, D), F32, kind="Internal").ap()

        x = sb("x", [P, NT, D])
        xln = sb("xln", [P, NT, D])
        xT = sb("xT", [128, KD, N])
        ct = sb("ct", [P, NT, NPAD])
        wt = sb("wt", [P, NT, NPAD])
        at = sb("at", [P, NT, N])
        negm = sb("negm", [P, NT, N])
        ring = sb("ring", [128, RING * CHUNK])
        work = sb("work", [128, 12100])
        hs = sb("hs", [P, NT, 260])
        small = sb("small", [128, 1904])

        class Carver:
            def __init__(self, tile):
                self.tile, self.at = tile, 0

            def __call__(self, shape, dt=F32, parts=128):
                n = 1
                for s in shape:
                    n *= s
                words = (n + 1) // 2 if dt in (BF16, F16) else n
                v = self.tile[0:parts, self.at:self.at + words]
                self.at += words
                assert self.at <= self.tile.shape[1], self.at
                if dt != F32:
                    v = v.bitcast(dt)[:, 0:n]
                if len(shape) == 2:
                    v = v.rearrange("p (a b) -> p a b", a=shape[0])
                elif len(shape) == 3:
                    v = v.rearrange("p (a b c) -> p a b c", a=shape[0], b=shape[1])
                return v

        sm = Carver(small)
        ident = sb("ident", [128, 128])
        iota_i = sb("iota_i", [128, NPAD], I32)
        iota_f = sb("iota_f", [128, NPAD])
        iota_h = iota_i[:, 0:NPAD // 2].bitcast(F16)
        sel = sb("sel", [128, 2 * WB])
        tri_b = sm([P], BF16, P)
        tri_f = sm([P], F32, P)
        ones_bf = sm([P], BF16, P)
        strict = sm([E1], F32, E1)
        ones_f = sm([128], F32)
        half_neg = sm([D])
        w_l0a = sb("w_l0a", [128, KD, D + 8])
        w_l0b = sb("w_l0b", [128, KD, D + 2])
        w_l2 = sb("w_l2", [128, KD, D + 8])
        w_l3 = w_l0a[:, :, 0:D]
        w_gcn = sb("w_gcn", [128, KD, 64])
        w_out = sb("w_out", [64, D])
        gate0 = sb("gate0", [128, KD, E0])
        gate1 = sb("gate1", [128, KD, E1])
        gate2 = sb("gate2", [128, KD, E2])
        gate3 = sb("gate3", [128, KD, E2])
        rbias = sb("rbias", [1, E0 + E1 + E2])
        b1_l0a = sb("b1_l0a", [128, KD])
        b_gcn = sb("b_gcn", [64, 1])
        b2_l0b = sb("b2_l0b", [P, D])
        b_out = b2_l0b
        b1T0 = sb("b1T0", [128, F0 // 128, E0])
        b1T1 = sb("b1T1", [128, F1 // 128, E1])
        b2T1 = sb("b2T1", [128, KD, E1])
        bnT = sb("bnT", [128, 4, KD, E2])
        b1T3 = sb("b1T3", [128, KD, E2])
        brow = sb("brow", [E2, D])

        psA = pb("psA", [128, 8, 128])
        psB = pb("psB", [128, 8, 128])
        psC = pb("psC", [128, 512])
        psD = pb("psD", [128, 512])
        psE = pb("psE", [128, 512])
        psF = pb("psF", [128, 512])

        st6 = sm([NT, 6], F32, P)
        mv = sm([NT, 2], F32, P)
        vare = sm([NT], F32, P)
        rstd = sm([NT], F32, P)
        al = sm([NT, 8], F32, P)
        al2 = sm([NT, 4], F32, P)
        mx = sm([NT, 4], F32, P)
        zz = sm([NT, 4], F32, P)
        r1 = sm([NT, 4], F32, P)
        r2 = sm([NT, 4], F32, P)
        rden = sm([NT], F32, P)
        outdeg = sm([NT], F32, P)
        nsrc = sm([NT], F32, P)
        cnt = sm([NBLK], F32, P)
        basef = sm([NBLK], F32, 1)
        base_i = sm([NBLK], I32, 1)
        flagf = sm([4], F32, 1)
        flag_i = sm([2], I32, 1)
        flag2_i = sm([2], I32, 1)
        scol = sm([NT, 3], F32, P)
        mx8 = sm([NT, 8], F32, P)
        ix8 = sm([NT, 8], U32, P)
        ixf = sm([NT, 2], F32, P)
        wgt = sm([NT, 8], F32, P)
        wgT = sm([N], F32, 8)
        gsel = sm([NT, 2], F32, P)
        sloti = sm([NT, 4], I32, P)
        tokid = sm([NT], F32, P)
        tok_i = sm([NT], I32, P)
        cntcol = sm([1], F32, E1)

        wk = Carver(work)
        ohs = [wk([CH, N + 1], BF16, P) for _ in range(2)]
        ohd = [wk([CH, 4, WB], BF16, P) for _ in range(2)]
        accs = [wk([N]) for _ in range(2)]
        ebt = [wk([CH, 5], F32, P) for _ in range(2)]
        rk = Carver(ring)
        src_i = rk([EPP], I32, P)
        dst_i = rk([EPP], I32, P)
        ew = rk([EPP], F32, P)
        res = rk([EPP], F32, P)
        bf_part = rk([EPP + 1], BF16, P)
        pack = rk([EPP, 5], F32, P)
        junk_e = rk([EPP], F32, P)
        b1r0 = rk([F0], F32, E0)
        b1r1 = rk([F1], F32, E1)
        b2r1 = rk([D], F32, E1)
        bnp = [rk([D], F32, E2) for _ in range(10)]
        b1r3 = rk([D], F32, E2)
        rw3 = rk([D], F32, E2)
        attv = [rk([D]) for _ in range(6)]
        attm = rk([KD, D])
        wk = Carver(work)
        u = [wk([NT, N], F32, P) for _ in range(2)]
        v = wk([NT, N], F32, P)
        junk = wk([N], F32, P)
        gat = wk([NT, D], F32, P)
        l2_bias = wk([D], F32, P)
        l2_gamma = wk([D], F32, P)
        l2_beta = wk([D], F32, P)
        wk = Carver(work)
        bufs = wk([E0, D], F32, CAP)
        bufT = wk([KD, E0 * CAP])
        h0 = wk([F0 // 128, CAP])
        ysb = wk([E0, D], F32, CAP)
        yg0 = wk([NT, D], F32, P)
        nan_m = wk([NT, D], I32, P)
        clip = wk([NT, D], F32, P)
        bound = work[0:P, 0:NT * D].rearrange("p (a b) -> p a b", a=NT)
        inf_m = work[0:P, NT * D:2 * NT * D].bitcast(I32).rearrange("p (a b) -> p a b", a=NT)
        oh0 = wk([NT, E0], F32, P)
        ohb0 = wk([NT, E0], BF16, P)
        t0 = wk([NT, E0], F32, P)
        zrow = wk([D], F32, CAP)
        wk = Carver(work)
        xs = wk([2 * NT, D], F32, P)
        xsT = wk([KD, SLOTS + WIN])
        yT = wk([KD, SLOTS + WIN])
        yg1 = xsT[0:P].rearrange("p k n -> p (k n)")[:, 0:2 * NT * D].rearrange("p (t d) -> p t d", d=D)
        h1 = wk([F1 // 128, WIN])
        oh1 = wk([2 * NT, E1], F32, P)
        ohb1 = wk([NT, E1], BF16, P)
        pos1 = wk([NT, E1], F32, P)
        t1 = wk([NT, E1], F32, P)
        lg = wk([NT, E1], F32, P)
        offb = wk([E1], F32, P)
        cntb = wk([E1], F32, P)
        starts_f = wk([E1, ROUNDS], F32, 1)
        starts = wk([E1, ROUNDS], I32, 1)
        wk = Carver(work)
        h1d = [wk([KD, N]) for _ in range(2)]
        h2d = [wk([KD, N]) for _ in range(2)]
        lg8 = sm([NT, 8], F32, P)
        ex8 = sm([NT, 8], F32, P)
        t8 = sm([NT, 8], F32, P)
        agg = work[0:P, 0:NT * 64].rearrange("p (a b) -> p a b", a=NT)
        hT = work[0:64, 400:400 + N]

        def cols(ap):
            return ap.rearrange("p (j q) -> p j q", q=P)

        def hidden0(f):
            return (psA, psB)[f // 4][:, f // 2 % 2 * 4 + f % 2, 0:CAP]

        def hidden1_ps(f):
            return (psC, psD, psE, psF)[f][:, 0:WIN]

        def slot(s):
            return ring[:, s * CHUNK:(s + 1) * CHUNK]

        tokens_by_tile = "(j p) d -> p j d"
        block = ctx.enter_context(nc.Block())

        @block.sync
        def _(sp):
            small_loads = [0]

            def load(dst, src, sem="params_loaded", **kw):
                sp.dma_start(dst, src, **kw).then_inc(S(sem), 16)
                small_loads[0] += 1

            sp.dma_start(dst_i, a["dst"].rearrange("(p t) -> p t", t=EPP)).then_inc(S("dst_loaded"), 16)
            sp.dma_start(src_i, a["src"].rearrange("(p t) -> p t", t=EPP)).then_inc(S("edges_loaded"), 16)
            sp.dma_start(ew, a["edge_weight"].rearrange("(p t) -> p t", t=EPP)).then_inc(S("edges_loaded"), 16)
            sp.dma_start(x[:], a["x"].rearrange(tokens_by_tile, p=P)).then_inc(S("x_loaded"), 16)

            def kpn(w):
                return w.rearrange("(k p) n -> p k n", p=128)

            load(w_l0a[:, :, 0:D], kpn(a["L0_gnn_W1"]))
            load(w_l0b[:, :, 0:D], kpn(a["L0_gnn_W2"]))
            load(w_l2[:, :, 0:D], kpn(a["L2_gnn_W"]))
            for i, name in enumerate(["L0_gnn_att_src1", "L0_gnn_att_dst1", "L0_gnn_att_src2", "L0_gnn_att_dst2",
                                      "L2_gnn_att_src", "L2_gnn_att_dst"]):
                load(attv[i], a[name].rearrange("h c -> (h c)").partition_broadcast(128))
            load(b1_l0a[:], a["L0_gnn_b1"].rearrange("(k p) -> p k", p=128), allow_slow_non_contiguous=True)
            load(b1r0, a["L0_ffn_b1"])
            load(b1r1, a["L1_ffn_b1"])
            load(b2r1, a["L1_ffn_b2"])
            for i, name in enumerate(["b1", "g1", "be1", "m1", "v1", "b2", "g2", "be2", "m2", "v2"]):
                load(bnp[i], a["L2_ffn_" + name])
            load(b1r3, a["L3_ffn_b1"])
            load(rw3, a["L3_ffn_router_w"])
            load(w_gcn[:], kpn(a["L1_gnn_W_gcn"]))
            load(w_out[:], a["L1_gnn_W_out"])
            load(gate0[:], kpn(a["L0_ffn_gate_w"]))
            load(gate1[:], kpn(a["L1_ffn_Wr"]))
            load(gate2[:], kpn(a["L2_ffn_Wr"]))
            load(rbias[:, 0:E0], a["L0_ffn_gate_b"].rearrange("(a n) -> a n", a=1))
            load(rbias[:, E0:E0 + E1], a["L1_ffn_br"].rearrange("(a n) -> a n", a=1))
            load(rbias[:, E0 + E1:], a["L2_ffn_br"].rearrange("(a n) -> a n", a=1))
            load(b_gcn[:], a["L1_gnn_b_gcn"].rearrange("(p a) -> p a", a=1))
            load(b2_l0b[:], a["L0_gnn_b2"].partition_broadcast(P))
            load(brow[:], a["L0_ffn_b2"])
            assert small_loads[0] == PARAMS

            sp.wait_ge(*reached("pack_ready", 1))
            sp.dma_start(edges_d.rearrange("(p t) k -> p (t k)", t=EPP), pack.rearrange("p t k -> p (t k)"))\
                .then_inc(S("edges_packed"), 16)
            sp.wait_ge(*reached("edges_packed", 16))
            sp.wait_ge(*reached("base_ready", 1))

            def edge_run(start):
                return edges_d[bass.ds(start, CHE), :].rearrange("(p t) k -> p (t k)", t=CH)

            def load_run(b, q):
                base = sp.value_load(base_i[0:1, bass.ds(b, 1)], min_val=0, max_val=E - CHE)
                sp.dma_start(ebt[q].rearrange("p t k -> p (t k)"), edge_run(base))\
                    .then_inc(S(f"edge_run_loaded{q}"), 16)

            for q in range(2):
                load_run(q, q)
            with sp.Fori(1, NBLK // 2) as i:
                for q in range(2):
                    sp.wait_ge(*reached("ohs_ready", 2 * i + q - 1))
                    sp.wait_ge(*reached("kinds_ready", 2 * i + q - 1))
                    load_run(2 * i + q, q)

            sp.wait_ge(*reached("params_used", 1))
            sp.wait_ge(*reached("params_turned", 1))

            def load_l0(c):
                e, half = c // 2, c % 2
                s = c % RING
                src = (a["L0_ffn_w2"] if half else a["L0_ffn_w1"])[e]
                sp.dma_start(slot(s).rearrange("p (k n) -> p k n", k=8 if half else KD), kpn(src))\
                    .then_inc(S(f"l0_weights{s}"), 16)

            for c in range(RING):
                load_l0(c)

            sp.wait_ge(*reached("flag_ready", 1))
            missed = sp.value_load(flag_i[0:1, 0:1], min_val=0, max_val=1)
            with sp.If(missed == 1):
                with sp.Fori(0, NBLK) as b:
                    with sp.Fori(0, NCHUNK) as c:
                        sp.wait_ge(*reached("all_added", b * NCHUNK + c + 1))
                        sp.dma_start(ebt[0].rearrange("p t k -> p (t k)"), edge_run(c * CHE))\
                            .then_inc(S("all_loaded"), 16)
            with sp.Else():
                sp.nop()
            sp.nop()

            sp.wait_ge(*reached("l0a_proj", NT))
            sp.dma_start(w_l3, kpn(a["L3_gnn_weight"])).then_inc(S("w_l3_loaded"), 16)
            if stages >= 2:
                sp.wait_ge(*reached("zrow_ready", 1))
                for e in range(E0):
                    sp.dma_start(buf_d[e * CAP:(e + 1) * CAP, :], zrow).then_inc(S("buf_zeroed"), 16)
                sp.wait_ge(*reached("tokens_sent0", 16 * NT))
                sp.dma_start(bufs, buf_d[0:E0 * CAP, :].rearrange("(e c) d -> c e d", e=E0))\
                    .then_inc(S("bufs_loaded"), 16)
                for c in range(RING, 2 * RING):
                    e = (c - RING) // 2
                    if c % 2:
                        sp.wait_ge(*reached("l0_y", e + 1))
                    else:
                        sp.wait_ge(*reached("l0_hidden", (e + 1) * (F0 // 256)))
                    load_l0(c)

            def load_l1(e, s):
                sp.dma_start(slot(s)[:, 0:CHUNK // 2].rearrange("p (k n) -> p k n", k=KD),
                             kpn(a["L1_ffn_W1"][e] if isinstance(e, int) else
                                 a["L1_ffn_W1"][bass.ds(e, 1)].rearrange("a k n -> (a k) n")))\
                    .then_inc(S(f"l1_weights{s}"), 16)
                sp.dma_start(slot(s)[:, CHUNK // 2:].rearrange("p (k n) -> p k n", k=F1 // 128),
                             kpn(a["L1_ffn_W2"][e] if isinstance(e, int) else
                                 a["L1_ffn_W2"][bass.ds(e, 1)].rearrange("a k n -> (a k) n")))\
                    .then_inc(S(f"l1_weights{s}"), 16)

            if stages >= 4:
                for s in range(RING):
                    e = (RING + s) // 2
                    if s % 2:
                        sp.wait_ge(*reached("l0_y", e + 1))
                    else:
                        sp.wait_ge(*reached("l0_hidden", (e + 1) * (F0 // 256)))
                    load_l1(s, s)
            if stages >= 3:
                sp.wait_ge(*reached("row_added", 1))
                sp.dma_start(b_out[:], a["L1_gnn_b_out"].partition_broadcast(P)).then_inc(S("b_out_loaded"), 16)
            if stages >= 6:
                sp.wait_ge(*reached("l0f_bias", NT))
                sp.dma_start(brow[:], a["L2_ffn_bo"]).then_inc(S("l2f_brow_loaded"), 16)
            if stages >= 2:
                sp.wait_ge(*reached("ysb_ready", 1))
                sp.dma_start(ybuf_d.rearrange("(e c) d -> c e d", e=E0), ysb).then_inc(S("ybuf_stored"), 16)
            if stages >= 4:
                sp.wait_ge(*reached("tokens_sent1", 32 * NT))
                sp.dma_start(xs, xs_d.rearrange("(t p) d -> p t d", p=P)).then_inc(S("xs_loaded"), 16)
                sp.wait_ge(*reached("flag2_ready", 1))
                full = sp.value_load(flag2_i[0:1, 0:1], min_val=0, max_val=1)
                with sp.If(full == 1):
                    for s in range(RING):
                        sp.wait_ge(*reached(f"l1_weights{s}", 32))
                    with sp.Fori(0, E1) as e:
                        sp.wait_ge(*reached("any_expert_used", e + 1))
                        w1 = a["L1_ffn_W1"][bass.ds(e, 1)].rearrange("a k n -> (a k) n")
                        w2 = a["L1_ffn_W2"][bass.ds(e, 1)].rearrange("a k n -> (a k) n")
                        sp.dma_start(slot(0)[:, 0:CHUNK // 2].rearrange("p (k n) -> p k n", k=KD), kpn(w1))\
                            .then_inc(S("any_expert_loaded"), 16)
                        sp.dma_start(slot(0)[:, CHUNK // 2:].rearrange("p (k n) -> p k n", k=F1 // 128), kpn(w2))\
                            .then_inc(S("any_expert_loaded"), 16)
                with sp.Else():
                    with sp.Fori(1, E1 // RING) as r:
                        for s in range(RING):
                            sp.wait_ge(*reached("l1_used", (r - 1) * RING + s + 1))
                            load_l1(r * RING + s, s)
                sp.nop()
                sp.wait_ge(*reached("ys_ready", 1))
                sp.dma_start(ys_d.rearrange("(t p) d -> p t d", p=P), xs).then_inc(S("ys_stored"), 16)
            if stages >= 5:
                sp.wait_ge(*reached("l1_tokens_back", 32 * NT))
                sp.dma_start(l2_bias, a["L2_gnn_bias"].partition_broadcast(P)).then_inc(S("l2_rows_loaded"), 16)
                sp.dma_start(l2_gamma, a["L2_gnn_gamma"].partition_broadcast(P)).then_inc(S("l2_rows_loaded"), 16)
                sp.dma_start(l2_beta, a["L2_gnn_beta"].partition_broadcast(P)).then_inc(S("l2_rows_loaded"), 16)

            def load_dense(tag, q, names, first):
                def one(e, wait):
                    for n, name in enumerate(names):
                        w = a[name][e] if isinstance(e, int) else \
                            a[name][bass.ds(e, 1)].rearrange("a k n -> (a k) n")
                        sp.dma_start(slot(first + q)[:, n * KD * D:(n + 1) * KD * D]
                                     .rearrange("p (k n) -> p k n", k=KD), kpn(w))\
                            .then_inc(S(f"{tag}_weights{q}"), 16)
                return one

            l2_names = ["L2_ffn_W1", "L2_ffn_W2", "L2_ffn_Wo"]
            l3_names = ["L3_ffn_w1", "L3_ffn_w2"]
            for tag, names, first, st in (("l2", l2_names, 0, 6), ("l3", l3_names, 2, 8)):
                if stages < st:
                    continue
                if st == 8:
                    sp.wait_ge(*reached("l2f_bias", NT))
                    sp.dma_start(brow[:], a["L3_ffn_b2"]).then_inc(S("l3f_brow_loaded"), 16)
                if st == 6:
                    sp.wait_ge(*reached("l1_experts_done", 1))
                loads = [load_dense(tag, q, names, first) for q in range(2)]
                for q in range(2):
                    loads[q](q, None)
                with sp.Fori(1, E2 // 2) as r:
                    for q in range(2):
                        sp.wait_ge(*reached(f"{tag}f_y", (2 * (r - 1) + q + 1) * NT))
                        loads[q](2 * r + q, None)

            sp.wait_ge(*reached("x_final", 1))
            sp.dma_start(out.rearrange(tokens_by_tile, p=P), x[:]).then_inc(S("out_stored"), 16)
            sp.wait_ge(*reached("out_stored", 16))

        @block.gpsimd
        def _(pool):
            st = Steps(S("pool_steps"))
            nc.gpsimd.iota(iota_i[:], [[1, NPAD]], base=0, channel_multiplier=0).then_inc(S("iota_ready"), 1)
            st.done(nc.gpsimd.memset(ident[:], 0.0))
            st.done(nc.gpsimd.memset(sel[:], 0.0))
            st.done(nc.gpsimd.memset(tri_f, 1.0))
            st.done(nc.gpsimd.memset(strict, 1.0))
            st.done(nc.gpsimd.memset(ones_f, 1.0))
            st.done(nc.gpsimd.memset(half_neg, -0.5))
            st.done(nc.gpsimd.memset(ones_bf, 1.0))
            st.wait(pool)

            def diag(t, base, n, step=1, op=ALU.not_equal, fill=1.0, cm=1):
                st.done(nc.gpsimd.affine_select(out=t, in_=t, compare_op=op, fill=fill, base=base,
                                                pattern=[[step, n]], channel_multiplier=cm))

            diag(ident[:], 0, 128, -1)
            diag(sel[:, 0:WB], 0, WB, -1)
            for k in range(1, 4):
                diag(sel[:, WB:], -k * WB, WB, -1)
                st.wait(pool)
            diag(tri_f, 0, P, 1, ALU.is_ge, 0.0, -1)
            diag(strict, -1, E1, 1, ALU.is_ge, 0.0, -1)
            st.wait(pool)
            nc.gpsimd.iota(tok_i, [[P, NT]], base=0, channel_multiplier=1).then_inc(S("consts_ready"), 1)
            pool.wait_ge(*reached("bn_var_ready", 1))
            nc.gpsimd.tensor_tensor(bnp[4], bnp[4], half_neg[0:E2, 0:D], ALU.pow)
            nc.gpsimd.tensor_tensor(bnp[9], bnp[9], half_neg[0:E2, 0:D], ALU.pow).then_inc(S("bn_pow_ready"), 1)

            def kinds(s):
                d = ohd[s]
                return nc.gpsimd.tensor_tensor(
                    d[:, :, 1:4, :], d[:, :, 0:1, :].to_broadcast([P, CH, 3, WB]),
                    ebt[s][:, :, 2:5].unsqueeze(3).to_broadcast([P, CH, 3, WB]), ALU.mult)

            with pool.Fori(0, NBLK // 2) as i:
                for q in range(2):
                    pool.wait_ge(*reached("ohd_ready", 2 * i + q + 1))
                    kinds(q).then_inc(S("kinds_ready"), 1)
            pool.wait_ge(*reached("flag_ready", 1))
            missed = pool.value_load(flag_i[0:1, 0:1], min_val=0, max_val=1)
            with pool.If(missed == 1):
                with pool.Fori(0, NBLK) as b:
                    with pool.Fori(0, NCHUNK) as c:
                        pool.wait_ge(*reached("all_ohd", b * NCHUNK + c + 1))
                        kinds(0).then_inc(S("all_kinds"), 1)
            with pool.Else():
                pool.nop()
            pool.nop()

            def power(tag):
                pool.wait_ge(*reached(tag + "_var", 1))
                nc.gpsimd.tensor_tensor(rstd, vare, half_neg[0:P, 0:NT], ALU.pow).then_inc(S(tag + "_rstd"), 1)

            power("l0g")
            if stages >= 2:
                power("l0f")
                pool.wait_ge(*reached("slots0_ready", 1))
                pool.wait_ge(*reached("buf_zeroed", 16 * E0))
                for j in range(NT):
                    nc.gpsimd.indirect_dma_start(
                        buf_d, bass.IndirectOffsetOnAxis(ap=sloti[:, j, 0:1], axis=0), xln[:, j, :], None)\
                        .then_inc(S("tokens_sent0"), 16)
                pool.wait_ge(*reached("ybuf_stored", 16))
                for j in range(NT):
                    nc.gpsimd.indirect_dma_start(
                        yg0[:, j, :], None, ybuf_d, bass.IndirectOffsetOnAxis(ap=sloti[:, j, 1:2], axis=0))\
                        .then_inc(S("l0_tokens_back"), 16)
            if stages >= 3:
                pool.wait_ge(*reached("deg_ready", 1))
                nc.gpsimd.tensor_tensor(nsrc, outdeg, half_neg[0:P, 0:NT], ALU.pow).then_inc(S("nsrc_ready"), 1)
                power("l1g")
                pool.wait_ge(*reached("indeg_ready", 1))
                nc.gpsimd.tensor_tensor(rden, vare, half_neg[0:P, 0:NT], ALU.pow).then_inc(S("ndst_ready"), 1)
            if stages >= 4:
                power("l1f")
                pool.wait_ge(*reached("slots1_ready", 1))
                for k in range(2):
                    for j in range(NT):
                        nc.gpsimd.indirect_dma_start(
                            xs_d, bass.IndirectOffsetOnAxis(ap=sloti[:, j, k:k + 1], axis=0), xln[:, j, :], None)\
                            .then_inc(S("tokens_sent1"), 16)
                pool.wait_ge(*reached("ys_stored", 16))
                for k in range(2):
                    for j in range(NT):
                        nc.gpsimd.indirect_dma_start(
                            yg1[:, k * NT + j, :], None, ys_d,
                            bass.IndirectOffsetOnAxis(ap=sloti[:, j, k:k + 1], axis=0))\
                            .then_inc(S("l1_tokens_back"), 16)
            if stages >= 5:
                power("l2g")
                power("l2n")
            if stages >= 6:
                power("l2f")
            if stages >= 7:
                power("l3g")
            if stages >= 8:
                power("l3f")

        @block.scalar
        def _(act):
            act.nop().then_inc(S("acc_free"), 2)
            act.nop().then_inc(S("counts_free"), 2)

            def evac_acc(s):
                return nc.scalar.activation(cols(accs[s]), (psA, psB)[s][:, 0:NT, 0:P], ACT.Copy)

            act.wait_ge(*reached("params_acc", 1))
            nc.scalar.activation(b1T0[:], psA[:, 0, 0:64].rearrange("p (f e) -> p f e", e=E0), ACT.Copy)
            nc.scalar.activation(b1T1[:], psC[:, 0:256].rearrange("p (f e) -> p f e", e=E1), ACT.Copy)
            nc.scalar.activation(b2T1[:], psD[:, 0:128].rearrange("p (f e) -> p f e", e=E1), ACT.Copy)
            nc.scalar.activation(b1T3[:], psE[:, 0:16].rearrange("p (f e) -> p f e", e=E2), ACT.Copy)
            nc.scalar.activation(gate3[:], psF[:, 0:16].rearrange("p (f e) -> p f e", e=E2), ACT.Copy)
            nc.scalar.activation(bnT[:], psB[:, 0, 0:64].rearrange("p (w f e) -> p w f e", f=KD, e=E2), ACT.Copy)\
                .then_inc(S("params_turned"), 1)

            def counts_out(i, q, before):
                b = 2 * i + q - 1
                act.wait_ge(*reached("block_ready", b + 1))
                ps = (psC, psD)[(q + 1) % 2][0:P, 0:NT * 2 * WB].rearrange("p (j c) -> p j c", c=2 * WB)
                nc.scalar.activation(ct[:, :, bass.ds(b * WB, WB)], ps[:, :, 0:WB], ACT.Copy)
                nc.scalar.activation(wt[:, :, bass.ds(b * WB, WB)], ps[:, :, WB:], ACT.Copy)\
                    .then_inc(S("counts_free"), 1)

            def acc_out(n, q):
                act.wait_ge(*reached("acc_ready", n + 1))
                evac_acc(q).then_inc(S("acc_free"), 1)

            acc_out(0, 0)
            acc_out(1, 1)
            counts_out(0, 1, 0)
            with act.Fori(1, NBLK // 2) as i:
                for q in range(2):
                    acc_out(2 * i + q, q)
                    counts_out(i, q, None)
            counts_out(NBLK // 2, 0, None)

            act.wait_ge(*reached("flag_ready", 1))
            missed = act.value_load(flag_i[0:1, 0:1], min_val=0, max_val=1)
            with act.If(missed == 1):
                with act.Fori(0, NBLK) as b:
                    with act.Fori(0, NCHUNK) as c:
                        act.wait_ge(*reached("all_acc", b * NCHUNK + c + 1))
                        evac_acc(0).then_inc(S("all_acc_out"), 1)
            with act.Else():
                act.nop()
            act.nop()

            def turned(tag, bias=None):
                act.wait_ge(*reached(tag + "_turned0", 1))
                if bias is None:
                    nc.scalar.activation(cols(xT[:, 0, :]), psA[:, 0:NT, 0:P], ACT.Copy).then_inc(S(tag + "_xT0"), 1)
                else:
                    nc.scalar.activation(cols(xT[:, 0, :]), psA[:, 0:NT, 0:P], ACT.Relu, bias=bias[:, 0:1])\
                        .then_inc(S(tag + "_xT0"), 1)
                    act.wait_ge(*reached(tag + "_turned1", 1))
                    nc.scalar.activation(cols(xT[:, 1, :]), psB[:, 0:NT, 0:P], ACT.Relu, bias=bias[:, 1:2])\
                        .then_inc(S(tag + "_xT1"), 1)

            def attention(tag, heads):
                ch = D // heads
                act.wait_ge(*reached(tag + "_ones", 1))
                for j in range(NT):
                    act.wait_ge(*reached(tag + "_proj", j + 1))
                    nc.scalar.activation(al[:, j, 0:2 * heads], (psC, psD)[j % 2][0:P, D:D + 2 * heads], ACT.Copy)\
                        .then_inc(S(tag + "_al"), 1)
                    nc.scalar.activation(hs[:, j, 0:heads * (ch + 1)].rearrange("p (h c) -> p h c", h=heads)[:, :, 0:ch],
                                         (psC, psD)[j % 2][0:P, 0:D].rearrange("p (h c) -> p h c", h=heads),
                                         ACT.Copy).then_inc(S(tag + "_hs"), 1)
                act.wait_ge(*reached(tag + "_rows", 1))
                for h in range(heads):
                    act.wait_ge(*reached(tag + "_r1", h + 1))
                    if h >= 2:
                        act.wait_ge(*reached(tag + "_agg", h - 1))
                    for j in range(NT):
                        ins = nc.scalar.activation(cols(u[h % 2][:, j, :]), psA[0:P, 0:NT, 0:P], ACT.Exp,
                                                   bias=al[:, j, h:h + 1])
                    ins.then_inc(S(tag + "_u"), 1)
                    act.wait_ge(*reached(tag + "_r2", h + 1))
                    if h >= 1:
                        act.wait_ge(*reached(tag + "_max", h))
                    for j in range(NT):
                        ins = nc.scalar.activation(cols(v[:, j, :]), psB[0:P, 0:NT, 0:P], ACT.Exp,
                                                   bias=al2[:, j, h:h + 1])
                    ins.then_inc(S(tag + "_v"), 1)

            act.wait_ge(*reached("graph_ready", 1))
            nc.scalar.activation(at[:], ct[:, :, 0:N], ACT.Copy).then_inc(S("at_copied"), 1)
            turned("l0g")
            attention("l0a", 4)
            turned("l0m", b1_l0a)
            attention("l0b", 1)
            if stages >= 2:
                turned("l0f")
                act.wait_ge(*reached("shift0_ready", 1))
                nc.scalar.activation(ex8, lg8, ACT.Exp).then_inc(S("exp0_ready"), 1)
                act.wait_ge(*reached("bufs_turned0", 1))
                nc.scalar.activation(bufT[:, 0, :].rearrange("p (e c) -> p e c", e=E0), psA[:, :, 0:CAP], ACT.Copy)\
                    .then_inc(S("bufT0"), 1)
                with act.Fori(0, E0 // 4) as r:
                    for q in range(4):
                        for f in range(F0 // 128):
                            act.wait_ge(*reached("l0_hidden", (4 * r + q) * (F0 // 256) + f // 2 + 1))
                            nc.scalar.activation(h0[:, f, :], hidden0(f), ACT.Relu,
                                                 bias=b1T0[:, f, bass.ds(4 * r + q, 1)]).then_inc(S("l0_relu"), 1)
            if stages >= 3:
                turned("l1g")
                for j in range(NT):
                    act.wait_ge(*reached("gcn_proj", j + 1))
                    if j == 0:
                        act.wait_ge(*reached("nsrc_ready", 1))
                    nc.scalar.activation(hs[:, j, 0:64], (psC, psD)[j % 2][0:P, 0:64], ACT.Copy,
                                         scale=nsrc[:, j:j + 1]).then_inc(S("gcn_hs"), 1)
                act.wait_ge(*reached("gcn_turned", 1))
                nc.scalar.activation(cols(hT), psA[0:64, 0:NT, 0:P], ACT.Relu, bias=b_gcn[:, 0:1])\
                    .then_inc(S("gcn_hT"), 1)
            if stages >= 4:
                turned("l1f")
                act.wait_ge(*reached("shift1_ready", 1))
                nc.scalar.activation(gsel[:, :, 1], gsel[:, :, 0], ACT.Exp).then_inc(S("exp1_ready"), 1)
                for g in range(2):
                    act.wait_ge(*reached("xs_turned", 2 * g + 1))
                    nc.scalar.activation(xsT[:, 0, g * N:(g + 1) * N].rearrange("p (j q) -> p j q", q=P),
                                         psA[:, 0:NT, 0:P], ACT.Copy).then_inc(S("xsT_act"), 1)
                act.wait_ge(*reached("flag2_ready", 1))
                full = act.value_load(flag2_i[0:1, 0:1], min_val=0, max_val=1)

                def hidden1(f, e):
                    return nc.scalar.activation(h1[:, f, :], hidden1_ps(f), ACT.Relu,
                                                bias=b1T1[:, f, bass.ds(e, 1)])

                nf = F1 // 128
                with act.If(full == 1):
                    with act.Fori(0, E1) as e:
                        with act.Fori(0, ROUNDS) as r:
                            for f in range(nf):
                                act.wait_ge(*reached("any_hidden", (e * ROUNDS + r) * nf + f + 1))
                                hidden1(f, e).then_inc(S("any_relu"), 1)
                with act.Else():
                    with act.Fori(0, E1 // RING) as r:
                        for q in range(RING):
                            for f in range(nf):
                                act.wait_ge(*reached("l1_hidden", (RING * r + q) * nf + f + 1))
                                hidden1(f, RING * r + q).then_inc(S("l1_relu"), 1)
                act.nop()
                for g in (0, 2, 4):
                    act.wait_ge(*reached("ys_turned", g + 1))
                    nc.scalar.activation(xs[:, 2 * g:2 * g + 2, :].rearrange("p t (m d) -> p (t m) d", m=2),
                                         psA[0:P, 0:4, 0:128], ACT.Copy).then_inc(S("ys_act"), 1)
            if stages >= 5:
                turned("l2g")
                attention("l2a", 4)

            def dense(tag, func, gated):
                turned(tag)
                act.wait_ge(*reached(tag + "_shift", 1))
                nc.scalar.activation(ex8, lg8, ACT.Exp).then_inc(S(tag + "_exp"), 1)
                layers = 2 if tag == "l2f" else 1
                act.nop().then_inc(S(tag + "_act"), 2)
                with act.Fori(0, E2 // 2) as r:
                    for layer in range(layers):
                        for q in range(2):
                            e = 2 * r + q
                            for m in range(KD):
                                act.wait_ge(*reached(tag + "_hidden", ((r * layers + layer) * 2 + q) * KD + m + 1))
                                o = cols((h1d, h2d)[layer][q][:, m, :])
                                i_ = (psA, psB)[m][:, 0:NT, 0:P]
                                if tag == "l2f":
                                    ins = nc.scalar.activation(o, i_, func, bias=bnT[:, 2 * layer + 1, m, bass.ds(e, 1)],
                                                               scale=bnT[:, 2 * layer, m, bass.ds(e, 1)])
                                else:
                                    ins = nc.scalar.activation(o, i_, func, bias=b1T3[:, m, bass.ds(e, 1)])
                                ins.then_inc(S(tag + "_act"), 1)

            if stages >= 6:
                dense("l2f", ACT.Relu, True)
            if stages >= 7:
                turned("l3g")
                for j in range(NT):
                    act.wait_ge(*reached("l3_proj", j + 1))
                    nc.scalar.activation(hs[:, j, 0:D], (psC, psD)[j % 2][0:P, 0:D], ACT.Copy)\
                        .then_inc(S("l3_hs"), 1)
            if stages >= 8:
                dense("l3f", ACT.Gelu, False)

        @block.tensor
        def _(pe):
            pe.wait_ge(*reached("consts_ready", 1))
            pe.wait_ge(*reached("cnt_ready", NBLK - 1))
            nc.tensor.matmul(psE[0:1, 0:NBLK], ones_f[0:P, 0:1], cnt, start=True, stop=True).then_inc(S("base_sum"), 1)
            pe.wait_ge(*reached("params_loaded", 16 * PARAMS))
            pe.wait_ge(*reached("bn_ready", 1))
            pe.wait_ge(*reached("base_ready", 1))
            for f in range(F0 // 128):
                nc.tensor.transpose(psA[:, 0, f * E0:(f + 1) * E0], b1r0[:, f * 128:(f + 1) * 128], ident[0:E0, 0:E0])
            for f in range(F1 // 128):
                nc.tensor.transpose(psC[:, f * E1:(f + 1) * E1], b1r1[:, f * 128:(f + 1) * 128], ident[0:E1, 0:E1])
            for k in range(KD):
                nc.tensor.transpose(psD[:, k * E1:(k + 1) * E1], b2r1[:, k * 128:(k + 1) * 128], ident[0:E1, 0:E1])
                nc.tensor.transpose(psE[:, k * E2:(k + 1) * E2], b1r3[:, k * 128:(k + 1) * 128], ident[0:E2, 0:E2])
                nc.tensor.transpose(psF[:, k * E2:(k + 1) * E2], rw3[:, k * 128:(k + 1) * 128], ident[0:E2, 0:E2])
            for n, t in enumerate((bnp[1], bnp[2], bnp[6], bnp[7])):
                for k in range(KD):
                    c = (n * KD + k) * E2
                    ins = nc.tensor.transpose(psB[:, 0, c:c + E2], t[:, k * 128:(k + 1) * 128], ident[0:E2, 0:E2])
            ins.then_inc(S("params_acc"), 1)
            pe.wait_ge(*reached("params_turned", 1))

            def accumulate(s):
                acc = (psA, psB)[s]
                for t in range(CH):
                    w = ohd[s][:, t].rearrange("p k d -> p (k d)")
                    nc.tensor.matmul(acc[:, 0:4, 0:P], w, cols(ohs[s][:, t, 0:4 * P]), start=(t == 0), stop=(t == CH - 1))
                    ins = nc.tensor.matmul(acc[:, 4, 0:P], w, ohs[s][:, t, 4 * P:N], start=(t == 0), stop=(t == CH - 1))
                return ins

            def split(s, ps):
                for j in range(NT):
                    ins = nc.tensor.matmul(ps[0:P, j * 2 * WB:(j + 1) * 2 * WB], accs[s][:, j * P:(j + 1) * P], sel[:],
                                           start=True, stop=True)
                return ins

            def gather_block(b, q):
                pe.wait_ge(*reached("kinds_ready", b + 1))
                pe.wait_ge(*reached("ohs_ready", b + 1))
                pe.wait_ge(*reached("acc_free", b + 1))
                accumulate(q).then_inc(S("acc_ready"), 1)

            def split_block(b, q):
                pe.wait_ge(*reached("acc_free", b + 3))
                pe.wait_ge(*reached("counts_free", b + 1))
                split(q, (psC, psD)[q]).then_inc(S("block_ready"), 1)

            gather_block(0, 0)
            gather_block(1, 1)
            split_block(0, 0)
            with pe.Fori(1, NBLK // 2) as i:
                gather_block(2 * i, 0)
                split_block(2 * i - 1, 1)
                gather_block(2 * i + 1, 1)
                split_block(2 * i, 0)
            split_block(NBLK - 1, 1)

            pe.wait_ge(*reached("outdeg_ready", 1))
            nc.tensor.matmul(psE[0:1, 0:NT], ones_f[0:P, 0:1], outdeg, start=True, stop=True).then_inc(S("total_sum"), 1)
            pe.wait_ge(*reached("flag_ready", 1))
            missed = pe.value_load(flag_i[0:1, 0:1], min_val=0, max_val=1)
            with pe.If(missed == 1):
                with pe.Fori(0, NBLK) as b:
                    with pe.Fori(0, NCHUNK) as c:
                        n = b * NCHUNK + c
                        pe.wait_ge(*reached("all_kinds", n + 1))
                        pe.wait_ge(*reached("all_ohs", n + 1))
                        accumulate(0).then_inc(S("all_acc"), 1)
                        pe.wait_ge(*reached("all_acc_out", n + 1))
                        split(0, psC).then_inc(S("all_split"), 1)
            with pe.Else():
                pe.nop()
            pe.nop()

            def turn(tag, src_sem, src):
                pe.wait_ge(*reached(src_sem, 1))
                for k in range(KD):
                    for j in range(NT):
                        ins = nc.tensor.transpose((psA, psB)[k][:, j, 0:P], src[:, j, k * 128:(k + 1) * 128],
                                                  ident[0:P, 0:P])
                    ins.then_inc(S(f"{tag}_turned{k}"), 1)

            def project(tag, xtag, w, width, sem_out, sem_in, wait_first=None):
                pe.wait_ge(*reached(xtag + "_xT0", 1))
                pe.wait_ge(*reached(xtag + "_xT1", 1))
                for j in range(NT):
                    if j >= 2:
                        for s_ in sem_in:
                            pe.wait_ge(*reached(s_, j - 1))
                    for k in range(KD):
                        ins = nc.tensor.matmul((psC, psD)[j % 2][0:P, 0:width], xT[:, k, j * P:(j + 1) * P], w[:, k, 0:width],
                                               start=(k == 0), stop=(k == KD - 1))
                    ins.then_inc(S(sem_out), 1)

            def row(ps, col):
                for j in range(NT):
                    ins = nc.tensor.transpose(ps[0:P, j, 0:P], col(j).to_broadcast([P, P]), ident[0:P, 0:P])
                return ins

            def attention(tag, xtag, w, heads):
                ch = D // heads
                project(tag, xtag, w, D + 2 * heads, tag + "_proj", [tag + "_hs", tag + "_al"])
                pe.wait_ge(*reached(tag + "_al", NT))
                for h in range(heads):
                    if h >= 2:
                        pe.wait_ge(*reached(tag + "_masked", (h - 1) * NT))
                    row((psA, psB)[h % 2], lambda j: al[:, j, h:h + 1]).then_inc(S(tag + "_bc"), 1)
                pe.wait_ge(*reached(tag + "_rows", 1))

                def rows(h):
                    if h >= 1:
                        pe.wait_ge(*reached(tag + "_u", h))
                    row(psA, lambda j: r1[:, j, h:h + 1]).then_inc(S(tag + "_r1"), 1)
                    if h >= 1:
                        pe.wait_ge(*reached(tag + "_v", h))
                    row(psB, lambda j: r2[:, j, h:h + 1]).then_inc(S(tag + "_r2"), 1)

                pe.wait_ge(*reached(tag + "_hs", NT))
                rows(0)
                for h in range(heads):
                    if h + 1 < heads:
                        rows(h + 1)
                    pe.wait_ge(*reached(tag + "_p", h + 1))
                    if heads > 1:
                        if h >= 2:
                            pe.wait_ge(*reached(tag + "_out", h - 1))
                        for j in range(NT):
                            for i in range(NT):
                                ins = nc.tensor.matmul((psC, psD)[h % 2][0:P, j * 65:(j + 1) * 65],
                                                       u[h % 2][:, i, j * P:(j + 1) * P], hs[:, i, h * 65:(h + 1) * 65],
                                                       start=(i == 0), stop=(i == NT - 1))
                        ins.then_inc(S(tag + "_agg"), 1)
                    else:
                        for j in range(NT):
                            if j >= 2:
                                pe.wait_ge(*reached(tag + "_out", j - 1))
                            for i in range(NT):
                                ins = nc.tensor.matmul((psC, psD)[j % 2][0:P, 0:D + 1],
                                                       u[0][:, i, j * P:(j + 1) * P], hs[:, i, 0:D + 1],
                                                       start=(i == 0), stop=(i == NT - 1))
                            ins.then_inc(S(tag + "_agg"), 1)

            pe.wait_ge(*reached("at_ready", 1))
            for j in range(NT):
                if j >= 2:
                    pe.wait_ge(*reached("negm_done", j - 1))
                for i in range(NT):
                    ins = nc.tensor.transpose((psA, psB)[j % 2][0:P, i, 0:P], at[:, i, j * P:(j + 1) * P], ident[0:P, 0:P])
                ins.then_inc(S("at_turned"), 1)
            pe.wait_ge(*reached("negm_done", NT))

            turn("l0g", "l0g_xln", xln)
            attention("l0a", "l0g", w_l0a, 4)
            turn("l0m", "l0a_done", gat)
            attention("l0b", "l0m", w_l0b, 1)

            def logits(tag, gate, ne, rb):
                pe.wait_ge(*reached(tag + "_xT0", 1))
                pe.wait_ge(*reached(tag + "_xT1", 1))
                for j in range(NT):
                    o = psC[0:P, j * ne:(j + 1) * ne]
                    for k in range(KD):
                        ins = nc.tensor.matmul(o, xT[:, k, j * P:(j + 1) * P], gate[:, k, :], start=(k == 0),
                                               stop=(k == KD - 1 and rb is None))
                    if rb is not None:
                        ins = nc.tensor.matmul(o, ones_f[0:1, 0:P], rbias[:, rb:rb + ne], start=False, stop=True)
                ins.then_inc(S(tag + "_logits"), 1)

            def ranks(tag, ohb, ne):
                pe.wait_ge(*reached(tag + "_onehot", 1))
                for j in range(NT):
                    o = psD[0:P, j * ne:(j + 1) * ne]
                    for i in range(j + 1):
                        ins = nc.tensor.matmul(o, tri_b if i == j else ones_bf, ohb[:, i, :], start=(i == 0), stop=(i == j))
                return ins

            def expert_bias(tag, wsem, wsrc, brow):
                pe.wait_ge(*reached(wsem, 1))
                if tag != "l0f":
                    pe.wait_ge(*reached(tag + "_brow_loaded", 16))
                for j in range(NT):
                    ins = nc.tensor.transpose(psA[0:8, j, 0:P], wsrc[:, j, :], ident[0:P, 0:P])
                ins.then_inc(S(tag + "_wturned"), 1)
                pe.wait_ge(*reached(tag + "_wT", 1))
                for j in range(NT):
                    if j >= 2:
                        pe.wait_ge(*reached(tag + "_bias_out", j - 1))
                    nc.tensor.matmul((psC, psD)[j % 2][0:P, 0:D], wgT[:, j * P:(j + 1) * P], brow[:], start=True, stop=True)\
                        .then_inc(S(tag + "_bias"), 1)

            if stages >= 2:
                turn("l0f", "l0f_xln", xln)
                logits("l0f", gate0, E0, 0)
                ranks("l0f", ohb0, E0).then_inc(S("l0_ranks"), 1)
                pe.wait_ge(*reached("slots0_ready", 1))
                expert_bias("l0f", "l0f_onehot", oh0, brow)
                pe.wait_ge(*reached("bufs_loaded", 16))
                for k in range(KD):
                    for e in range(E0):
                        ins = nc.tensor.transpose((psA, psB)[k][:, e, 0:CAP], bufs[:, e, k * 128:(k + 1) * 128],
                                                  ident[0:CAP, 0:CAP])
                    ins.then_inc(S(f"bufs_turned{k}"), 1)
                pe.wait_ge(*reached("bufT0", 1))
                pe.wait_ge(*reached("bufT1", 1))
                nf = F0 // 128
                with pe.Fori(0, 2) as r:
                    for q in range(4):
                        e = 4 * r + q
                        w1 = slot(2 * q).rearrange("p (k n) -> p k n", k=KD)
                        w2 = slot(2 * q + 1).rearrange("p (k n) -> p k n", k=nf)
                        pe.wait_ge(*reached(f"l0_weights{2 * q}", 16 * r + 16))
                        for f in range(nf):
                            for k in range(KD):
                                ins = nc.tensor.matmul(hidden0(f), w1[:, k, f * 128:(f + 1) * 128],
                                                       bufT[:, k, bass.ds(e * CAP, CAP)], start=(k == 0), stop=(k == KD - 1))
                            if f % 2:
                                ins.then_inc(S("l0_hidden"), 1)
                        pe.wait_ge(*reached(f"l0_weights{2 * q + 1}", 16 * r + 16))
                        pe.wait_ge(*reached("l0_y_free", e + 1))
                        y = (psC, psD)[q % 2][0:CAP, 0:D]
                        for f in range(nf):
                            pe.wait_ge(*reached("l0_relu", e * nf + f + 1))
                            ins = nc.tensor.matmul(y, h0[:, f, :], w2[:, f, :], start=(f == 0), stop=(f == nf - 1))
                        ins.then_inc(S("l0_y"), 1)
            if stages >= 3:
                turn("l1g", "l1g_xln", xln)
                project("gcn", "l1g", w_gcn, 64, "gcn_proj", ["gcn_hs"])
                pe.wait_ge(*reached("gcn_hs", NT))
                pe.wait_ge(*reached("gcn_ones", 1))
                for j in range(NT):
                    for i in range(NT):
                        ins = nc.tensor.matmul(psE[0:P, j * 65:(j + 1) * 65], ct[:, i, j * P:(j + 1) * P], hs[:, i, 0:65],
                                               start=(i == 0), stop=(i == NT - 1))
                ins.then_inc(S("gcn_agg"), 1)
                pe.wait_ge(*reached("gcn_scaled", 1))
                for j in range(NT):
                    ins = nc.tensor.transpose(psA[0:64, j, 0:P], agg[:, j, :], ident[0:P, 0:P])
                ins.then_inc(S("gcn_turned"), 1)
                pe.wait_ge(*reached("gcn_hT", 1))
                for j in range(NT):
                    if j >= 2:
                        pe.wait_ge(*reached("gcn_out", j - 1))
                    nc.tensor.matmul((psC, psD)[j % 2][0:P, 0:D], hT[:, j * P:(j + 1) * P], w_out[:], start=True, stop=True)\
                        .then_inc(S("gcn_y"), 1)
            if stages >= 4:
                turn("l1f", "l1f_xln", xln)
                logits("l1f", gate1, E1, E0)
                ranks("l1f", ohb1, E1)
                for i in range(NT):
                    ins = nc.tensor.matmul(psE[0:P, 0:E1], ones_bf, ohb1[:, i, :], start=(i == 0), stop=(i == NT - 1))
                for i in range(NT):
                    ins = nc.tensor.matmul(psF[0:E1, 0:1], ohb1[:, i, :], ones_bf[:, 0:1], start=(i == 0), stop=(i == NT - 1))
                ins.then_inc(S("l1_ranks"), 1)
                pe.wait_ge(*reached("cntcol_ready", 1))
                nc.tensor.matmul(psC[0:P, 0:E1], cntcol.to_broadcast([E1, P]), strict, start=True, stop=True)\
                    .then_inc(S("l1_offsets"), 1)
                pe.wait_ge(*reached("xs_loaded", 16))
                for g in range(4):
                    k, half = g % 2, g // 2
                    if half:
                        pe.wait_ge(*reached("xsT_act" if k == 0 else "xsT_dve", 1))
                    for j in range(NT):
                        ins = nc.tensor.transpose((psA, psB)[k][:, j, 0:P], xs[:, half * NT + j, k * 128:(k + 1) * 128],
                                                  ident[0:P, 0:P])
                    ins.then_inc(S("xs_turned"), 1)
                pe.wait_ge(*reached("xsT_act", 2))
                pe.wait_ge(*reached("xsT_dve", 2))
                pe.wait_ge(*reached("flag2_ready", 1))
                full = pe.value_load(flag2_i[0:1, 0:1], min_val=0, max_val=1)
                nf = F1 // 128

                def hidden1(s, f, start):
                    w1 = slot(s)[:, 0:CHUNK // 2].rearrange("p (k n) -> p k n", k=KD)
                    for k in range(KD):
                        ins = nc.tensor.matmul(hidden1_ps(f), w1[:, k, f * 128:(f + 1) * 128],
                                               xsT[:, k, bass.ds(start, WIN)], start=(k == 0), stop=(k == KD - 1))
                    return ins

                def out1(s, ps, wait):
                    w2 = slot(s)[:, CHUNK // 2:].rearrange("p (k n) -> p k n", k=nf)
                    for m in range(KD):
                        for f in range(nf):
                            if m == 0:
                                wait(f)
                            ins = nc.tensor.matmul(ps[:, m, 0:WIN], w2[:, f, m * 128:(m + 1) * 128], h1[:, f, :],
                                                   start=(f == 0), stop=(f == nf - 1))
                    return ins

                with pe.If(full == 1):
                    with pe.Fori(0, E1) as e:
                        with pe.Fori(0, ROUNDS) as r:
                            n = e * ROUNDS + r
                            pe.wait_ge(*reached("any_expert_loaded", 32 * e + 32))
                            start = pe.value_load(starts[0:1, bass.ds(e, 1), bass.ds(r, 1)].rearrange("p a b -> p (a b)"),
                                                  min_val=0, max_val=SLOTS)
                            for f in range(nf):
                                hidden1(0, f, start).then_inc(S("any_hidden"), 1)
                            pe.wait_ge(*reached("any_y_free", n + 1))
                            out1(0, psA, lambda f: pe.wait_ge(*reached("any_relu", n * nf + f + 1))).then_inc(S("any_y"), 1)
                with pe.Else():
                    with pe.Fori(0, E1 // RING) as r:
                        for q in range(RING):
                            e = r * RING + q
                            start = pe.value_load(starts[0:1, bass.ds(e, 1), 0:1].rearrange("p a b -> p (a b)"),
                                                  min_val=0, max_val=SLOTS)
                            pe.wait_ge(*reached(f"l1_weights{q}", 32 * r + 32))
                            for f in range(nf):
                                hidden1(q, f, start).then_inc(S("l1_hidden"), 1)
                            pe.wait_ge(*reached("l1_y_free", e + 1))
                            out1(q, (psA, psB)[q % 2], lambda f: pe.wait_ge(*reached("l1_relu", e * nf + f + 1)))\
                                .then_inc(S("l1_used"), 1)
                pe.nop()
                pe.wait_ge(*reached("yT_ready", 1))
                for g in range(5):
                    if g >= 2:
                        pe.wait_ge(*reached("ys_dve" if g % 2 else "ys_act", g // 2))
                    for t in range(2):
                        for m in range(KD):
                            c = (2 * g + t) * P
                            ins = nc.tensor.transpose((psA, psB)[g % 2][0:P, t * KD + m, :], yT[:, m, c:c + P], ident[:])
                    ins.then_inc(S("ys_turned"), 1)
            if stages >= 5:
                turn("l2g", "l2g_xln", xln)
                attention("l2a", "l2g", w_l2, 4)

            def dense(tag, wtag, first, gate, rb, brow, layers):
                turn(tag, tag + "_xln", xln)
                logits(tag, gate, E2, rb)
                expert_bias(tag, tag + "_w", wgt, brow)
                with pe.Fori(0, E2 // 2) as r:
                    for q in range(2):
                        pe.wait_ge(*reached(f"{wtag}_weights{q}", 16 * (layers + 1) * (r + 1)))
                    for layer in range(layers):
                        for q in range(2):
                            w = slot(first + q)[:, layer * KD * D:(layer + 1) * KD * D].rearrange("p (k n) -> p k n", k=KD)
                            src = xT if layer == 0 else h1d[q]
                            n = (r * layers + layer) * 2 + q
                            if layer:
                                pe.wait_ge(*reached(tag + "_act", (r * layers * 2 + q + 1) * KD + 2))
                            for m in range(KD):
                                ps = (psA, psB)[m]
                                pe.wait_ge(*reached(tag + "_act", n * KD + m + 1))
                                for k in range(KD):
                                    wk_ = w[:, k, m * 128:(m + 1) * 128]
                                    nc.tensor.matmul(ps[:, 0:4, 0:P], wk_, cols(src[:, k, 0:4 * P]),
                                                     start=(k == 0), stop=(k == KD - 1))
                                    ins = nc.tensor.matmul(ps[:, 4, 0:P], wk_, src[:, k, 4 * P:N],
                                                           start=(k == 0), stop=(k == KD - 1))
                                ins.then_inc(S(tag + "_hidden"), 1)
                    for q in range(2):
                        hsrc = (h1d, h2d)[layers - 1][q]
                        w = slot(first + q)[:, layers * KD * D:(layers + 1) * KD * D].rearrange("p (k n) -> p k n", k=KD)
                        pe.wait_ge(*reached(tag + "_act", ((r * layers + layers - 1) * 2 + q + 1) * KD + 2))
                        for j in range(NT):
                            n = (2 * r + q) * NT + j
                            pe.wait_ge(*reached(tag + "_y_free", n + 1))
                            for k in range(KD):
                                ins = nc.tensor.matmul(((psC, psD)[(q * NT + j) % 2])[0:P, 0:D], hsrc[:, k, j * P:(j + 1) * P],
                                                       w[:, k, :], start=(k == 0), stop=(k == KD - 1))
                            ins.then_inc(S(tag + "_y"), 1)

            if stages >= 6:
                dense("l2f", "l2", 0, gate2, E0 + E1, brow, 2)
            if stages >= 7:
                turn("l3g", "l3g_xln", xln)
                pe.wait_ge(*reached("w_l3_loaded", 16))
                project("l3", "l3g", w_l3, D, "l3_proj", ["l3_hs"])
                pe.wait_ge(*reached("l3_hs", NT))
                for j in range(NT):
                    if j >= 2:
                        pe.wait_ge(*reached("l3_out", j - 1))
                    for i in range(NT):
                        ins = nc.tensor.matmul((psC, psD)[j % 2][0:P, 0:D], wt[:, i, j * P:(j + 1) * P], hs[:, i, 0:D],
                                               start=(i == 0), stop=(i == NT - 1))
                    ins.then_inc(S("l3_agg"), 1)
            if stages >= 8:
                dense("l3f", "l3", 2, gate3, None, brow, 1)

        @block.vector
        def _(dve):
            V = nc.vector
            st = Steps(S("dve_steps"))

            def step(ins):
                st.done(ins)
                st.wait(dve)

            V.nop().then_inc(S("all_added"), 1)
            dve.wait_ge(*reached("dst_loaded", 16))
            V.memset(cnt, 0.0)
            step(V.tensor_copy(pack[:, :, 1], dst_i))
            for b in range(1, NBLK):
                ins = V.tensor_scalar(junk_e, pack[:, :, 1], float(b * WB), 0.0, ALU.is_lt, ALU.add, accum_out=cnt[:, b:b + 1])
                ins.then_inc(S("cnt_ready"), 1)
                dve.wait_ge(*reached("cnt_ready", b))
            dve.wait_ge(*reached("edges_loaded", 32))
            V.tensor_copy(pack[:, :, 0], src_i)
            step(V.tensor_copy(bf_part[:, 0:EPP], ew))
            step(V.tensor_copy(pack[:, :, 2], bf_part[:, 0:EPP]))
            step(V.tensor_tensor(res, ew, pack[:, :, 2], ALU.subtract))
            step(V.tensor_copy(bf_part[:, 0:EPP], res))
            step(V.tensor_copy(pack[:, :, 3], bf_part[:, 0:EPP]))
            V.tensor_tensor(pack[:, :, 4], res, pack[:, :, 3], ALU.subtract).then_inc(S("pack_ready"), 1)
            dve.wait_ge(*reached("base_sum", 1))
            step(V.tensor_scalar(basef, psE[0:1, 0:NBLK], float(E - CHE), None, ALU.min))
            V.tensor_copy(base_i, basef).then_inc(S("base_ready"), 1)
            dve.wait_ge(*reached("iota_ready", 1))
            step(V.tensor_copy(iota_f[:], iota_i[:]))
            V.tensor_copy(iota_h, iota_f[:])
            dve.wait_ge(*reached("consts_ready", 1))
            V.tensor_copy(tri_b, tri_f)
            step(V.tensor_copy(tokid, tok_i))
            dve.wait_ge(*reached("params_loaded", 16 * PARAMS))
            V.tensor_scalar(bnp[4], bnp[4], BN_EPS, None, ALU.add)
            V.tensor_scalar(bnp[9], bnp[9], BN_EPS, None, ALU.add).then_inc(S("bn_var_ready"), 1)
            for w, heads, v0 in ((w_l0a, 4, 0), (w_l0b, 1, 2), (w_l2, 4, 4)):
                for n in range(2):
                    step(V.tensor_tensor(attm, w[:, :, 0:D], attv[v0 + n].unsqueeze(1).to_broadcast([128, KD, D]), ALU.mult))
                    step(V.tensor_reduce(w[:, :, D + n * heads:D + (n + 1) * heads],
                                         attm.rearrange("p k (h c) -> p k h c", h=heads), AX, ALU.add))
            dve.wait_ge(*reached("bn_pow_ready", 1))
            for n in (0, 5):
                b_, g_, be_, m_, v_ = bnp[n:n + 5]
                step(V.tensor_tensor(g_, g_, v_, ALU.mult))
                step(V.tensor_tensor(b_, b_, m_, ALU.subtract))
                step(V.tensor_tensor(b_, b_, g_, ALU.mult))
                ins = V.tensor_tensor(be_, be_, b_, ALU.add)
                step(ins)
            V.nop().then_inc(S("bn_ready"), 1)
            V.nop().then_inc(S("params_used"), 1)

            def onehots(s, b, sem_d, sem_s):
                e = ebt[s]
                V.tensor_tensor(ohd[s][:, :, 0, :], iota_f[0:P, bass.ds(b * WB, WB)].unsqueeze(1).to_broadcast([P, CH, WB]),
                                e[:, :, 1:2].to_broadcast([P, CH, WB]), ALU.is_equal).then_inc(S(sem_d), 1)
                for t in range(CH):
                    ins = V.tensor_scalar(ohs[s][:, t, 0:N], iota_h[0:P, 0:N], e[:, t, 0:1], None, ALU.is_equal)
                ins.then_inc(S(sem_s), 1)

            def block_onehots(i, q, first):
                b = 2 * i + q
                dve.wait_ge(*reached(f"edge_run_loaded{q}", 16 * i + 16))
                if not first:
                    dve.wait_ge(*reached("acc_ready", b - 1))
                onehots(q, b, "ohd_ready", "ohs_ready")

            block_onehots(0, 0, True)
            block_onehots(0, 1, True)
            with dve.Fori(1, NBLK // 2) as i:
                for q in range(2):
                    block_onehots(i, q, False)
            dve.wait_ge(*reached("counts_free", NBLK + 2))
            V.tensor_reduce(outdeg, ct[:], AX, ALU.add).then_inc(S("outdeg_ready"), 1)
            dve.wait_ge(*reached("total_sum", 1))
            step(V.tensor_reduce(flagf[:, 0:1], psE[0:1, 0:NT], AX, ALU.add))
            step(V.tensor_scalar(flagf[:, 1:2], flagf[:, 0:1], float(E), None, ALU.not_equal))
            V.tensor_copy(flag_i[:, 0:1], flagf[:, 1:2]).then_inc(S("flag_ready"), 1)
            dve.wait_ge(*reached("flag_ready", 1))
            missed = dve.value_load(flag_i[0:1, 0:1], min_val=0, max_val=1)
            with dve.If(missed == 1):
                V.memset(ct[:], 0.0)
                V.memset(wt[:], 0.0).then_inc(S("all_zeroed"), 1)
                dve.wait_ge(*reached("all_zeroed", 1))
                with dve.Fori(0, NBLK) as b:
                    with dve.Fori(0, NCHUNK) as c:
                        n = b * NCHUNK + c
                        dve.wait_ge(*reached("all_loaded", 16 * n + 16))
                        onehots(0, b, "all_ohd", "all_ohs")
                        dve.wait_ge(*reached("all_split", n + 1))
                        dve.wait_ge(*reached("all_added", n + 1))
                        ps = psC[0:P, 0:NT * 2 * WB].rearrange("p (j c) -> p j c", c=2 * WB)
                        cb, wb = ct[:, :, bass.ds(b * WB, WB)], wt[:, :, bass.ds(b * WB, WB)]
                        V.tensor_tensor(cb, ps[:, :, 0:WB], cb, ALU.add)
                        V.tensor_tensor(wb, ps[:, :, WB:], wb, ALU.add).then_inc(S("all_added"), 1)
                dve.wait_ge(*reached("all_added", NBLK * NCHUNK + 1))
                V.tensor_reduce(outdeg, ct[:], AX, ALU.add).then_inc(S("all_zeroed"), 1)
                dve.wait_ge(*reached("all_zeroed", 2))
            with dve.Else():
                V.nop()
            V.nop().then_inc(S("graph_ready"), 1)
            dve.wait_ge(*reached("at_copied", 1))
            for j in range(NT):
                d = at[:, j, j * P:(j + 1) * P]
                ins = V.tensor_tensor(d, ct[:, j, j * P:(j + 1) * P], ident[0:P, 0:P], ALU.add)
            ins.then_inc(S("at_ready"), 1)
            for j in range(NT):
                dve.wait_ge(*reached("at_turned", j + 1))
                V.tensor_scalar(cols(negm[:, j, :]), (psA, psB)[j % 2][0:P, 0:NT, 0:P], 0.5, NEG, ALU.is_lt, ALU.mult)\
                    .then_inc(S("negm_done"), 1)

            def normalise(tag, src, dst, sem):
                for j in range(NT):
                    ins = V.bn_stats(st6[:, j, :], src[:, j, :])
                step(ins)
                for j in range(NT):
                    ins = V.bn_aggr(mv[:, j, :], st6[:, j, :])
                step(ins)
                V.tensor_scalar(vare, mv[:, :, 1], LN_EPS, None, ALU.add).then_inc(S(tag + "_var"), 1)
                dve.wait_ge(*reached(tag + "_rstd", 1))
                for j in range(NT):
                    ins = V.tensor_scalar(dst[:, j, :], src[:, j, :], mv[:, j, 0:1], rstd[:, j:j + 1],
                                          ALU.subtract, ALU.mult)
                ins.then_inc(S(sem), 1)

            def turned(tag):
                dve.wait_ge(*reached(tag + "_turned1", 1))
                V.tensor_copy(cols(xT[:, 1, :]), psB[:, 0:NT, 0:P]).then_inc(S(tag + "_xT1"), 1)

            def attention(tag, heads, write):
                ch = D // heads
                nh = heads
                V.memset(hs[:, :, 0:heads * (ch + 1)].rearrange("p j (h c) -> p j h c", h=heads)[:, :, :, ch:ch + 1], 1.0)\
                    .then_inc(S(tag + "_ones"), 1)
                for h in range(heads):
                    dve.wait_ge(*reached(tag + "_bc", h + 1))
                    for j in range(NT):
                        ins = V.tensor_tensor_reduce(out=cols(junk), in0=(psA, psB)[h % 2][0:P, 0:NT, 0:P],
                                                     in1=cols(negm[:, j, :]), scale=1.0, scalar=NEG, op0=ALU.add,
                                                     op1=ALU.max, accum_out=mx[:, j, h:h + 1])
                        ins.then_inc(S(tag + "_masked"), 1)
                        dve.wait_ge(*reached(tag + "_masked", h * NT + j + 1))
                dve.wait_ge(*reached(tag + "_al", NT))
                ald, als = al[:, :, nh:2 * nh], al[:, :, 0:nh]
                z, m = zz[:, :, 0:nh], mx[:, :, 0:nh]
                step(V.tensor_tensor(z, m, ald, ALU.add))
                step(V.scalar_tensor_tensor(out=m, in0=z, scalar=SLOPE, in1=z, op0=ALU.mult, op1=ALU.max))
                V.tensor_scalar(al2[:, :, 0:nh], als, SLOPE, None, ALU.mult)
                V.tensor_tensor(r1[:, :, 0:nh], ald, m, ALU.subtract)
                V.scalar_tensor_tensor(out=r2[:, :, 0:nh], in0=ald, scalar=SLOPE, in1=m, op0=ALU.mult, op1=ALU.subtract)\
                    .then_inc(S(tag + "_rows"), 1)
                for h in range(heads):
                    dve.wait_ge(*reached(tag + "_u", h + 1))
                    dve.wait_ge(*reached(tag + "_v", h + 1))
                    V.tensor_tensor(u[h % 2], u[h % 2], v, ALU.max).then_inc(S(tag + "_max"), 1)
                    dve.wait_ge(*reached(tag + "_max", h + 1))
                    V.scalar_tensor_tensor(out=u[h % 2], in0=u[h % 2], scalar=1.0, in1=at[:], op0=ALU.min, op1=ALU.mult)\
                        .then_inc(S(tag + "_p"), 1)
                    write(h)

            def write_head(tag):
                def write(h):
                    dve.wait_ge(*reached(tag + "_agg", h + 1))
                    ps = (psC, psD)[h % 2][0:P, 0:NT * 65].rearrange("p (j c) -> p j c", c=65)
                    if tag == "l2a":
                        step(V.tensor_scalar(rden, ps[:, :, 64], 1e-16, None, ALU.add))
                        step(V.reciprocal(rden, rden))
                    else:
                        step(V.reciprocal(rden, ps[:, :, 64]))
                    V.tensor_tensor(gat[:, :, h * 64:(h + 1) * 64], ps[:, :, 0:64],
                                    rden.unsqueeze(2).to_broadcast([P, NT, 64]), ALU.mult).then_inc(S(tag + "_out"), 1)
                return write

            def write_l0b(h):
                for j in range(NT):
                    dve.wait_ge(*reached("l0b_agg", j + 1))
                    ps = (psC, psD)[j % 2]
                    step(V.reciprocal(rden[:, j:j + 1], ps[0:P, D:D + 1]))
                    V.scalar_tensor_tensor(out=x[:, j, :], in0=ps[0:P, 0:D], scalar=rden[:, j:j + 1], in1=x[:, j, :],
                                           op0=ALU.mult, op1=ALU.add).then_inc(S("l0b_out"), 1)

            def add_row(dst, src, rowv):
                return V.tensor_tensor(dst, src, rowv.unsqueeze(1).to_broadcast([P, NT, D]), ALU.add)

            dve.wait_ge(*reached("x_loaded", 16))
            normalise("l0g", x, xln, "l0g_xln")
            turned("l0g")
            add_row(x[:], x[:], b2_l0b[:]).then_inc(S("row_added"), 1)
            dve.wait_ge(*reached("row_added", 1))
            attention("l0a", 4, write_head("l0a"))
            dve.wait_ge(*reached("l0a_out", 4))
            V.nop().then_inc(S("l0a_done"), 1)
            attention("l0b", 1, write_l0b)
            dve.wait_ge(*reached("l0b_out", NT))

            def top(tag, lgt):
                for j in range(NT):
                    ins = V.max(mx8[:, j, :], lgt[:, j, :])
                step(ins)
                for j in range(NT):
                    ins = V.max_index(ix8[:, j, :], mx8[:, j, :], lgt[:, j, :])
                step(ins)
                step(V.tensor_copy(ixf, ix8[:, :, 0:2]))

            def onehot(dst, col, ne):
                return V.tensor_tensor(dst, iota_f[0:P, 0:ne].unsqueeze(1).to_broadcast([P, NT, ne]),
                                       ixf[:, :, col:col + 1].to_broadcast([P, NT, ne]), ALU.is_equal)

            def bias_rows(tag, each):
                dve.wait_ge(*reached(tag + "_wturned", 1))
                V.tensor_copy(cols(wgT), psA[0:8, 0:NT, 0:P]).then_inc(S(tag + "_wT"), 1)
                for j in range(NT):
                    dve.wait_ge(*reached(tag + "_bias", j + 1))
                    each(j, (psC, psD)[j % 2][0:P, 0:D]).then_inc(S(tag + "_bias_out"), 1)

            if stages >= 2:
                V.memset(zrow, 0.0).then_inc(S("zrow_ready"), 1)
                normalise("l0f", x, xln, "l0f_xln")
                turned("l0f")
                dve.wait_ge(*reached("l0f_logits", 1))
                step(V.tensor_copy(lg8, psC[0:P, 0:NT * E0].rearrange("p (j e) -> p j e", e=E0)))
                top("l0", lg8)
                step(onehot(oh0, 0, E0))
                V.tensor_copy(ohb0, oh0).then_inc(S("l0f_onehot"), 1)
                V.tensor_tensor(lg8, lg8, mx8[:, :, 0:1].to_broadcast([P, NT, E0]), ALU.subtract)\
                    .then_inc(S("shift0_ready"), 1)
                dve.wait_ge(*reached("l0_ranks", 1))
                step(V.tensor_tensor(t0, psD[0:P, 0:NT * E0].rearrange("p (j e) -> p j e", e=E0), oh0, ALU.mult))
                step(V.tensor_reduce(scol[:, :, 0], t0, AX, ALU.add))
                step(V.tensor_scalar(scol[:, :, 1], scol[:, :, 0], CAP + 0.5, None, ALU.is_lt))
                step(V.tensor_scalar(scol[:, :, 0], scol[:, :, 0], float(CAP), -1.0, ALU.min, ALU.add))
                step(V.scalar_tensor_tensor(out=scol[:, :, 0], in0=ixf[:, :, 0], scalar=float(CAP), in1=scol[:, :, 0],
                                            op0=ALU.mult, op1=ALU.add))
                step(V.tensor_copy(sloti[:, :, 1], scol[:, :, 0]))
                step(V.scalar_tensor_tensor(out=scol[:, :, 2], in0=tokid, scalar=float(E0 * CAP), in1=scol[:, :, 0],
                                            op0=ALU.add, op1=ALU.subtract))
                step(V.tensor_scalar(zz[:, :, 0], scol[:, :, 1], -1.0, 1.0, ALU.mult, ALU.add))
                step(V.tensor_tensor(scol[:, :, 2], scol[:, :, 2], zz[:, :, 0], ALU.mult))
                step(V.tensor_tensor(scol[:, :, 2], scol[:, :, 2], scol[:, :, 0], ALU.add))
                V.tensor_copy(sloti[:, :, 0], scol[:, :, 2]).then_inc(S("slots0_ready"), 1)
                dve.wait_ge(*reached("exp0_ready", 1))
                step(V.tensor_reduce(zz[:, :, 0], ex8, AX, ALU.add))
                step(V.reciprocal(zz[:, :, 0], zz[:, :, 0]))
                step(V.tensor_tensor(rden, zz[:, :, 0], scol[:, :, 1], ALU.mult))
                bias_rows("l0f", lambda j, ps: V.tensor_copy(clip[:, j, :], ps))
                dve.wait_ge(*reached("bufs_turned1", 1))
                V.tensor_copy(bufT[:, 1, :].rearrange("p (e c) -> p e c", e=E0), psB[:, :, 0:CAP]).then_inc(S("bufT1"), 1)
                V.nop().then_inc(S("l0_y_free"), 2)
                with dve.Fori(0, 2) as r:
                    for q in range(4):
                        e = 4 * r + q
                        dve.wait_ge(*reached("l0_y", e + 1))
                        V.tensor_copy(ysb[:, bass.ds(e, 1), :].rearrange("p a d -> p (a d)"), (psC, psD)[q % 2][0:CAP, 0:D])\
                            .then_inc(S("l0_y_free"), 1)
                dve.wait_ge(*reached("l0_y_free", E0 + 2))
                V.nop().then_inc(S("ysb_ready"), 1)
                dve.wait_ge(*reached("l0_tokens_back", 16 * NT))
                step(V.tensor_tensor(yg0, yg0, clip, ALU.add))
                step(V.tensor_tensor(yg0, yg0, rden.unsqueeze(2).to_broadcast([P, NT, D]), ALU.mult))
                step(V.tensor_scalar(clip, yg0, 1e4, -1e4, ALU.min, ALU.max))
                step(V.tensor_tensor(nan_m, yg0, yg0, ALU.not_equal))
                step(V.tensor_scalar(bound, yg0, FLT_MAX, -FLT_MAX, ALU.min, ALU.max))
                step(V.tensor_tensor(inf_m, bound, yg0, ALU.not_equal))
                step(V.copy_predicated(yg0, inf_m, clip))
                step(V.memset(clip, 0.0))
                step(V.copy_predicated(yg0, nan_m, clip))
                step(V.tensor_tensor(x[:], x[:], yg0, ALU.add))
            if stages >= 3:
                V.tensor_scalar(outdeg, outdeg, 1.0, None, ALU.max).then_inc(S("deg_ready"), 1)
                V.memset(hs[:, :, 64:65], 1.0).then_inc(S("gcn_ones"), 1)
                normalise("l1g", x, xln, "l1g_xln")
                turned("l1g")
                dve.wait_ge(*reached("b_out_loaded", 16))
                step(add_row(x[:], x[:], b_out[:]))
                dve.wait_ge(*reached("gcn_agg", 1))
                ps = psE[0:P, 0:NT * 65].rearrange("p (j c) -> p j c", c=65)
                V.tensor_scalar(vare, ps[:, :, 64], 1.0, None, ALU.max).then_inc(S("indeg_ready"), 1)
                dve.wait_ge(*reached("ndst_ready", 1))
                V.tensor_tensor(agg, ps[:, :, 0:64], rden.unsqueeze(2).to_broadcast([P, NT, 64]), ALU.mult)\
                    .then_inc(S("gcn_scaled"), 1)
                for j in range(NT):
                    dve.wait_ge(*reached("gcn_y", j + 1))
                    V.tensor_tensor(x[:, j, :], (psC, psD)[j % 2][0:P, 0:D], x[:, j, :], ALU.add).then_inc(S("gcn_out"), 1)
                dve.wait_ge(*reached("gcn_out", NT))
            if stages >= 4:
                normalise("l1f", x, xln, "l1f_xln")
                turned("l1f")
                dve.wait_ge(*reached("l1f_logits", 1))
                step(V.tensor_copy(lg, psC[0:P, 0:NT * E1].rearrange("p (j e) -> p j e", e=E1)))
                top("l1", lg)
                V.tensor_tensor(gsel[:, :, 0], mx8[:, :, 1], mx8[:, :, 0], ALU.subtract).then_inc(S("shift1_ready"), 1)
                onehot(oh1[:, 0:NT, :], 0, E1)
                step(onehot(oh1[:, NT:, :], 1, E1))
                V.tensor_tensor(ohb1, oh1[:, 0:NT, :], oh1[:, NT:, :], ALU.add).then_inc(S("l1f_onehot"), 1)
                dve.wait_ge(*reached("l1_ranks", 1))
                V.tensor_copy(cntcol, psF[0:E1, 0:1]).then_inc(S("cntcol_ready"), 1)
                V.tensor_copy(pos1, psD[0:P, 0:NT * E1].rearrange("p (j e) -> p j e", e=E1))
                V.tensor_copy(cntb, psE[0:P, 0:E1])
                dve.wait_ge(*reached("l1_offsets", 1))
                step(V.tensor_copy(offb, psC[0:P, 0:E1]))
                step(V.tensor_tensor(pos1, pos1, offb.unsqueeze(1).to_broadcast([P, NT, E1]), ALU.add))
                for k in range(2):
                    step(V.tensor_tensor(t1, pos1, oh1[:, k * NT:(k + 1) * NT, :], ALU.mult))
                    step(V.tensor_reduce(scol[:, :, k], t1, AX, ALU.add))
                    step(V.tensor_scalar(scol[:, :, k], scol[:, :, k], -1.0, None, ALU.add))
                    ins = V.tensor_copy(sloti[:, :, k], scol[:, :, k])
                ins.then_inc(S("slots1_ready"), 1)
                dve.wait_ge(*reached("exp1_ready", 1))
                step(V.tensor_scalar(gsel[:, :, 0], gsel[:, :, 1], 1.0, None, ALU.add))
                step(V.reciprocal(gsel[:, :, 0], gsel[:, :, 0]))
                step(V.tensor_tensor(gsel[:, :, 1], gsel[:, :, 1], gsel[:, :, 0], ALU.mult))
                for r in range(ROUNDS):
                    ins = V.scalar_tensor_tensor(out=starts_f[:, :, r], in0=cntb[0:1, :], scalar=float(r * WIN),
                                                 in1=offb[0:1, :], op0=ALU.min, op1=ALU.add)
                step(V.tensor_reduce(flagf[:, 2:3], cntb[0:1, :], AX, ALU.max))
                step(V.tensor_scalar(flagf[:, 3:4], flagf[:, 2:3], WIN + 0.5, None, ALU.is_gt))
                V.tensor_copy(starts, starts_f)
                V.memset(xsT[:, :, SLOTS:], 0.0)
                V.tensor_copy(flag2_i[:, 0:1], flagf[:, 3:4]).then_inc(S("flag2_ready"), 1)
                for g in range(2):
                    dve.wait_ge(*reached("xs_turned", 2 * g + 2))
                    V.tensor_copy(xsT[:, 1, g * N:(g + 1) * N].rearrange("p (j q) -> p j q", q=P), psB[:, 0:NT, 0:P])\
                        .then_inc(S("xsT_dve"), 1)
                dve.wait_ge(*reached("flag2_ready", 1))
                full = dve.value_load(flag2_i[0:1, 0:1], min_val=0, max_val=1)

                def out1(ps, e, start):
                    for m in range(KD):
                        ins = V.tensor_scalar(yT[:, m, bass.ds(start, WIN)], ps[:, m, 0:WIN], b2T1[:, m, bass.ds(e, 1)], None,
                                              ALU.add)
                    return ins

                V.nop().then_inc(S("l1_y_free"), 2)
                V.nop().then_inc(S("any_y_free"), 1)
                V.nop().then_inc(S("any_expert_used"), 1)
                with dve.If(full == 1):
                    with dve.Fori(0, E1) as e:
                        with dve.Fori(0, ROUNDS) as r:
                            n = e * ROUNDS + r
                            start = dve.value_load(starts[0:1, bass.ds(e, 1), bass.ds(r, 1)].rearrange("p a b -> p (a b)"),
                                                   min_val=0, max_val=SLOTS)
                            dve.wait_ge(*reached("any_y", n + 1))
                            dve.wait_ge(*reached("any_y_free", n + 1))
                            out1(psA, e, start).then_inc(S("any_y_free"), 1)
                        V.nop().then_inc(S("any_expert_used"), 1)
                    dve.wait_ge(*reached("any_y_free", E1 * ROUNDS + 1))
                with dve.Else():
                    with dve.Fori(0, E1 // RING) as r:
                        for q in range(RING):
                            e = r * RING + q
                            start = dve.value_load(starts[0:1, bass.ds(e, 1), 0:1].rearrange("p a b -> p (a b)"),
                                                   min_val=0, max_val=SLOTS)
                            dve.wait_ge(*reached("l1_used", e + 1))
                            dve.wait_ge(*reached("l1_y_free", e + 2))
                            out1((psA, psB)[q % 2], e, start).then_inc(S("l1_y_free"), 1)
                    dve.wait_ge(*reached("l1_y_free", E1 + 2))
                V.nop().then_inc(S("yT_ready"), 1)
                V.nop().then_inc(S("l1_experts_done"), 1)
                for g in (1, 3):
                    dve.wait_ge(*reached("ys_turned", g + 1))
                    V.tensor_copy(xs[:, 2 * g:2 * g + 2, :].rearrange("p t (m d) -> p (t m) d", m=2), psB[0:P, 0:4, 0:128])\
                        .then_inc(S("ys_dve"), 1)
                dve.wait_ge(*reached("ys_act", 3))
                dve.wait_ge(*reached("ys_dve", 2))
                V.nop().then_inc(S("ys_ready"), 1)
                dve.wait_ge(*reached("l1_tokens_back", 32 * NT))
                for k in range(2):
                    for j in range(NT):
                        ins = V.scalar_tensor_tensor(out=x[:, j, :], in0=yg1[:, k * NT + j, :], scalar=gsel[:, j, k:k + 1],
                                                     in1=x[:, j, :], op0=ALU.mult, op1=ALU.add)
                    step(ins)
            if stages >= 5:
                normalise("l2g", x, xln, "l2g_xln")
                turned("l2g")
                attention("l2a", 4, write_head("l2a"))
                dve.wait_ge(*reached("l2a_out", 4))
                dve.wait_ge(*reached("l2_rows_loaded", 48))
                step(add_row(gat, gat, l2_bias))
                normalise("l2n", gat, gat, "l2n_xln")
                dve.wait_ge(*reached("l2n_xln", 1))
                step(V.tensor_tensor(gat, gat, l2_gamma.unsqueeze(1).to_broadcast([P, NT, D]), ALU.mult))
                step(add_row(x[:], x[:], l2_beta))
                step(V.tensor_tensor(x[:], x[:], gat, ALU.add))

            def dense(tag, two):
                normalise(tag, x, xln, tag + "_xln")
                turned(tag)
                dve.wait_ge(*reached(tag + "_logits", 1))
                step(V.tensor_copy(lg8, psC[0:P, 0:NT * 8].rearrange("p (j e) -> p j e", e=8)))
                top(tag, lg8)
                V.tensor_tensor(lg8, lg8, mx8[:, :, 0:1].to_broadcast([P, NT, 8]), ALU.subtract).then_inc(S(tag + "_shift"), 1)
                if two:
                    onehot(t8, 0, 8)
                    step(onehot(wgt, 1, 8))
                    step(V.tensor_tensor(t8, t8, wgt, ALU.add))
                    step(V.tensor_tensor(x[:], x[:], xln[:], ALU.add))
                dve.wait_ge(*reached(tag + "_exp", 1))
                step(V.tensor_reduce(zz[:, :, 0], ex8, AX, ALU.add))
                step(V.reciprocal(zz[:, :, 0], zz[:, :, 0]))
                ins = V.tensor_tensor(wgt, ex8, zz[:, :, 0:1].to_broadcast([P, NT, 8]), ALU.mult)
                if two:
                    step(ins)
                    step(V.tensor_tensor(wgt, wgt, t8, ALU.mult))
                    step(V.tensor_reduce(zz[:, :, 0], wgt, AX, ALU.add))
                    step(V.tensor_scalar(zz[:, :, 0], zz[:, :, 0], 1e-12, None, ALU.max))
                    step(V.reciprocal(zz[:, :, 0], zz[:, :, 0]))
                    ins = V.tensor_tensor(wgt, wgt, zz[:, :, 0:1].to_broadcast([P, NT, 8]), ALU.mult)
                ins.then_inc(S(tag + "_w"), 1)
                bias_rows(tag, lambda j, ps: V.tensor_tensor(x[:, j, :], ps, x[:, j, :], ALU.add))
                dve.wait_ge(*reached(tag + "_bias_out", NT))
                V.nop().then_inc(S(tag + "_y_free"), 2)
                with dve.Fori(0, E2 // 2) as r:
                    for q in range(2):
                        for j in range(NT):
                            n = (2 * r + q) * NT + j
                            dve.wait_ge(*reached(tag + "_y", n + 1))
                            dve.wait_ge(*reached(tag + "_y_free", n + 1))
                            V.scalar_tensor_tensor(out=x[:, j, :], in0=(psC, psD)[(q * NT + j) % 2][0:P, 0:D],
                                                   scalar=wgt[:, j, bass.ds(2 * r + q, 1)], in1=x[:, j, :],
                                                   op0=ALU.mult, op1=ALU.add).then_inc(S(tag + "_y_free"), 1)
                dve.wait_ge(*reached(tag + "_y_free", E2 * NT + 2))

            if stages >= 6:
                dense("l2f", False)
            if stages >= 7:
                normalise("l3g", x, xln, "l3g_xln")
                turned("l3g")
                for j in range(NT):
                    dve.wait_ge(*reached("l3_agg", j + 1))
                    V.scalar_tensor_tensor(out=x[:, j, :], in0=(psC, psD)[j % 2][0:P, 0:D], scalar=0.0, in1=x[:, j, :],
                                           op0=ALU.max, op1=ALU.add).then_inc(S("l3_out"), 1)
                dve.wait_ge(*reached("l3_out", NT))
            if stages >= 8:
                dense("l3f", True)
            V.nop().then_inc(S("x_final"), 1)


NAMES = ["x", "src", "dst", "edge_weight"] + ["L0_gnn_" + n for n in (
    "W1", "att_src1", "att_dst1", "b1", "W2", "att_src2", "att_dst2", "b2")] + ["L0_ffn_" + n for n in (
    "gate_w", "gate_b", "w1", "b1", "w2", "b2")] + ["L1_gnn_" + n for n in ("W_gcn", "b_gcn", "W_out", "b_out")] + [
    "L1_ffn_" + n for n in ("Wr", "br", "W1", "b1", "W2", "b2")] + ["L2_gnn_" + n for n in (
    "W", "att_src", "att_dst", "bias", "gamma", "beta")] + ["L2_ffn_" + n for n in (
    "Wr", "br", "W1", "b1", "g1", "be1", "m1", "v1", "W2", "b2", "g2", "be2", "m2", "v2", "Wo", "bo")] + [
    "L3_gnn_weight"] + ["L3_ffn_" + n for n in ("router_w", "w1", "b1", "w2", "b2")]


def kernel(**inputs):
    import numpy as np
    import concourse.bacc as bacc
    from concourse.bass_utils import run_bass_kernel_spmd

    nc = bacc.Bacc("TRN2", target_bir_lowering=False, num_devices=1)
    arrays, aps = {}, {}
    for name in NAMES:
        v = np.ascontiguousarray(inputs[name])
        arrays["in_" + name] = v
        aps[name] = nc.dram_tensor("in_" + name, v.shape, mybir.dt.from_np(v.dtype), kind="ExternalInput").ap()
    out = nc.dram_tensor("out_x", (N, D), F32, kind="ExternalOutput").ap()
    build(nc, aps, out)
    r = run_bass_kernel_spmd(nc, [arrays], core_ids=[0])
    return r.results[0]["out_x"]
```

```python
from contextlib import ExitStack

import concourse.bass as bass
from concourse import mybir

F32 = mybir.dt.float32
I32 = mybir.dt.int32
U32 = mybir.dt.uint32
BF16 = mybir.dt.bfloat16
F16 = mybir.dt.float16
ALU = mybir.AluOpType
ACT = mybir.ActivationFunctionType
AX = mybir.AxisListType.X

N, D, E = 625, 256, 20625
P, NT = 125, 5
KD = D // 128
EPP = E // P
CH = 10
CHE = CH * P
CHA = 5
NCHUNK = E // (CHA * P)
WB = 32
NBLK = (N + WB - 1) // WB
NPAD = NBLK * WB
LN_EPS, BN_EPS, SLOPE = 1e-5, 1e-3, 0.2
NEG = -1e30
E0, F0, CAP = 8, 1024, 98
E1, F1 = 64, 512
SLOTS = 2 * N
WIN = 96
ROUNDS = (N + WIN - 1) // WIN
E2 = 8
CHUNK = 2048
RING = 8
DENSE = {"l2f": (("L2_ffn_W1", "L2_ffn_W2", "L2_ffn_Wo"), (0, 1, 4, 5)),
         "l3f": (("L3_ffn_w1", "L3_ffn_w2"), (2, 3, 6, 7))}
FLT_MAX = 3.4028235e38
PARAMS = 27


TAGS = ("l0g", "l0a", "l0m", "l0b", "l0f", "l1g", "l1f", "l2g", "l2a", "l2n", "l2f", "l3g", "l3f")
NORMS = ("l0g", "l0f", "l1g", "l1f", "l2g", "l2n", "l2f", "l3g", "l3f")
TURNS = ("l0g", "l0m", "l0f", "l1g", "l1f", "l2g", "l2f", "l3g", "l3f")
ATTS = ("l0a", "l0b", "l2a")
HEADS = {"l0a": 4, "l0b": 1, "l2a": 4}
RECURRING = {k: (NORMS, 1) for k in ("var", "rstd", "xln")}
RECURRING |= {k: (TURNS, 1) for k in ("turned0", "turned1", "xT0", "xT1")}
RECURRING |= {k: (ATTS, NT) for k in ("proj", "hs", "al")}
RECURRING |= {k: (ATTS, 1) for k in ("ones", "rows")}
RECURRING |= {k: (ATTS, HEADS) for k in ("bc", "r1", "r2")}
RECURRING |= {k: (ATTS, {t: n * NT for t, n in HEADS.items()}) for k in ("masked", "u", "v", "max", "p")}
RECURRING |= {"agg": (ATTS, {"l0a": 4 * NT, "l0b": NT + 1, "l2a": 4 * NT}), "out": (ATTS, {"l0a": 4, "l0b": NT, "l2a": 4})}
RECURRING |= {"logits": (("l0f", "l1f", "l2f", "l3f"), 1), "onehot": (("l0f", "l1f"), 1)}
RECURRING |= {k: (("l0f", "l2f", "l3f"), 1) for k in ("wturned", "wT")}
RECURRING |= {k: (("l0f", "l2f", "l3f"), NT) for k in ("bias", "bias_out")}
RECURRING |= {k: (("l2f", "l3f"), 1) for k in ("shift", "exp", "w")}
RECURRING |= {"hidden": (("l2f", "l3f"), {"l2f": 2 * KD * E2, "l3f": KD * E2})}
RECURRING |= {"act": (("l2f", "l3f"), {"l2f": 2 * KD * E2 + 2, "l3f": KD * E2 + 2})}
RECURRING |= {"y": (("l2f", "l3f"), NT * E2), "y_free": (("l2f", "l3f"), NT * E2 + 2)}

ONCE = {
    "dve_stage": ("pack_ready", "base_ready", "l0a_folded", "flag_ready", "graph_ready", "at_ready", "bn_var_ready",
                  "row_added", "l0a_done", "l0b_folded", "params_used", "bn_ready", "zrow_ready", "shift0_ready", "slots0_ready", "bufT1",
                  "ysb_ready", "deg_ready", "gcn_ones", "indeg_ready", "gcn_scaled", "shift1_ready", "cntcol_ready",
                  "slots1_ready", "flag2_ready", "yT_ready", "l1_experts_done", "ys_ready", "x_final"),
    "pe_stage": ("base_sum", "total_sum", "params_acc", "l0_ranks", "bufs_turned0", "bufs_turned1", "gcn_agg",
                 "gcn_turned", "l1_ranks", "l1_offsets"),
    "act_stage": ("params_turned", "exp0_ready", "bufT0", "gcn_hT", "exp1_ready"),
    "pool_stage": ("iota_ready", "consts_ready", "bn_pow_ready", "nsrc_ready", "ndst_ready"),
}
STAGE_OF = {name: (sem, n) for sem, names in ONCE.items() for n, name in enumerate(names)}


class Steps:

    def __init__(self, sem):
        self.sem, self.n = sem, 0

    def done(self, ins):
        ins.then_inc(self.sem, 1)
        self.n += 1

    def wait(self, eng):
        eng.wait_ge(self.sem, self.n)


def build(nc, a, out, stages=8):
    with ExitStack() as ctx:
        def sb(name, shape, dt=F32):
            return ctx.enter_context(nc.sbuf_tensor(name, shape, dt))

        def pb(name, shape, dt=F32):
            return ctx.enter_context(nc.psum_tensor(name, shape, dt))

        sems = {}

        def S(name):
            if name[:3] in TAGS and name[4:] in RECURRING:
                name = "each_" + name[4:]
            elif name in STAGE_OF:
                name = STAGE_OF[name][0]
            if name not in sems:
                sems[name] = ctx.enter_context(nc.semaphore(name))
            return sems[name]

        def reached(name, count):
            tag, kind = name[:3], name[4:]
            if tag in TAGS and kind in RECURRING:
                order, per = RECURRING[kind]
                for t in order[:order.index(tag)]:
                    count = count + (per[t] if isinstance(per, dict) else per)
            elif name in STAGE_OF:
                count = count + STAGE_OF[name][1]
            return S(name), count

        edges_d = nc.dram_tensor("edges_d", (E, 5), F32, kind="Internal").ap()
        buf_d = nc.dram_tensor("buf_d", (E0 * CAP + N, D), F32, kind="Internal").ap()
        ybuf_d = nc.dram_tensor("ybuf_d", (E0 * CAP, D), F32, kind="Internal").ap()
        xs_d = nc.dram_tensor("xs_d", (SLOTS, D), F32, kind="Internal").ap()
        ys_d = nc.dram_tensor("ys_d", (SLOTS, D), F32, kind="Internal").ap()

        x = sb("x", [P, NT, D])
        xln = sb("xln", [P, NT, D])
        xT = sb("xT", [128, KD, N])
        ct = sb("ct", [P, NT, NPAD])
        wt = sb("wt", [P, NT, NPAD])
        at = sb("at", [P, NT, NPAD])
        negm = sb("negm", [P, NT, N])
        ring = sb("ring", [128, RING * CHUNK])
        work = sb("work", [128, 12100])
        hs = sb("hs", [P, NT, 260])
        small = sb("small", [128, 1904])

        class Carver:
            def __init__(self, tile):
                self.tile, self.at = tile, 0

            def __call__(self, shape, dt=F32, parts=128):
                n = 1
                for s in shape:
                    n *= s
                words = (n + 1) // 2 if dt in (BF16, F16) else n
                v = self.tile[0:parts, self.at:self.at + words]
                self.at += words
                assert self.at <= self.tile.shape[1], self.at
                if dt != F32:
                    v = v.bitcast(dt)[:, 0:n]
                if len(shape) == 2:
                    v = v.rearrange("p (a b) -> p a b", a=shape[0])
                elif len(shape) == 3:
                    v = v.rearrange("p (a b c) -> p a b c", a=shape[0], b=shape[1])
                return v

        sm = Carver(small)
        ident = sb("ident", [128, 128])
        iota_i = sb("iota_i", [128, NPAD], I32)
        iota_f = sb("iota_f", [128, NPAD])
        iota_h = iota_i[:, 0:NPAD // 2].bitcast(F16)
        sel = sb("sel", [128, 2 * WB])
        tri_b = sm([P], BF16, P)
        tri_f = sm([P], F32, P)
        ones_bf = sm([P], BF16, P)
        strict = sm([E1], F32, E1)
        ones_f = sm([128], F32)
        half_neg = sm([D])
        w_l0a = sb("w_l0a", [128, KD, D + 8])
        w_l0b = sb("w_l0b", [128, KD, D + 2])
        w_l2 = sb("w_l2", [128, KD, D + 8])
        w_l3 = w_l0a[:, :, 0:D]
        w_gcn = sb("w_gcn", [128, KD, 64])
        w_out = sb("w_out", [64, D])
        gate0 = sb("gate0", [128, KD, E0])
        gate1 = sb("gate1", [128, KD, E1])
        gate2 = sb("gate2", [128, KD, E2])
        gate3 = sb("gate3", [128, KD, E2])
        rbias = sb("rbias", [1, E0 + E1 + E2])
        b1_l0a = sb("b1_l0a", [128, KD])
        b_gcn = sb("b_gcn", [64, 1])
        b2_l0b = sb("b2_l0b", [P, D])
        b_out = b2_l0b
        b1T0 = sb("b1T0", [128, F0 // 128, E0])
        b1T1 = sb("b1T1", [128, F1 // 128, E1])
        b2T1 = sb("b2T1", [128, KD, E1])
        bnT = sb("bnT", [128, 10, KD, E2])
        b1T3 = sb("b1T3", [128, KD, E2])
        brow = sb("brow", [E2, D])

        psA = pb("psA", [128, 8, 128])
        psB = pb("psB", [128, 8, 128])
        psC = pb("psC", [128, 512])
        psD = pb("psD", [128, 512])
        psE = pb("psE", [128, 512])
        psF = pb("psF", [128, 512])

        st6 = sm([NT, 6], F32, P)
        mv = sm([NT, 2], F32, P)
        vare = sm([NT], F32, P)
        rstd = sm([NT], F32, P)
        al = sm([NT, 8], F32, P)
        al2 = sm([NT, 4], F32, P)
        mx = sm([NT, 4], F32, P)
        zz = sm([NT, 4], F32, P)
        r1 = sm([NT, 4], F32, P)
        r2 = sm([NT, 4], F32, P)
        rden = sm([NT], F32, P)
        outdeg = sm([NT], F32, P)
        nsrc = sm([NT], F32, P)
        cnt = sm([NBLK], F32, P)
        basef = sm([NBLK], F32, 1)
        base_i = sm([NBLK], I32, 1)
        flagf = sm([4], F32, 1)
        flag_i = sm([2], I32, 1)
        flag2_i = sm([2], I32, 1)
        scol = sm([NT, 3], F32, P)
        mx8 = sm([NT, 8], F32, P)
        ix8 = sm([NT, 8], U32, P)
        ixf = sm([NT, 2], F32, P)
        wgt = sm([NT, 8], F32, P)
        wgT = sm([N], F32, 8)
        gsel = sm([NT, 2], F32, P)
        sloti = sm([NT, 4], I32, P)
        tokid = sm([NT], F32, P)
        tok_i = sm([NT], I32, P)
        cntcol = sm([1], F32, E1)

        wk = Carver(work)
        ohs = [wk([CH, N + 1], BF16, P) for _ in range(2)]
        ohd = [wk([CH, 4, WB], BF16, P) for _ in range(2)]
        accs = [wk([N]) for _ in range(2)]
        ebt = [wk([CH, 5], F32, P) for _ in range(2)]
        rk = Carver(ring)
        src_i = rk([EPP], I32, P)
        dst_i = rk([EPP], I32, P)
        ew = rk([EPP], F32, P)
        res = rk([EPP], F32, P)
        bf_part = rk([EPP + 1], BF16, P)
        pack = rk([EPP, 5], F32, P)
        junk_e = rk([EPP], F32, P)
        b1r0 = rk([F0], F32, E0)
        b1r1 = rk([F1], F32, E1)
        b2r1 = rk([D], F32, E1)
        bnp = [rk([D], F32, E2) for _ in range(10)]
        b1r3 = rk([D], F32, E2)
        rw3 = rk([D], F32, E2)
        attv = [rk([D]) for _ in range(6)]
        attm = rk([KD, D])
        wk = Carver(work)
        u = [wk([NT, N], F32, P) for _ in range(2)]
        v = wk([NT, N], F32, P)
        gat = wk([NT, D], F32, P)
        l2_bias = wk([D], F32, P)
        l2_gamma = wk([D], F32, P)
        l2_beta = wk([D], F32, P)
        wk = Carver(work)
        bufs = wk([E0, D], F32, CAP)
        bufT = wk([KD, E0 * CAP])
        h0 = wk([F0 // 128, CAP])
        ysb = wk([E0, D], F32, CAP)
        yg0 = wk([NT, D], F32, P)
        nan_m = wk([NT, D], I32, P)
        clip = wk([NT, D], F32, P)
        bound = work[0:P, 0:NT * D].rearrange("p (a b) -> p a b", a=NT)
        inf_m = work[0:P, NT * D:2 * NT * D].bitcast(I32).rearrange("p (a b) -> p a b", a=NT)
        oh0 = wk([NT, E0], F32, P)
        ohb0 = wk([NT, E0], BF16, P)
        t0 = wk([NT, E0], F32, P)
        zrow = wk([D], F32, CAP)
        wk = Carver(work)
        xs = wk([2 * NT, D], F32, P)
        xsT = wk([KD, SLOTS + WIN])
        yT = wk([KD, SLOTS + WIN])
        yg1 = xsT[0:P].rearrange("p k n -> p (k n)")[:, 0:2 * NT * D].rearrange("p (t d) -> p t d", d=D)
        h1 = [wk([F1 // 128, WIN]) for _ in range(2)]
        oh1 = wk([2 * NT, E1], F32, P)
        ohb1 = wk([NT, E1], BF16, P)
        pos1 = wk([NT, E1], F32, P)
        t1 = wk([NT, E1], F32, P)
        lg = wk([NT, E1], F32, P)
        offb = wk([E1], F32, P)
        cntb = wk([E1], F32, P)
        starts_f = wk([E1, ROUNDS], F32, 1)
        starts = wk([E1, ROUNDS], I32, 1)
        wk = Carver(work)
        h1d = [wk([KD, N]) for _ in range(2)]
        h2d = [wk([KD, N]) for _ in range(2)]
        lg8 = sm([NT, 8], F32, P)
        ex8 = sm([NT, 8], F32, P)
        t8 = sm([NT, 8], F32, P)
        agg = work[0:P, 0:NT * 64].rearrange("p (a b) -> p a b", a=NT)
        hT = work[0:64, 400:400 + N]

        def cols(ap):
            return ap.rearrange("p (j q) -> p j q", q=P)

        def hidden0(f):
            return (psA, psB)[f // 4][:, f // 2 % 2 * 4 + f % 2, 0:CAP]

        def hidden1_ps(f):
            return (psC, psD, psE, psF)[f][:, 0:WIN]

        def slot(s):
            return ring[:, s * CHUNK:(s + 1) * CHUNK]

        tokens_by_tile = "(j p) d -> p j d"
        last_out = psA[0:P].rearrange("p a b -> p (a b)")[:, 0:D + 1]

        def kpn(w):
            return w.rearrange("(k p) n -> p k n", p=128)

        block = ctx.enter_context(nc.Block())

        @block.sync
        def _(sp):
            sp.dma_start(dst_i, a["dst"].rearrange("(p t) -> p t", t=EPP)).then_inc(S("dst_loaded"), 16)
            sp.dma_start(src_i, a["src"].rearrange("(p t) -> p t", t=EPP)).then_inc(S("edges_loaded"), 16)
            sp.dma_start(ew, a["edge_weight"].rearrange("(p t) -> p t", t=EPP)).then_inc(S("edges_loaded"), 16)
            sp.dma_start(x[:], a["x"].rearrange(tokens_by_tile, p=P)).then_inc(S("x_loaded"), 16)

            sp.wait_ge(*reached("pack_ready", 1))
            sp.dma_start(edges_d.rearrange("(p t) k -> p (t k)", t=EPP), pack.rearrange("p t k -> p (t k)"))\
                .then_inc(S("edges_packed"), 16)
            sp.wait_ge(*reached("edges_packed", 16))
            sp.wait_ge(*reached("base_ready", 1))

            def edge_run(start, n):
                return edges_d[bass.ds(start, n * P), :].rearrange("(p t) k -> p (t k)", t=n)

            def load_run(b, q):
                base = sp.value_load(base_i[0:1, bass.ds(b, 1)], min_val=0, max_val=E - CHE)
                sp.dma_start(ebt[q].rearrange("p t k -> p (t k)"), edge_run(base, CH))\
                    .then_inc(S(f"edge_run_loaded{q}"), 16)

            for q in range(2):
                load_run(q, q)
            with sp.Fori(1, NBLK // 2) as i:
                for q in range(2):
                    sp.wait_ge(*reached("ohs_ready", 2 * i + q - 1))
                    sp.wait_ge(*reached("kinds_ready", 2 * i + q - 1))
                    load_run(2 * i + q, q)

            sp.wait_ge(*reached("flag_ready", 1))
            missed = sp.value_load(flag_i[0:1, 0:1], min_val=0, max_val=1)
            with sp.If(missed == 1):
                with sp.Fori(0, NBLK) as b:
                    with sp.Fori(0, NCHUNK) as c:
                        sp.wait_ge(*reached("all_added", b * NCHUNK + c + 1))
                        sp.dma_start(ebt[0][:, 0:CHA].rearrange("p t k -> p (t k)"), edge_run(c * (CHA * P), CHA))\
                            .then_inc(S("all_loaded"), 16)
            with sp.Else():
                sp.nop()
            sp.nop()

            sp.wait_ge(*reached("params_used", 1))
            sp.wait_ge(*reached("params_acc", 1))

            def load_l0(c):
                e, half = c // 2, c % 2
                s = c % RING
                src = (a["L0_ffn_w2"] if half else a["L0_ffn_w1"])[e]
                sp.dma_start(slot(s).rearrange("p (k n) -> p k n", k=8 if half else KD), kpn(src))\
                    .then_inc(S(f"l0_weights{s}"), 16)

            for c in range(RING):
                load_l0(c)

            sp.wait_ge(*reached("l0a_proj", NT))
            sp.dma_start(w_l3, kpn(a["L3_gnn_weight"])).then_inc(S("w_l3_loaded"), 16)
            if stages >= 2:
                sp.wait_ge(*reached("zrow_ready", 1))
                for e in range(E0):
                    sp.dma_start(buf_d[e * CAP:(e + 1) * CAP, :], zrow).then_inc(S("buf_zeroed"), 16)
                sp.wait_ge(*reached("tokens_sent0", 16 * NT))
                sp.dma_start(bufs, buf_d[0:E0 * CAP, :].rearrange("(e c) d -> c e d", e=E0))\
                    .then_inc(S("bufs_loaded"), 16)
                for c in range(RING, 2 * RING):
                    e = (c - RING) // 2
                    if c % 2:
                        sp.wait_ge(*reached("l0_y", e + 1))
                    else:
                        sp.wait_ge(*reached("l0_hidden", (e + 1) * (F0 // 256)))
                    load_l0(c)

            def load_l1(e, s):
                sp.dma_start(slot(s)[:, 0:CHUNK // 2].rearrange("p (k n) -> p k n", k=KD),
                             kpn(a["L1_ffn_W1"][e] if isinstance(e, int) else
                                 a["L1_ffn_W1"][bass.ds(e, 1)].rearrange("a k n -> (a k) n")))\
                    .then_inc(S(f"l1_weights{s}"), 16)
                sp.dma_start(slot(s)[:, CHUNK // 2:].rearrange("p (k n) -> p k n", k=F1 // 128),
                             kpn(a["L1_ffn_W2"][e] if isinstance(e, int) else
                                 a["L1_ffn_W2"][bass.ds(e, 1)].rearrange("a k n -> (a k) n")))\
                    .then_inc(S(f"l1_weights{s}"), 16)

            if stages >= 4:
                for s in range(RING):
                    e = (RING + s) // 2
                    if s % 2:
                        sp.wait_ge(*reached("l0_y", e + 1))
                    else:
                        sp.wait_ge(*reached("l0_hidden", (e + 1) * (F0 // 256)))
                    load_l1(s, s)
            if stages >= 3:
                sp.wait_ge(*reached("row_added", 1))
                sp.dma_start(b_out[:], a["L1_gnn_b_out"].partition_broadcast(P)).then_inc(S("b_out_loaded"), 16)
            if stages >= 6:
                sp.wait_ge(*reached("l0f_bias", NT))
                sp.dma_start(brow[:], a["L2_ffn_bo"]).then_inc(S("l2f_brow_loaded"), 16)
            if stages >= 2:
                sp.wait_ge(*reached("ysb_ready", 1))
                sp.dma_start(ybuf_d.rearrange("(e c) d -> c e d", e=E0), ysb).then_inc(S("ybuf_stored"), 16)
            if stages >= 4:
                sp.wait_ge(*reached("tokens_sent1", 32 * NT))
                sp.dma_start(xs, xs_d.rearrange("(t p) d -> p t d", p=P)).then_inc(S("xs_loaded"), 16)
                sp.wait_ge(*reached("flag2_ready", 1))
                full = sp.value_load(flag2_i[0:1, 0:1], min_val=0, max_val=1)
                with sp.If(full == 1):
                    for s in range(RING):
                        sp.wait_ge(*reached(f"l1_weights{s}", 32))
                    with sp.Fori(0, E1) as e:
                        sp.wait_ge(*reached("any_expert_used", e + 1))
                        w1 = a["L1_ffn_W1"][bass.ds(e, 1)].rearrange("a k n -> (a k) n")
                        w2 = a["L1_ffn_W2"][bass.ds(e, 1)].rearrange("a k n -> (a k) n")
                        sp.dma_start(slot(0)[:, 0:CHUNK // 2].rearrange("p (k n) -> p k n", k=KD), kpn(w1))\
                            .then_inc(S("any_expert_loaded"), 16)
                        sp.dma_start(slot(0)[:, CHUNK // 2:].rearrange("p (k n) -> p k n", k=F1 // 128), kpn(w2))\
                            .then_inc(S("any_expert_loaded"), 16)
                with sp.Else():
                    with sp.Fori(1, E1 // RING) as r:
                        for s in range(RING):
                            sp.wait_ge(*reached("l1_used", (r - 1) * RING + s + 3))
                            load_l1(r * RING + s, s)
                sp.nop()
                sp.wait_ge(*reached("ys_ready", 1))
                sp.dma_start(ys_d.rearrange("(t p) d -> p t d", p=P), xs).then_inc(S("ys_stored"), 16)
            if stages >= 5:
                sp.wait_ge(*reached("l1_tokens_back", 32 * NT))
                sp.dma_start(l2_bias, a["L2_gnn_bias"].partition_broadcast(P)).then_inc(S("l2_rows_loaded"), 16)
                sp.dma_start(l2_gamma, a["L2_gnn_gamma"].partition_broadcast(P)).then_inc(S("l2_rows_loaded"), 16)
                sp.dma_start(l2_beta, a["L2_gnn_beta"].partition_broadcast(P)).then_inc(S("l2_rows_loaded"), 16)

            def load_dense(tag, e, i):
                names, slots = DENSE[tag]
                for n, name in enumerate(names):
                    w = a[name][e] if isinstance(e, int) else a[name][bass.ds(e, 1)].rearrange("a k n -> (a k) n")
                    sp.dma_start(slot(slots[i])[:, n * KD * D:(n + 1) * KD * D].rearrange("p (k n) -> p k n", k=KD), kpn(w))\
                        .then_inc(S(f"{tag}_weights{i}"), 16)

            sp.wait_ge(*reached("l1_experts_done", 1))
            for tag in ("l2f", "l3f"):
                for i in range(4):
                    load_dense(tag, i, i)
            for tag in ("l2f", "l3f"):
                if tag == "l3f":
                    sp.wait_ge(*reached("l2f_bias", NT))
                    sp.dma_start(brow[:], a["L3_ffn_b2"]).then_inc(S("l3f_brow_loaded"), 16)
                for i in range(4):
                    sp.wait_ge(*reached(tag + "_y", (i + 1) * NT))
                    load_dense(tag, 4 + i, i)

            sp.wait_ge(*reached("x_final", 1))
            sp.dma_start(out.rearrange(tokens_by_tile, p=P), x[:]).then_inc(S("out_stored"), 16)
            sp.wait_ge(*reached("out_stored", 16))

        @block.gpsimd
        def _(pool):
            st = Steps(S("pool_steps"))
            nc.gpsimd.iota(iota_i[:], [[1, NPAD]], base=0, channel_multiplier=0).then_inc(S("iota_ready"), 1)
            st.done(nc.gpsimd.memset(ident[:], 0.0))
            st.done(nc.gpsimd.memset(sel[:], 0.0))
            st.done(nc.gpsimd.memset(tri_f, 1.0))
            st.done(nc.gpsimd.memset(strict, 1.0))
            st.done(nc.gpsimd.memset(ones_f, 1.0))
            st.done(nc.gpsimd.memset(half_neg, -0.5))
            st.done(nc.gpsimd.memset(ones_bf, 1.0))
            st.wait(pool)

            def diag(t, base, n, step=1, op=ALU.not_equal, fill=1.0, cm=1):
                st.done(nc.gpsimd.affine_select(out=t, in_=t, compare_op=op, fill=fill, base=base,
                                                pattern=[[step, n]], channel_multiplier=cm))

            diag(ident[:], 0, 128, -1)
            diag(sel[:, 0:WB], 0, WB, -1)
            for k in range(1, 4):
                diag(sel[:, WB:], -k * WB, WB, -1)
                st.wait(pool)
            diag(tri_f, 0, P, 1, ALU.is_ge, 0.0, -1)
            diag(strict, -1, E1, 1, ALU.is_ge, 0.0, -1)
            st.wait(pool)
            nc.gpsimd.iota(tok_i, [[P, NT]], base=0, channel_multiplier=1).then_inc(S("consts_ready"), 1)

            def power(tag):
                pool.wait_ge(*reached(tag + "_var", 1))
                nc.gpsimd.tensor_tensor(rstd, vare, half_neg[0:P, 0:NT], ALU.pow).then_inc(S(tag + "_rstd"), 1)

            power("l0g")

            def kinds(s, n):
                d = ohd[s][:, 0:n]
                return nc.gpsimd.tensor_tensor(
                    d[:, :, 1:4, :], d[:, :, 0:1, :].to_broadcast([P, n, 3, WB]),
                    ebt[s][:, 0:n, 2:5].unsqueeze(3).to_broadcast([P, n, 3, WB]), ALU.mult)

            with pool.Fori(0, NBLK // 2) as i:
                for q in range(2):
                    pool.wait_ge(*reached("ohd_ready", 2 * i + q + 1))
                    kinds(q, CH).then_inc(S("kinds_ready"), 1)
            pool.wait_ge(*reached("flag_ready", 1))
            missed = pool.value_load(flag_i[0:1, 0:1], min_val=0, max_val=1)
            with pool.If(missed == 1):
                with pool.Fori(0, NBLK) as b:
                    with pool.Fori(0, NCHUNK) as c:
                        pool.wait_ge(*reached("all_ohd", b * NCHUNK + c + 1))
                        kinds(0, CHA).then_inc(S("all_kinds"), 1)
            with pool.Else():
                pool.nop()
            pool.nop()

            pool.wait_ge(*reached("bn_var_ready", 1))
            hn = half_neg[:, 0:KD * E2].rearrange("p (f e) -> p f e", e=E2)
            nc.gpsimd.tensor_tensor(bnT[:, 4], bnT[:, 4], hn, ALU.pow)
            nc.gpsimd.tensor_tensor(bnT[:, 9], bnT[:, 9], hn, ALU.pow).then_inc(S("bn_pow_ready"), 1)
            if stages >= 2:
                power("l0f")
                pool.wait_ge(*reached("slots0_ready", 1))
                pool.wait_ge(*reached("buf_zeroed", 16 * E0))
                for j in range(NT):
                    nc.gpsimd.indirect_dma_start(
                        buf_d, bass.IndirectOffsetOnAxis(ap=sloti[:, j, 0:1], axis=0), xln[:, j, :], None)\
                        .then_inc(S("tokens_sent0"), 16)
                pool.wait_ge(*reached("ybuf_stored", 16))
                for j in range(NT):
                    nc.gpsimd.indirect_dma_start(
                        yg0[:, j, :], None, ybuf_d, bass.IndirectOffsetOnAxis(ap=sloti[:, j, 1:2], axis=0))\
                        .then_inc(S("l0_tokens_back"), 16)
            if stages >= 3:
                pool.wait_ge(*reached("deg_ready", 1))
                nc.gpsimd.tensor_tensor(nsrc, outdeg, half_neg[0:P, 0:NT], ALU.pow).then_inc(S("nsrc_ready"), 1)
                power("l1g")
                pool.wait_ge(*reached("indeg_ready", 1))
                nc.gpsimd.tensor_tensor(rden, vare, half_neg[0:P, 0:NT], ALU.pow).then_inc(S("ndst_ready"), 1)
            if stages >= 4:
                power("l1f")
                pool.wait_ge(*reached("slots1_ready", 1))
                for k in range(2):
                    for j in range(NT):
                        nc.gpsimd.indirect_dma_start(
                            xs_d, bass.IndirectOffsetOnAxis(ap=sloti[:, j, k:k + 1], axis=0), xln[:, j, :], None)\
                            .then_inc(S("tokens_sent1"), 16)
                pool.wait_ge(*reached("ys_stored", 16))
                for k in range(2):
                    for j in range(NT):
                        nc.gpsimd.indirect_dma_start(
                            yg1[:, k * NT + j, :], None, ys_d,
                            bass.IndirectOffsetOnAxis(ap=sloti[:, j, k:k + 1], axis=0))\
                            .then_inc(S("l1_tokens_back"), 16)
            if stages >= 5:
                power("l2g")
                power("l2n")
            if stages >= 6:
                power("l2f")
            if stages >= 7:
                power("l3g")
            if stages >= 8:
                power("l3f")

        @block.scalar
        def _(act):
            small_loads = [0]

            def load(dst, src, **kw):
                act.dma_start(dst, src, **kw).then_inc(S("params_loaded" if small_loads[0] >= 9 else "proj_loaded"), 16)
                small_loads[0] += 1

            load(w_l0a[:, :, 0:D], kpn(a["L0_gnn_W1"]))
            load(w_l0b[:, :, 0:D], kpn(a["L0_gnn_W2"]))
            load(w_l2[:, :, 0:D], kpn(a["L2_gnn_W"]))
            for i, name in enumerate(["L0_gnn_att_src1", "L0_gnn_att_dst1", "L0_gnn_att_src2", "L0_gnn_att_dst2",
                                      "L2_gnn_att_src", "L2_gnn_att_dst"]):
                load(attv[i], a[name].rearrange("h c -> (h c)").partition_broadcast(128))
            load(b1_l0a[:], a["L0_gnn_b1"].rearrange("(k p) -> p k", p=128), allow_slow_non_contiguous=True)
            load(b1r0, a["L0_ffn_b1"])
            load(b1r1, a["L1_ffn_b1"])
            load(b2r1, a["L1_ffn_b2"])
            for i, name in enumerate(["b1", "g1", "be1", "m1", "v1", "b2", "g2", "be2", "m2", "v2"]):
                load(bnp[i], a["L2_ffn_" + name])
            load(b1r3, a["L3_ffn_b1"])
            load(rw3, a["L3_ffn_router_w"])
            load(w_gcn[:], kpn(a["L1_gnn_W_gcn"]))
            load(w_out[:], a["L1_gnn_W_out"])
            load(gate0[:], kpn(a["L0_ffn_gate_w"]))
            load(gate1[:], kpn(a["L1_ffn_Wr"]))
            load(gate2[:], kpn(a["L2_ffn_Wr"]))
            load(rbias[:, 0:E0], a["L0_ffn_gate_b"].rearrange("(a n) -> a n", a=1))
            load(rbias[:, E0:E0 + E1], a["L1_ffn_br"].rearrange("(a n) -> a n", a=1))
            load(rbias[:, E0 + E1:], a["L2_ffn_br"].rearrange("(a n) -> a n", a=1))
            load(b_gcn[:], a["L1_gnn_b_gcn"].rearrange("(p a) -> p a", a=1))
            load(b2_l0b[:], a["L0_gnn_b2"].partition_broadcast(P))
            load(brow[:], a["L0_ffn_b2"])
            assert small_loads[0] == PARAMS + 9

            act.nop().then_inc(S("acc_free"), 2)
            act.nop().then_inc(S("counts_free"), 2)

            def evac_acc(s):
                return nc.scalar.activation(cols(accs[s]), (psA, psB)[s][:, 0:NT, 0:P], ACT.Copy)

            def turned(tag, bias=None):
                act.wait_ge(*reached(tag + "_turned0", 1))
                if bias is None:
                    nc.scalar.activation(cols(xT[:, 0, :]), psA[:, 0:NT, 0:P], ACT.Copy).then_inc(S(tag + "_xT0"), 1)
                else:
                    nc.scalar.activation(cols(xT[:, 0, :]), psA[:, 0:NT, 0:P], ACT.Relu, bias=bias[:, 0:1])\
                        .then_inc(S(tag + "_xT0"), 1)
                    act.wait_ge(*reached(tag + "_turned1", 1))
                    nc.scalar.activation(cols(xT[:, 1, :]), psB[:, 0:NT, 0:P], ACT.Relu, bias=bias[:, 1:2])\
                        .then_inc(S(tag + "_xT1"), 1)

            def projected(tag, heads):
                ch = D // heads
                act.wait_ge(*reached(tag + "_ones", 1))
                for j in range(NT):
                    act.wait_ge(*reached(tag + "_proj", j + 1))
                    nc.scalar.activation(al[:, j, 0:2 * heads], (psC, psD)[j % 2][0:P, D:D + 2 * heads], ACT.Copy)\
                        .then_inc(S(tag + "_al"), 1)
                    nc.scalar.activation(hs[:, j, 0:heads * (ch + 1)].rearrange("p (h c) -> p h c", h=heads)[:, :, 0:ch],
                                         (psC, psD)[j % 2][0:P, 0:D].rearrange("p (h c) -> p h c", h=heads),
                                         ACT.Copy).then_inc(S(tag + "_hs"), 1)

            turned("l0g")
            projected("l0a", 4)

            def counts_out(i, q, before):
                b = 2 * i + q - 1
                act.wait_ge(*reached("block_ready", b + 1))
                ps = (psC, psD)[(q + 1) % 2][0:P, 0:NT * 2 * WB].rearrange("p (j c) -> p j c", c=2 * WB)
                nc.scalar.activation(ct[:, :, bass.ds(b * WB, WB)], ps[:, :, 0:WB], ACT.Copy)
                nc.scalar.activation(at[:, :, bass.ds(b * WB, WB)], ps[:, :, 0:WB], ACT.Copy,
                                     accum_out=cnt[:, bass.ds(b, 1)])
                nc.scalar.activation(wt[:, :, bass.ds(b * WB, WB)], ps[:, :, WB:], ACT.Copy)\
                    .then_inc(S("counts_free"), 1)

            def acc_out(n, q):
                act.wait_ge(*reached("acc_ready", n + 1))
                evac_acc(q).then_inc(S("acc_free"), 1)

            acc_out(0, 0)
            acc_out(1, 1)
            counts_out(0, 1, 0)
            with act.Fori(1, NBLK // 2) as i:
                for q in range(2):
                    acc_out(2 * i + q, q)
                    counts_out(i, q, None)
            counts_out(NBLK // 2, 0, None)
            act.wait_ge(*reached("params_acc", 1))
            nc.scalar.activation(b1T0[:], psA[:, 0, 0:64].rearrange("p (f e) -> p f e", e=E0), ACT.Copy)
            nc.scalar.activation(b1T1[:], psC[:, 0:256].rearrange("p (f e) -> p f e", e=E1), ACT.Copy)
            nc.scalar.activation(b2T1[:], psD[:, 0:128].rearrange("p (f e) -> p f e", e=E1), ACT.Copy)
            nc.scalar.activation(b1T3[:], psF[:, 16:32].rearrange("p (f e) -> p f e", e=E2), ACT.Copy)
            nc.scalar.activation(gate3[:], psF[:, 0:16].rearrange("p (f e) -> p f e", e=E2), ACT.Copy)
            nc.scalar.activation(bnT[:].rearrange("p w f e -> p (w f e)"),
                                 psB[:].rearrange("p a b -> p (a b)")[:, 0:10 * KD * E2], ACT.Copy)\
                .then_inc(S("params_turned"), 1)

            act.wait_ge(*reached("flag_ready", 1))
            missed = act.value_load(flag_i[0:1, 0:1], min_val=0, max_val=1)
            with act.If(missed == 1):
                with act.Fori(0, NBLK) as b:
                    with act.Fori(0, NCHUNK) as c:
                        act.wait_ge(*reached("all_acc", b * NCHUNK + c + 1))
                        evac_acc(0).then_inc(S("all_acc_out"), 1)
            with act.Else():
                act.nop()
            act.nop()

            def attention(tag, heads):
                act.wait_ge(*reached(tag + "_rows", 1))
                for h in range(heads):
                    act.wait_ge(*reached(tag + "_r1", h + 1))
                    for i in range(NT):
                        if h >= 2:
                            act.wait_ge(*reached(tag + "_agg", (h - 2) * NT + i + 1))
                        nc.scalar.activation(cols(u[h % 2][:, i, :]), psA[0:P, 0:NT, 0:P], ACT.Exp,
                                             bias=al[:, i, h:h + 1]).then_inc(S(tag + "_u"), 1)
                    act.wait_ge(*reached(tag + "_r2", h + 1))
                    for i in range(NT):
                        if h >= 1:
                            act.wait_ge(*reached(tag + "_max", (h - 1) * NT + i + 1))
                        nc.scalar.activation(cols(v[:, i, :]), psB[0:P, 0:NT, 0:P], ACT.Exp,
                                             bias=al2[:, i, h:h + 1]).then_inc(S(tag + "_v"), 1)

            attention("l0a", 4)
            turned("l0m", b1_l0a)
            projected("l0b", 1)
            attention("l0b", 1)
            if stages >= 2:
                turned("l0f")
                act.wait_ge(*reached("shift0_ready", 1))
                nc.scalar.activation(ex8, lg8, ACT.Exp).then_inc(S("exp0_ready"), 1)
                act.wait_ge(*reached("bufs_turned0", 1))
                nc.scalar.activation(bufT[:, 0, :].rearrange("p (e c) -> p e c", e=E0), psA[:, :, 0:CAP], ACT.Copy)\
                    .then_inc(S("bufT0"), 1)
                with act.Fori(0, E0 // 4) as r:
                    for q in range(4):
                        for f in range(F0 // 128):
                            act.wait_ge(*reached("l0_hidden", (4 * r + q) * (F0 // 256) + f // 2 + 1))
                            nc.scalar.activation(h0[:, f, :], hidden0(f), ACT.Relu,
                                                 bias=b1T0[:, f, bass.ds(4 * r + q, 1)]).then_inc(S("l0_relu"), 1)
            if stages >= 3:
                turned("l1g")
                for j in range(NT):
                    act.wait_ge(*reached("gcn_proj", j + 1))
                    if j == 0:
                        act.wait_ge(*reached("nsrc_ready", 1))
                    nc.scalar.activation(hs[:, j, 0:64], (psC, psD)[j % 2][0:P, 0:64], ACT.Copy,
                                         scale=nsrc[:, j:j + 1]).then_inc(S("gcn_hs"), 1)
                act.wait_ge(*reached("gcn_turned", 1))
                nc.scalar.activation(cols(hT), psA[0:64, 0:NT, 0:P], ACT.Relu, bias=b_gcn[:, 0:1])\
                    .then_inc(S("gcn_hT"), 1)
            if stages >= 4:
                turned("l1f")
                act.wait_ge(*reached("shift1_ready", 1))
                nc.scalar.activation(gsel[:, :, 1], gsel[:, :, 0], ACT.Exp).then_inc(S("exp1_ready"), 1)
                for g in range(2):
                    act.wait_ge(*reached("xs_turned", 2 * g + 1))
                    nc.scalar.activation(xsT[:, 0, g * N:(g + 1) * N].rearrange("p (j q) -> p j q", q=P),
                                         psA[:, 0:NT, 0:P], ACT.Copy).then_inc(S("xsT_act"), 1)
                act.wait_ge(*reached("flag2_ready", 1))
                full = act.value_load(flag2_i[0:1, 0:1], min_val=0, max_val=1)

                def hidden1(f, e, q):
                    return nc.scalar.activation(h1[q][:, f, :], hidden1_ps(f), ACT.Relu,
                                                bias=b1T1[:, f, bass.ds(e, 1)])

                nf = F1 // 128
                with act.If(full == 1):
                    with act.Fori(0, E1) as e:
                        with act.Fori(0, ROUNDS) as r:
                            for f in range(nf):
                                act.wait_ge(*reached("any_hidden", (e * ROUNDS + r) * nf + f + 1))
                                hidden1(f, e, 0).then_inc(S("any_relu"), 1)
                with act.Else():
                    with act.Fori(0, E1 // RING) as r:
                        for q in range(RING):
                            for f in range(nf):
                                act.wait_ge(*reached("l1_hidden", (RING * r + q) * nf + f + 1))
                                if f == 0:
                                    act.wait_ge(*reached("l1_used", RING * r + q + 1))
                                hidden1(f, RING * r + q, q % 2).then_inc(S("l1_relu"), 1)
                act.nop()
                for g in (0, 2, 4):
                    act.wait_ge(*reached("ys_turned", g + 1))
                    nc.scalar.activation(xs[:, 2 * g:2 * g + 2, :].rearrange("p t (m d) -> p (t m) d", m=2),
                                         psA[0:P, 0:4, 0:128], ACT.Copy).then_inc(S("ys_act"), 1)
            if stages >= 5:
                turned("l2g")
                projected("l2a", 4)
                attention("l2a", 4)

            def dense(tag, func, gated):
                turned(tag)
                act.wait_ge(*reached(tag + "_shift", 1))
                act.wait_ge(*reached("bn_ready", 1))
                nc.scalar.activation(ex8, lg8, ACT.Exp).then_inc(S(tag + "_exp"), 1)
                layers = 2 if tag == "l2f" else 1
                act.nop().then_inc(S(tag + "_act"), 2)
                with act.Fori(0, 2) as r:
                    for t in range(2):
                        for layer in range(layers):
                            for q in range(2):
                                e = 4 * r + 2 * t + q
                                for m in range(KD):
                                    n = (((2 * r + t) * layers + layer) * 2 + q) * KD + m
                                    act.wait_ge(*reached(tag + "_hidden", n + 1))
                                    o = cols((h1d, h2d)[layer][q][:, m, :])
                                    i_ = (psA, psB)[m][:, 0:NT, 0:P]
                                    if tag == "l2f":
                                        ins = nc.scalar.activation(o, i_, func, bias=bnT[:, 5 * layer + 2, m, bass.ds(e, 1)],
                                                                   scale=bnT[:, 5 * layer + 1, m, bass.ds(e, 1)])
                                    else:
                                        ins = nc.scalar.activation(o, i_, func, bias=b1T3[:, m, bass.ds(e, 1)])
                                    ins.then_inc(S(tag + "_act"), 1)

            if stages >= 6:
                dense("l2f", ACT.Relu, True)
            if stages >= 7:
                turned("l3g")
                for j in range(NT):
                    act.wait_ge(*reached("l3_proj", j + 1))
                    nc.scalar.activation(hs[:, j, 0:D], (psC, psD)[j % 2][0:P, 0:D], ACT.Copy)\
                        .then_inc(S("l3_hs"), 1)
            if stages >= 8:
                dense("l3f", ACT.Gelu, False)

        @block.tensor
        def _(pe):
            pe.wait_ge(*reached("consts_ready", 1))
            pe.wait_ge(*reached("cnt_ready", NBLK - 1))
            nc.tensor.matmul(psE[0:1, 0:NBLK], ones_f[0:P, 0:1], cnt, start=True, stop=True).then_inc(S("base_sum"), 1)
            def turn(tag, src_sem, src):
                pe.wait_ge(*reached(src_sem, 1))
                for k in range(KD):
                    for j in range(NT):
                        ins = nc.tensor.transpose((psA, psB)[k][:, j, 0:P], src[:, j, k * 128:(k + 1) * 128],
                                                  ident[0:P, 0:P])
                    ins.then_inc(S(f"{tag}_turned{k}"), 1)

            turn("l0g", "l0g_xln", xln)
            def project(tag, xtag, w, width, sem_out, sem_in, wait_first=None):
                pe.wait_ge(*reached(xtag + "_xT0", 1))
                pe.wait_ge(*reached(xtag + "_xT1", 1))
                for j in range(NT):
                    if j >= 2:
                        for s_ in sem_in:
                            pe.wait_ge(*reached(s_, j - 1))
                    for k in range(KD):
                        ins = nc.tensor.matmul((psC, psD)[j % 2][0:P, 0:width], xT[:, k, j * P:(j + 1) * P], w[:, k, 0:width],
                                               start=(k == 0), stop=(k == KD - 1))
                    ins.then_inc(S(sem_out), 1)

            pe.wait_ge(*reached("l0a_folded", 1))
            project("l0a", "l0g", w_l0a, D + 8, "l0a_proj", ["l0a_hs", "l0a_al"])

            def accumulate(s, n):
                acc = (psA, psB)[s]
                for t in range(n):
                    w = ohd[s][:, t].rearrange("p k d -> p (k d)")
                    nc.tensor.matmul(acc[:, 0:4, 0:P], w, cols(ohs[s][:, t, 0:4 * P]), start=(t == 0), stop=(t == n - 1))
                    ins = nc.tensor.matmul(acc[:, 4, 0:P], w, ohs[s][:, t, 4 * P:N], start=(t == 0), stop=(t == n - 1))
                return ins

            def split(s, ps):
                for j in range(NT):
                    ins = nc.tensor.matmul(ps[0:P, j * 2 * WB:(j + 1) * 2 * WB], accs[s][:, j * P:(j + 1) * P], sel[:],
                                           start=True, stop=True)
                return ins

            def gather_block(b, q):
                pe.wait_ge(*reached("kinds_ready", b + 1))
                pe.wait_ge(*reached("ohs_ready", b + 1))
                pe.wait_ge(*reached("acc_free", b + 1))
                accumulate(q, CH).then_inc(S("acc_ready"), 1)

            def split_block(b, q):
                pe.wait_ge(*reached("acc_free", b + 3))
                pe.wait_ge(*reached("counts_free", b + 1))
                split(q, (psC, psD)[q]).then_inc(S("block_ready"), 1)

            pe.wait_ge(*reached("l0a_al", NT))
            pe.wait_ge(*reached("l0a_hs", NT))
            gather_block(0, 0)
            gather_block(1, 1)
            split_block(0, 0)
            with pe.Fori(1, NBLK // 2) as i:
                gather_block(2 * i, 0)
                split_block(2 * i - 1, 1)
                gather_block(2 * i + 1, 1)
                split_block(2 * i, 0)
            split_block(NBLK - 1, 1)

            pe.wait_ge(*reached("counts_free", NBLK + 2))
            nc.tensor.matmul(psE[0:1, 0:NBLK], ones_f[0:P, 0:1], cnt, start=True, stop=True).then_inc(S("total_sum"), 1)
            pe.wait_ge(*reached("params_loaded", 16 * PARAMS))
            pe.wait_ge(*reached("acc_free", NBLK + 2))
            pe.wait_ge(*reached("counts_free", NBLK + 2))
            for f in range(F0 // 128):
                nc.tensor.transpose(psA[:, 0, f * E0:(f + 1) * E0], b1r0[:, f * 128:(f + 1) * 128], ident[0:E0, 0:E0])
            for f in range(F1 // 128):
                nc.tensor.transpose(psC[:, f * E1:(f + 1) * E1], b1r1[:, f * 128:(f + 1) * 128], ident[0:E1, 0:E1])
            for k in range(KD):
                nc.tensor.transpose(psD[:, k * E1:(k + 1) * E1], b2r1[:, k * 128:(k + 1) * 128], ident[0:E1, 0:E1])
                nc.tensor.transpose(psF[:, (KD + k) * E2:(KD + k + 1) * E2], b1r3[:, k * 128:(k + 1) * 128], ident[0:E2, 0:E2])
                nc.tensor.transpose(psF[:, k * E2:(k + 1) * E2], rw3[:, k * 128:(k + 1) * 128], ident[0:E2, 0:E2])
            for n, t in enumerate(bnp):
                for k in range(KD):
                    c = (n * KD + k) * E2
                    ins = nc.tensor.transpose(psB[:].rearrange("p a b -> p (a b)")[:, c:c + E2], t[:, k * 128:(k + 1) * 128], ident[0:E2, 0:E2])
            ins.then_inc(S("params_acc"), 1)
            pe.wait_ge(*reached("flag_ready", 1))
            pe.wait_ge(*reached("params_turned", 1))
            missed = pe.value_load(flag_i[0:1, 0:1], min_val=0, max_val=1)
            with pe.If(missed == 1):
                with pe.Fori(0, NBLK) as b:
                    with pe.Fori(0, NCHUNK) as c:
                        n = b * NCHUNK + c
                        pe.wait_ge(*reached("all_kinds", n + 1))
                        pe.wait_ge(*reached("all_ohs", n + 1))
                        accumulate(0, CHA).then_inc(S("all_acc"), 1)
                        pe.wait_ge(*reached("all_acc_out", n + 1))
                        split(0, psC).then_inc(S("all_split"), 1)
            with pe.Else():
                pe.nop()
            pe.nop()

            def row(ps, col):
                for j in range(NT):
                    ins = nc.tensor.transpose(ps[0:P, j, 0:P], col(j).to_broadcast([P, P]), ident[0:P, 0:P])
                return ins

            def attention(tag, heads):
                pe.wait_ge(*reached(tag + "_al", NT))
                for h in range(heads):
                    if h >= 2:
                        pe.wait_ge(*reached(tag + "_masked", (h - 1) * NT))
                    row((psA, psB)[h % 2], lambda j: al[:, j, h:h + 1]).then_inc(S(tag + "_bc"), 1)
                pe.wait_ge(*reached(tag + "_rows", 1))

                def rows(h):
                    if h >= 1:
                        pe.wait_ge(*reached(tag + "_u", h * NT))
                    row(psA, lambda j: r1[:, j, h:h + 1]).then_inc(S(tag + "_r1"), 1)
                    if h >= 1:
                        pe.wait_ge(*reached(tag + "_v", h * NT))
                    row(psB, lambda j: r2[:, j, h:h + 1]).then_inc(S(tag + "_r2"), 1)

                pe.wait_ge(*reached(tag + "_hs", NT))
                rows(0)
                if heads == 1:
                    for i in range(NT):
                        pe.wait_ge(*reached(tag + "_p", i + 1))
                        for j in range(NT - 1):
                            ins = nc.tensor.matmul((psC, psD, psE, psF)[j][0:P, 0:D + 1], u[0][:, i, j * P:(j + 1) * P],
                                                   hs[:, i, 0:D + 1], start=(i == 0), stop=(i == NT - 1))
                        ins.then_inc(S(tag + "_agg"), 1)
                    for i in range(NT):
                        ins = nc.tensor.matmul(last_out, u[0][:, i, (NT - 1) * P:], hs[:, i, 0:D + 1],
                                               start=(i == 0), stop=(i == NT - 1))
                    ins.then_inc(S(tag + "_agg"), 1)
                    return
                for h in range(heads):
                    if h + 1 < heads:
                        rows(h + 1)
                    if h >= 2:
                        pe.wait_ge(*reached(tag + "_out", h - 1))
                    for i in range(NT):
                        pe.wait_ge(*reached(tag + "_p", h * NT + i + 1))
                        for j in range(NT):
                            ins = nc.tensor.matmul((psC, psD)[h % 2][0:P, j * 65:(j + 1) * 65],
                                                   u[h % 2][:, i, j * P:(j + 1) * P], hs[:, i, h * 65:(h + 1) * 65],
                                                   start=(i == 0 and j == 0), stop=(i == NT - 1 and j == NT - 1))
                        ins.then_inc(S(tag + "_agg"), 1)

            pe.wait_ge(*reached("at_ready", 1))
            for j in range(NT):
                if j >= 2:
                    pe.wait_ge(*reached("negm_done", j - 1))
                for i in range(NT):
                    ins = nc.tensor.transpose((psA, psB)[j % 2][0:P, i, 0:P], at[:, i, j * P:(j + 1) * P], ident[0:P, 0:P])
                ins.then_inc(S("at_turned"), 1)
            pe.wait_ge(*reached("negm_done", NT))

            attention("l0a", 4)
            turn("l0m", "l0a_done", gat)
            pe.wait_ge(*reached("l0b_folded", 1))
            project("l0b", "l0m", w_l0b, D + 2, "l0b_proj", ["l0b_hs", "l0b_al"])
            attention("l0b", 1)

            def logits(tag, gate, ne, rb):
                pe.wait_ge(*reached(tag + "_xT0", 1))
                pe.wait_ge(*reached(tag + "_xT1", 1))
                for j in range(NT):
                    o = psC[0:P, j * ne:(j + 1) * ne]
                    for k in range(KD):
                        ins = nc.tensor.matmul(o, xT[:, k, j * P:(j + 1) * P], gate[:, k, :], start=(k == 0),
                                               stop=(k == KD - 1 and rb is None))
                    if rb is not None:
                        ins = nc.tensor.matmul(o, ones_f[0:1, 0:P], rbias[:, rb:rb + ne], start=False, stop=True)
                ins.then_inc(S(tag + "_logits"), 1)

            def ranks(tag, ohb, ne):
                pe.wait_ge(*reached(tag + "_onehot", 1))
                for j in range(NT):
                    o = psD[0:P, j * ne:(j + 1) * ne]
                    for i in range(j + 1):
                        ins = nc.tensor.matmul(o, tri_b if i == j else ones_bf, ohb[:, i, :], start=(i == 0), stop=(i == j))
                return ins

            def expert_bias(tag, wsem, wsrc, brow):
                pe.wait_ge(*reached(wsem, 1))
                if tag != "l0f":
                    pe.wait_ge(*reached(tag + "_brow_loaded", 16))
                for j in range(NT):
                    ins = nc.tensor.transpose(psA[0:8, j, 0:P], wsrc[:, j, :], ident[0:P, 0:P])
                ins.then_inc(S(tag + "_wturned"), 1)
                pe.wait_ge(*reached(tag + "_wT", 1))
                for j in range(NT):
                    if j >= 2:
                        pe.wait_ge(*reached(tag + "_bias_out", j - 1))
                    nc.tensor.matmul((psC, psD)[j % 2][0:P, 0:D], wgT[:, j * P:(j + 1) * P], brow[:], start=True, stop=True)\
                        .then_inc(S(tag + "_bias"), 1)

            if stages >= 2:
                turn("l0f", "l0f_xln", xln)
                logits("l0f", gate0, E0, 0)
                ranks("l0f", ohb0, E0).then_inc(S("l0_ranks"), 1)
                pe.wait_ge(*reached("slots0_ready", 1))
                expert_bias("l0f", "l0f_onehot", oh0, brow)
                pe.wait_ge(*reached("bufs_loaded", 16))
                for k in range(KD):
                    for e in range(E0):
                        ins = nc.tensor.transpose((psA, psB)[k][:, e, 0:CAP], bufs[:, e, k * 128:(k + 1) * 128],
                                                  ident[0:CAP, 0:CAP])
                    ins.then_inc(S(f"bufs_turned{k}"), 1)
                pe.wait_ge(*reached("bufT0", 1))
                pe.wait_ge(*reached("bufT1", 1))
                nf = F0 // 128
                with pe.Fori(0, 2) as r:
                    for q in range(4):
                        e = 4 * r + q
                        w1 = slot(2 * q).rearrange("p (k n) -> p k n", k=KD)
                        w2 = slot(2 * q + 1).rearrange("p (k n) -> p k n", k=nf)
                        pe.wait_ge(*reached(f"l0_weights{2 * q}", 16 * r + 16))
                        for f in range(nf):
                            for k in range(KD):
                                ins = nc.tensor.matmul(hidden0(f), w1[:, k, f * 128:(f + 1) * 128],
                                                       bufT[:, k, bass.ds(e * CAP, CAP)], start=(k == 0), stop=(k == KD - 1))
                            if f % 2:
                                ins.then_inc(S("l0_hidden"), 1)
                        pe.wait_ge(*reached(f"l0_weights{2 * q + 1}", 16 * r + 16))
                        pe.wait_ge(*reached("l0_y_free", e + 1))
                        y = (psC, psD)[q % 2][0:CAP, 0:D]
                        for f in range(nf):
                            pe.wait_ge(*reached("l0_relu", e * nf + f + 1))
                            ins = nc.tensor.matmul(y, h0[:, f, :], w2[:, f, :], start=(f == 0), stop=(f == nf - 1))
                        ins.then_inc(S("l0_y"), 1)
            if stages >= 3:
                turn("l1g", "l1g_xln", xln)
                project("gcn", "l1g", w_gcn, 64, "gcn_proj", ["gcn_hs"])
                pe.wait_ge(*reached("gcn_hs", NT))
                pe.wait_ge(*reached("gcn_ones", 1))
                for j in range(NT):
                    for i in range(NT):
                        ins = nc.tensor.matmul(psE[0:P, j * 65:(j + 1) * 65], ct[:, i, j * P:(j + 1) * P], hs[:, i, 0:65],
                                               start=(i == 0), stop=(i == NT - 1))
                ins.then_inc(S("gcn_agg"), 1)
                pe.wait_ge(*reached("gcn_scaled", 1))
                for j in range(NT):
                    ins = nc.tensor.transpose(psA[0:64, j, 0:P], agg[:, j, :], ident[0:P, 0:P])
                ins.then_inc(S("gcn_turned"), 1)
                pe.wait_ge(*reached("gcn_hT", 1))
                for j in range(NT):
                    if j >= 2:
                        pe.wait_ge(*reached("gcn_out", j - 1))
                    nc.tensor.matmul((psC, psD)[j % 2][0:P, 0:D], hT[:, j * P:(j + 1) * P], w_out[:], start=True, stop=True)\
                        .then_inc(S("gcn_y"), 1)
            if stages >= 4:
                turn("l1f", "l1f_xln", xln)
                logits("l1f", gate1, E1, E0)
                ranks("l1f", ohb1, E1)
                for i in range(NT):
                    ins = nc.tensor.matmul(psE[0:P, 0:E1], ones_bf, ohb1[:, i, :], start=(i == 0), stop=(i == NT - 1))
                for i in range(NT):
                    ins = nc.tensor.matmul(psF[0:E1, 0:1], ohb1[:, i, :], ones_bf[:, 0:1], start=(i == 0), stop=(i == NT - 1))
                ins.then_inc(S("l1_ranks"), 1)
                pe.wait_ge(*reached("cntcol_ready", 1))
                nc.tensor.matmul(psC[0:P, 0:E1], cntcol.to_broadcast([E1, P]), strict, start=True, stop=True)\
                    .then_inc(S("l1_offsets"), 1)
                pe.wait_ge(*reached("xs_loaded", 16))
                for g in range(4):
                    k, half = g % 2, g // 2
                    if half:
                        pe.wait_ge(*reached("xsT_act" if k == 0 else "xsT_dve", 1))
                    for j in range(NT):
                        ins = nc.tensor.transpose((psA, psB)[k][:, j, 0:P], xs[:, half * NT + j, k * 128:(k + 1) * 128],
                                                  ident[0:P, 0:P])
                    ins.then_inc(S("xs_turned"), 1)
                pe.wait_ge(*reached("xsT_act", 2))
                pe.wait_ge(*reached("xsT_dve", 2))
                pe.wait_ge(*reached("flag2_ready", 1))
                full = pe.value_load(flag2_i[0:1, 0:1], min_val=0, max_val=1)
                nf = F1 // 128

                def hidden1(s, f, start):
                    w1 = slot(s)[:, 0:CHUNK // 2].rearrange("p (k n) -> p k n", k=KD)
                    for k in range(KD):
                        ins = nc.tensor.matmul(hidden1_ps(f), w1[:, k, f * 128:(f + 1) * 128],
                                               xsT[:, k, bass.ds(start, WIN)], start=(k == 0), stop=(k == KD - 1))
                    return ins

                def out1(s, ps, h, wait):
                    w2 = slot(s)[:, CHUNK // 2:].rearrange("p (k n) -> p k n", k=nf)
                    for m in range(KD):
                        for f in range(nf):
                            if m == 0:
                                wait(f)
                            ins = nc.tensor.matmul(ps[:, m, 0:WIN], w2[:, f, m * 128:(m + 1) * 128], h[:, f, :],
                                                   start=(f == 0), stop=(f == nf - 1))
                    return ins

                with pe.If(full == 1):
                    with pe.Fori(0, E1) as e:
                        with pe.Fori(0, ROUNDS) as r:
                            n = e * ROUNDS + r
                            pe.wait_ge(*reached("any_expert_loaded", 32 * e + 32))
                            start = pe.value_load(starts[0:1, bass.ds(e, 1), bass.ds(r, 1)].rearrange("p a b -> p (a b)"),
                                                  min_val=0, max_val=SLOTS)
                            for f in range(nf):
                                hidden1(0, f, start).then_inc(S("any_hidden"), 1)
                            pe.wait_ge(*reached("any_y_free", n + 1))
                            out1(0, psA, h1[0], lambda f: pe.wait_ge(*reached("any_relu", n * nf + f + 1))).then_inc(S("any_y"), 1)
                with pe.Else():
                    def hidden_of(r, q):
                        e = r * RING + q
                        start = pe.value_load(starts[0:1, bass.ds(e, 1), 0:1].rearrange("p a b -> p (a b)"),
                                              min_val=0, max_val=SLOTS)
                        pe.wait_ge(*reached(f"l1_weights{q}", 32 * r + 32))
                        for f in range(nf):
                            pe.wait_ge(*reached("l1_relu", e * nf + f + 1))
                            hidden1(q, f, start).then_inc(S("l1_hidden"), 1)

                    def out_of(r, q):
                        e = r * RING + q
                        pe.wait_ge(*reached("l1_y_free", e + 1))
                        out1(q, (psA, psB)[q % 2], h1[q % 2],
                             lambda f: pe.wait_ge(*reached("l1_relu", (e + 1) * nf + f + 1))).then_inc(S("l1_used"), 1)

                    hidden_of(0, 0)
                    with pe.Fori(0, E1 // RING - 1) as r:
                        for q in range(RING):
                            hidden_of(*((r, q + 1) if q + 1 < RING else (r + 1, 0)))
                            out_of(r, q)
                    for q in range(RING):
                        if q + 1 < RING:
                            hidden_of(E1 // RING - 1, q + 1)
                        out_of(E1 // RING - 1, q)
                pe.nop()
                pe.wait_ge(*reached("yT_ready", 1))
                for g in range(5):
                    if g >= 2:
                        pe.wait_ge(*reached("ys_dve" if g % 2 else "ys_act", g // 2))
                    for t in range(2):
                        for m in range(KD):
                            c = (2 * g + t) * P
                            ins = nc.tensor.transpose((psA, psB)[g % 2][0:P, t * KD + m, :], yT[:, m, c:c + P], ident[:])
                    ins.then_inc(S("ys_turned"), 1)
            if stages >= 5:
                turn("l2g", "l2g_xln", xln)
                project("l2a", "l2g", w_l2, D + 8, "l2a_proj", ["l2a_hs", "l2a_al"])
                attention("l2a", 4)

            def dense(tag, gate, rb, layers):
                turn(tag, tag + "_xln", xln)
                logits(tag, gate, E2, rb)
                expert_bias(tag, tag + "_w", wgt, brow)
                slots = DENSE[tag][1]
                with pe.Fori(0, 2) as r:
                    for t in range(2):
                        p = 2 * r + t
                        for q in range(2):
                            pe.wait_ge(*reached(f"{tag}_weights{2 * t + q}", 16 * (layers + 1) * (r + 1)))
                        for layer in range(layers):
                            for q in range(2):
                                w = slot(slots[2 * t + q])[:, layer * KD * D:(layer + 1) * KD * D]\
                                    .rearrange("p (k n) -> p k n", k=KD)
                                src = xT if layer == 0 else h1d[q]
                                n = (p * layers + layer) * 2 + q
                                if layer:
                                    pe.wait_ge(*reached(tag + "_act", (p * layers * 2 + q + 1) * KD + 2))
                                for m in range(KD):
                                    ps = (psA, psB)[m]
                                    pe.wait_ge(*reached(tag + "_act", n * KD + m + 1))
                                    for k in range(KD):
                                        wk_ = w[:, k, m * 128:(m + 1) * 128]
                                        nc.tensor.matmul(ps[:, 0:4, 0:P], wk_, cols(src[:, k, 0:4 * P]),
                                                         start=(k == 0), stop=(k == KD - 1))
                                        ins = nc.tensor.matmul(ps[:, 4, 0:P], wk_, src[:, k, 4 * P:N],
                                                               start=(k == 0), stop=(k == KD - 1))
                                    ins.then_inc(S(tag + "_hidden"), 1)
                        for q in range(2):
                            hsrc = (h1d, h2d)[layers - 1][q]
                            w = slot(slots[2 * t + q])[:, layers * KD * D:(layers + 1) * KD * D]\
                                .rearrange("p (k n) -> p k n", k=KD)
                            pe.wait_ge(*reached(tag + "_act", ((p * layers + layers - 1) * 2 + q + 1) * KD + 2))
                            for j in range(NT):
                                pe.wait_ge(*reached(tag + "_y_free", (2 * p + q) * NT + j + 1))
                                for k in range(KD):
                                    ins = nc.tensor.matmul(((psC, psD)[(q * NT + j) % 2])[0:P, 0:D],
                                                           hsrc[:, k, j * P:(j + 1) * P], w[:, k, :],
                                                           start=(k == 0), stop=(k == KD - 1))
                                ins.then_inc(S(tag + "_y"), 1)

            if stages >= 6:
                dense("l2f", gate2, E0 + E1, 2)
            if stages >= 7:
                turn("l3g", "l3g_xln", xln)
                pe.wait_ge(*reached("w_l3_loaded", 16))
                project("l3", "l3g", w_l3, D, "l3_proj", ["l3_hs"])
                pe.wait_ge(*reached("l3_hs", NT))
                for j in range(NT):
                    if j >= 2:
                        pe.wait_ge(*reached("l3_out", j - 1))
                    for i in range(NT):
                        ins = nc.tensor.matmul((psC, psD)[j % 2][0:P, 0:D], wt[:, i, j * P:(j + 1) * P], hs[:, i, 0:D],
                                               start=(i == 0), stop=(i == NT - 1))
                    ins.then_inc(S("l3_agg"), 1)
            if stages >= 8:
                dense("l3f", gate3, None, 1)

        @block.vector
        def _(dve):
            V = nc.vector
            st = Steps(S("dve_steps"))

            def step(ins):
                st.done(ins)
                st.wait(dve)

            V.nop().then_inc(S("all_added"), 1)
            dve.wait_ge(*reached("dst_loaded", 16))
            V.memset(cnt, 0.0)
            step(V.tensor_copy(pack[:, :, 1], dst_i))
            for b in range(1, NBLK):
                ins = V.tensor_scalar(junk_e, pack[:, :, 1], float(b * WB), 0.0, ALU.is_lt, ALU.add, accum_out=cnt[:, b:b + 1])
                ins.then_inc(S("cnt_ready"), 1)
                dve.wait_ge(*reached("cnt_ready", b))
            dve.wait_ge(*reached("edges_loaded", 32))
            V.tensor_copy(pack[:, :, 0], src_i)
            step(V.tensor_copy(bf_part[:, 0:EPP], ew))
            step(V.tensor_copy(pack[:, :, 2], bf_part[:, 0:EPP]))
            step(V.tensor_tensor(res, ew, pack[:, :, 2], ALU.subtract))
            step(V.tensor_copy(bf_part[:, 0:EPP], res))
            step(V.tensor_copy(pack[:, :, 3], bf_part[:, 0:EPP]))
            V.tensor_tensor(pack[:, :, 4], res, pack[:, :, 3], ALU.subtract).then_inc(S("pack_ready"), 1)
            dve.wait_ge(*reached("base_sum", 1))
            step(V.tensor_scalar(basef, psE[0:1, 0:NBLK], float(E - CHE), None, ALU.min))
            V.tensor_copy(base_i, basef).then_inc(S("base_ready"), 1)
            dve.wait_ge(*reached("iota_ready", 1))
            step(V.tensor_copy(iota_f[:], iota_i[:]))
            V.tensor_copy(iota_h, iota_f[:])
            dve.wait_ge(*reached("consts_ready", 1))
            V.tensor_copy(tri_b, tri_f)
            step(V.tensor_copy(tokid, tok_i))
            def normalise(tag, src, dst, sem):
                for j in range(NT):
                    ins = V.bn_stats(st6[:, j, :], src[:, j, :])
                step(ins)
                for j in range(NT):
                    ins = V.bn_aggr(mv[:, j, :], st6[:, j, :])
                step(ins)
                V.tensor_scalar(vare, mv[:, :, 1], LN_EPS, None, ALU.add).then_inc(S(tag + "_var"), 1)
                dve.wait_ge(*reached(tag + "_rstd", 1))
                for j in range(NT):
                    ins = V.tensor_scalar(dst[:, j, :], src[:, j, :], mv[:, j, 0:1], rstd[:, j:j + 1],
                                          ALU.subtract, ALU.mult)
                ins.then_inc(S(sem), 1)

            def turned(tag):
                dve.wait_ge(*reached(tag + "_turned1", 1))
                V.tensor_copy(cols(xT[:, 1, :]), psB[:, 0:NT, 0:P]).then_inc(S(tag + "_xT1"), 1)

            dve.wait_ge(*reached("x_loaded", 16))
            normalise("l0g", x, xln, "l0g_xln")
            def ones(tag, heads):
                ch = D // heads
                V.memset(hs[:, :, 0:heads * (ch + 1)].rearrange("p j (h c) -> p j h c", h=heads)[:, :, :, ch:ch + 1], 1.0)\
                    .then_inc(S(tag + "_ones"), 1)


            def fold(w, heads, v0):
                for n in range(2):
                    step(V.tensor_tensor(attm, w[:, :, 0:D], attv[v0 + n].unsqueeze(1).to_broadcast([128, KD, D]), ALU.mult))
                    step(V.tensor_reduce(w[:, :, D + n * heads:D + (n + 1) * heads],
                                         attm.rearrange("p k (h c) -> p k h c", h=heads), AX, ALU.add))

            dve.wait_ge(*reached("proj_loaded", 16 * 9))
            fold(w_l0a, 4, 0)
            V.nop().then_inc(S("l0a_folded"), 1)
            ones("l0a", 4)
            turned("l0g")

            def onehots(s, b, n, sem_d, sem_s):
                e = ebt[s][:, 0:n]
                V.tensor_tensor(ohd[s][:, 0:n, 0, :], iota_f[0:P, bass.ds(b * WB, WB)].unsqueeze(1).to_broadcast([P, n, WB]),
                                e[:, :, 1:2].to_broadcast([P, n, WB]), ALU.is_equal).then_inc(S(sem_d), 1)
                for t in range(n):
                    ins = V.tensor_scalar(ohs[s][:, t, 0:N], iota_h[0:P, 0:N], e[:, t, 0:1], None, ALU.is_equal)
                ins.then_inc(S(sem_s), 1)

            def block_onehots(i, q, first):
                b = 2 * i + q
                dve.wait_ge(*reached(f"edge_run_loaded{q}", 16 * i + 16))
                if not first:
                    dve.wait_ge(*reached("acc_ready", b - 1))
                onehots(q, b, CH, "ohd_ready", "ohs_ready")

            block_onehots(0, 0, True)
            block_onehots(0, 1, True)
            with dve.Fori(1, NBLK // 2) as i:
                for q in range(2):
                    block_onehots(i, q, False)
            dve.wait_ge(*reached("total_sum", 1))
            step(V.tensor_reduce(flagf[:, 0:1], psE[0:1, 0:NBLK], AX, ALU.add))
            step(V.tensor_scalar(flagf[:, 1:2], flagf[:, 0:1], float(E), None, ALU.not_equal))
            V.tensor_copy(flag_i[:, 0:1], flagf[:, 1:2]).then_inc(S("flag_ready"), 1)
            dve.wait_ge(*reached("flag_ready", 1))
            missed = dve.value_load(flag_i[0:1, 0:1], min_val=0, max_val=1)
            with dve.If(missed == 1):
                V.memset(ct[:], 0.0)
                V.memset(wt[:], 0.0).then_inc(S("all_zeroed"), 1)
                dve.wait_ge(*reached("all_zeroed", 1))
                with dve.Fori(0, NBLK) as b:
                    with dve.Fori(0, NCHUNK) as c:
                        n = b * NCHUNK + c
                        dve.wait_ge(*reached("all_loaded", 16 * n + 16))
                        onehots(0, b, CHA, "all_ohd", "all_ohs")
                        dve.wait_ge(*reached("all_split", n + 1))
                        dve.wait_ge(*reached("all_added", n + 1))
                        ps = psC[0:P, 0:NT * 2 * WB].rearrange("p (j c) -> p j c", c=2 * WB)
                        cb, wb = ct[:, :, bass.ds(b * WB, WB)], wt[:, :, bass.ds(b * WB, WB)]
                        V.tensor_tensor(cb, ps[:, :, 0:WB], cb, ALU.add)
                        V.tensor_tensor(wb, ps[:, :, WB:], wb, ALU.add).then_inc(S("all_added"), 1)
                dve.wait_ge(*reached("all_added", NBLK * NCHUNK + 1))
                V.tensor_copy(at[:], ct[:]).then_inc(S("all_zeroed"), 1)
                dve.wait_ge(*reached("all_zeroed", 2))
            with dve.Else():
                V.nop()
            V.nop().then_inc(S("graph_ready"), 1)
            for j in range(NT):
                ins = V.tensor_tensor(at[:, j, j * P:(j + 1) * P], ct[:, j, j * P:(j + 1) * P], ident[0:P, 0:P], ALU.add)
            ins.then_inc(S("at_ready"), 1)
            dve.wait_ge(*reached("params_turned", 1))
            V.tensor_scalar(bnT[:, 4], bnT[:, 4], BN_EPS, None, ALU.add)
            V.tensor_scalar(bnT[:, 9], bnT[:, 9], BN_EPS, None, ALU.add).then_inc(S("bn_var_ready"), 1)
            for j in range(NT):
                dve.wait_ge(*reached("at_turned", j + 1))
                V.tensor_scalar(cols(negm[:, j, :]), (psA, psB)[j % 2][0:P, 0:NT, 0:P], 0.5, NEG, ALU.is_lt, ALU.mult)\
                    .then_inc(S("negm_done"), 1)

            def attention(tag, heads, write, between=None):
                nh = heads
                for h in range(heads):
                    dve.wait_ge(*reached(tag + "_bc", h + 1))
                    for j in range(NT):
                        if h >= 1:
                            dve.wait_ge(*reached(tag + "_masked", (h - 1) * NT + j + 1))
                        V.tensor_tensor_reduce(out=cols(v[:, j, :]), in0=(psA, psB)[h % 2][0:P, 0:NT, 0:P],
                                               in1=cols(negm[:, j, :]), scale=1.0, scalar=NEG, op0=ALU.add,
                                               op1=ALU.max, accum_out=mx[:, j, h:h + 1]).then_inc(S(tag + "_masked"), 1)
                dve.wait_ge(*reached(tag + "_masked", heads * NT))
                dve.wait_ge(*reached(tag + "_al", NT))
                ald, als = al[:, :, nh:2 * nh], al[:, :, 0:nh]
                z, m = zz[:, :, 0:nh], mx[:, :, 0:nh]
                step(V.tensor_tensor(z, m, ald, ALU.add))
                step(V.scalar_tensor_tensor(out=m, in0=z, scalar=SLOPE, in1=z, op0=ALU.mult, op1=ALU.max))
                V.tensor_scalar(al2[:, :, 0:nh], als, SLOPE, None, ALU.mult)
                V.tensor_tensor(r1[:, :, 0:nh], ald, m, ALU.subtract)
                V.scalar_tensor_tensor(out=r2[:, :, 0:nh], in0=ald, scalar=SLOPE, in1=m, op0=ALU.mult, op1=ALU.subtract)\
                    .then_inc(S(tag + "_rows"), 1)
                if between is not None:
                    between()

                def larger(h, i):
                    dve.wait_ge(*reached(tag + "_v", h * NT + i + 1))
                    V.tensor_tensor(u[h % 2][:, i, :], u[h % 2][:, i, :], v[:, i, :], ALU.max).then_inc(S(tag + "_max"), 1)

                for h in range(heads):
                    dve.wait_ge(*reached(tag + "_u", (h + 1) * NT))
                    larger(h, 0)
                    for i in range(NT):
                        if i + 1 < NT:
                            larger(h, i + 1)
                        dve.wait_ge(*reached(tag + "_max", h * NT + i + 1))
                        V.scalar_tensor_tensor(out=u[h % 2][:, i, :], in0=u[h % 2][:, i, :], scalar=1.0, in1=at[:, i, 0:N],
                                               op0=ALU.min, op1=ALU.mult).then_inc(S(tag + "_p"), 1)
                    if h >= 1:
                        write(h - 1)
                write(heads - 1)

            def write_head(tag):
                def write(h):
                    dve.wait_ge(*reached(tag + "_agg", (h + 1) * NT))
                    if h >= 1:
                        dve.wait_ge(*reached(tag + "_out", h))
                    ps = (psC, psD)[h % 2][0:P, 0:NT * 65].rearrange("p (j c) -> p j c", c=65)
                    if tag == "l2a":
                        step(V.tensor_scalar(rden, ps[:, :, 64], 1e-16, None, ALU.add))
                        step(V.reciprocal(rden, rden))
                    else:
                        step(V.reciprocal(rden, ps[:, :, 64]))
                    V.tensor_tensor(gat[:, :, h * 64:(h + 1) * 64], ps[:, :, 0:64],
                                    rden.unsqueeze(2).to_broadcast([P, NT, 64]), ALU.mult).then_inc(S(tag + "_out"), 1)
                return write

            def write_l0b(h):
                for j in range(NT):
                    dve.wait_ge(*reached("l0b_agg", NT if j < NT - 1 else NT + 1))
                    ps = (psC, psD, psE, psF, last_out)[j]
                    step(V.reciprocal(rden[:, j:j + 1], ps[0:P, D:D + 1]))
                    V.scalar_tensor_tensor(out=x[:, j, :], in0=ps[0:P, 0:D], scalar=rden[:, j:j + 1], in1=x[:, j, :],
                                           op0=ALU.mult, op1=ALU.add).then_inc(S("l0b_out"), 1)

            def add_row(dst, src, rowv):
                return V.tensor_tensor(dst, src, rowv.unsqueeze(1).to_broadcast([P, NT, D]), ALU.add)

            add_row(x[:], x[:], b2_l0b[:]).then_inc(S("row_added"), 1)
            dve.wait_ge(*reached("row_added", 1))
            attention("l0a", 4, write_head("l0a"))
            dve.wait_ge(*reached("l0a_out", 4))
            V.nop().then_inc(S("l0a_done"), 1)
            fold(w_l0b, 1, 2)
            V.nop().then_inc(S("l0b_folded"), 1)
            ones("l0b", 1)

            def between():
                fold(w_l2, 4, 4)
                V.nop().then_inc(S("params_used"), 1)
                step(V.tensor_reduce(outdeg, ct[:], AX, ALU.add))

            attention("l0b", 1, write_l0b, between)
            dve.wait_ge(*reached("l0b_out", NT))
            dve.wait_ge(*reached("bn_pow_ready", 1))
            for n in (0, 5):
                b_, g_, be_, m_, v_ = (bnT[:, n + i] for i in range(5))
                step(V.tensor_tensor(g_, g_, v_, ALU.mult))
                step(V.tensor_tensor(b_, b_, m_, ALU.subtract))
                step(V.tensor_tensor(b_, b_, g_, ALU.mult))
                step(V.tensor_tensor(be_, be_, b_, ALU.add))
            V.nop().then_inc(S("bn_ready"), 1)

            def top(tag, lgt):
                for j in range(NT):
                    ins = V.max(mx8[:, j, :], lgt[:, j, :])
                step(ins)
                for j in range(NT):
                    ins = V.max_index(ix8[:, j, :], mx8[:, j, :], lgt[:, j, :])
                step(ins)
                step(V.tensor_copy(ixf, ix8[:, :, 0:2]))

            def onehot(dst, col, ne):
                return V.tensor_tensor(dst, iota_f[0:P, 0:ne].unsqueeze(1).to_broadcast([P, NT, ne]),
                                       ixf[:, :, col:col + 1].to_broadcast([P, NT, ne]), ALU.is_equal)

            def bias_rows(tag, each):
                dve.wait_ge(*reached(tag + "_wturned", 1))
                V.tensor_copy(cols(wgT), psA[0:8, 0:NT, 0:P]).then_inc(S(tag + "_wT"), 1)
                for j in range(NT):
                    dve.wait_ge(*reached(tag + "_bias", j + 1))
                    each(j, (psC, psD)[j % 2][0:P, 0:D]).then_inc(S(tag + "_bias_out"), 1)

            if stages >= 2:
                V.memset(zrow, 0.0).then_inc(S("zrow_ready"), 1)
                normalise("l0f", x, xln, "l0f_xln")
                turned("l0f")
                dve.wait_ge(*reached("l0f_logits", 1))
                step(V.tensor_copy(lg8, psC[0:P, 0:NT * E0].rearrange("p (j e) -> p j e", e=E0)))
                top("l0", lg8)
                step(onehot(oh0, 0, E0))
                V.tensor_copy(ohb0, oh0).then_inc(S("l0f_onehot"), 1)
                V.tensor_tensor(lg8, lg8, mx8[:, :, 0:1].to_broadcast([P, NT, E0]), ALU.subtract)\
                    .then_inc(S("shift0_ready"), 1)
                dve.wait_ge(*reached("l0_ranks", 1))
                step(V.tensor_tensor(t0, psD[0:P, 0:NT * E0].rearrange("p (j e) -> p j e", e=E0), oh0, ALU.mult))
                step(V.tensor_reduce(scol[:, :, 0], t0, AX, ALU.add))
                step(V.tensor_scalar(scol[:, :, 1], scol[:, :, 0], CAP + 0.5, None, ALU.is_lt))
                step(V.tensor_scalar(scol[:, :, 0], scol[:, :, 0], float(CAP), -1.0, ALU.min, ALU.add))
                step(V.scalar_tensor_tensor(out=scol[:, :, 0], in0=ixf[:, :, 0], scalar=float(CAP), in1=scol[:, :, 0],
                                            op0=ALU.mult, op1=ALU.add))
                step(V.tensor_copy(sloti[:, :, 1], scol[:, :, 0]))
                step(V.scalar_tensor_tensor(out=scol[:, :, 2], in0=tokid, scalar=float(E0 * CAP), in1=scol[:, :, 0],
                                            op0=ALU.add, op1=ALU.subtract))
                step(V.tensor_scalar(zz[:, :, 0], scol[:, :, 1], -1.0, 1.0, ALU.mult, ALU.add))
                step(V.tensor_tensor(scol[:, :, 2], scol[:, :, 2], zz[:, :, 0], ALU.mult))
                step(V.tensor_tensor(scol[:, :, 2], scol[:, :, 2], scol[:, :, 0], ALU.add))
                V.tensor_copy(sloti[:, :, 0], scol[:, :, 2]).then_inc(S("slots0_ready"), 1)
                dve.wait_ge(*reached("exp0_ready", 1))
                step(V.tensor_reduce(zz[:, :, 0], ex8, AX, ALU.add))
                step(V.reciprocal(zz[:, :, 0], zz[:, :, 0]))
                step(V.tensor_tensor(rden, zz[:, :, 0], scol[:, :, 1], ALU.mult))
                bias_rows("l0f", lambda j, ps: V.tensor_copy(clip[:, j, :], ps))
                dve.wait_ge(*reached("bufs_turned1", 1))
                V.tensor_copy(bufT[:, 1, :].rearrange("p (e c) -> p e c", e=E0), psB[:, :, 0:CAP]).then_inc(S("bufT1"), 1)
                V.nop().then_inc(S("l0_y_free"), 2)
                with dve.Fori(0, 2) as r:
                    for q in range(4):
                        e = 4 * r + q
                        dve.wait_ge(*reached("l0_y", e + 1))
                        V.tensor_copy(ysb[:, bass.ds(e, 1), :].rearrange("p a d -> p (a d)"), (psC, psD)[q % 2][0:CAP, 0:D])\
                            .then_inc(S("l0_y_free"), 1)
                dve.wait_ge(*reached("l0_y_free", E0 + 2))
                V.nop().then_inc(S("ysb_ready"), 1)
                dve.wait_ge(*reached("l0_tokens_back", 16 * NT))
                step(V.tensor_tensor(yg0, yg0, clip, ALU.add))
                step(V.tensor_tensor(yg0, yg0, rden.unsqueeze(2).to_broadcast([P, NT, D]), ALU.mult))
                step(V.tensor_scalar(clip, yg0, 1e4, -1e4, ALU.min, ALU.max))
                step(V.tensor_tensor(nan_m, yg0, yg0, ALU.not_equal))
                step(V.tensor_scalar(bound, yg0, FLT_MAX, -FLT_MAX, ALU.min, ALU.max))
                step(V.tensor_tensor(inf_m, bound, yg0, ALU.not_equal))
                step(V.copy_predicated(yg0, inf_m, clip))
                step(V.memset(clip, 0.0))
                step(V.copy_predicated(yg0, nan_m, clip))
                step(V.tensor_tensor(x[:], x[:], yg0, ALU.add))
            if stages >= 3:
                V.tensor_scalar(outdeg, outdeg, 1.0, None, ALU.max).then_inc(S("deg_ready"), 1)
                V.memset(hs[:, :, 64:65], 1.0).then_inc(S("gcn_ones"), 1)
                normalise("l1g", x, xln, "l1g_xln")
                turned("l1g")
                dve.wait_ge(*reached("b_out_loaded", 16))
                step(add_row(x[:], x[:], b_out[:]))
                dve.wait_ge(*reached("gcn_agg", 1))
                ps = psE[0:P, 0:NT * 65].rearrange("p (j c) -> p j c", c=65)
                V.tensor_scalar(vare, ps[:, :, 64], 1.0, None, ALU.max).then_inc(S("indeg_ready"), 1)
                dve.wait_ge(*reached("ndst_ready", 1))
                V.tensor_tensor(agg, ps[:, :, 0:64], rden.unsqueeze(2).to_broadcast([P, NT, 64]), ALU.mult)\
                    .then_inc(S("gcn_scaled"), 1)
                for j in range(NT):
                    dve.wait_ge(*reached("gcn_y", j + 1))
                    V.tensor_tensor(x[:, j, :], (psC, psD)[j % 2][0:P, 0:D], x[:, j, :], ALU.add).then_inc(S("gcn_out"), 1)
                dve.wait_ge(*reached("gcn_out", NT))
            if stages >= 4:
                normalise("l1f", x, xln, "l1f_xln")
                turned("l1f")
                dve.wait_ge(*reached("l1f_logits", 1))
                step(V.tensor_copy(lg, psC[0:P, 0:NT * E1].rearrange("p (j e) -> p j e", e=E1)))
                top("l1", lg)
                V.tensor_tensor(gsel[:, :, 0], mx8[:, :, 1], mx8[:, :, 0], ALU.subtract).then_inc(S("shift1_ready"), 1)
                onehot(oh1[:, 0:NT, :], 0, E1)
                step(onehot(oh1[:, NT:, :], 1, E1))
                V.tensor_tensor(ohb1, oh1[:, 0:NT, :], oh1[:, NT:, :], ALU.add).then_inc(S("l1f_onehot"), 1)
                dve.wait_ge(*reached("l1_ranks", 1))
                V.tensor_copy(cntcol, psF[0:E1, 0:1]).then_inc(S("cntcol_ready"), 1)
                V.tensor_copy(pos1, psD[0:P, 0:NT * E1].rearrange("p (j e) -> p j e", e=E1))
                V.tensor_copy(cntb, psE[0:P, 0:E1])
                dve.wait_ge(*reached("l1_offsets", 1))
                step(V.tensor_copy(offb, psC[0:P, 0:E1]))
                step(V.tensor_tensor(pos1, pos1, offb.unsqueeze(1).to_broadcast([P, NT, E1]), ALU.add))
                for k in range(2):
                    step(V.tensor_tensor(t1, pos1, oh1[:, k * NT:(k + 1) * NT, :], ALU.mult))
                    step(V.tensor_reduce(scol[:, :, k], t1, AX, ALU.add))
                    step(V.tensor_scalar(scol[:, :, k], scol[:, :, k], -1.0, None, ALU.add))
                    ins = V.tensor_copy(sloti[:, :, k], scol[:, :, k])
                ins.then_inc(S("slots1_ready"), 1)
                dve.wait_ge(*reached("exp1_ready", 1))
                step(V.tensor_scalar(gsel[:, :, 0], gsel[:, :, 1], 1.0, None, ALU.add))
                step(V.reciprocal(gsel[:, :, 0], gsel[:, :, 0]))
                step(V.tensor_tensor(gsel[:, :, 1], gsel[:, :, 1], gsel[:, :, 0], ALU.mult))
                for r in range(ROUNDS):
                    ins = V.scalar_tensor_tensor(out=starts_f[:, :, r], in0=cntb[0:1, :], scalar=float(r * WIN),
                                                 in1=offb[0:1, :], op0=ALU.min, op1=ALU.add)
                step(V.tensor_reduce(flagf[:, 2:3], cntb[0:1, :], AX, ALU.max))
                step(V.tensor_scalar(flagf[:, 3:4], flagf[:, 2:3], WIN + 0.5, None, ALU.is_gt))
                V.tensor_copy(starts, starts_f)
                V.memset(xsT[:, :, SLOTS:], 0.0)
                V.tensor_copy(flag2_i[:, 0:1], flagf[:, 3:4]).then_inc(S("flag2_ready"), 1)
                for g in range(2):
                    dve.wait_ge(*reached("xs_turned", 2 * g + 2))
                    V.tensor_copy(xsT[:, 1, g * N:(g + 1) * N].rearrange("p (j q) -> p j q", q=P), psB[:, 0:NT, 0:P])\
                        .then_inc(S("xsT_dve"), 1)
                dve.wait_ge(*reached("flag2_ready", 1))
                full = dve.value_load(flag2_i[0:1, 0:1], min_val=0, max_val=1)

                def out1(ps, e, start):
                    for m in range(KD):
                        ins = V.tensor_scalar(yT[:, m, bass.ds(start, WIN)], ps[:, m, 0:WIN], b2T1[:, m, bass.ds(e, 1)], None,
                                              ALU.add)
                    return ins

                V.nop().then_inc(S("l1_y_free"), 2)
                V.nop().then_inc(S("l1_used"), 2)
                V.nop().then_inc(S("l1_relu"), F1 // 128)
                V.nop().then_inc(S("any_y_free"), 1)
                V.nop().then_inc(S("any_expert_used"), 1)
                with dve.If(full == 1):
                    with dve.Fori(0, E1) as e:
                        with dve.Fori(0, ROUNDS) as r:
                            n = e * ROUNDS + r
                            start = dve.value_load(starts[0:1, bass.ds(e, 1), bass.ds(r, 1)].rearrange("p a b -> p (a b)"),
                                                   min_val=0, max_val=SLOTS)
                            dve.wait_ge(*reached("any_y", n + 1))
                            dve.wait_ge(*reached("any_y_free", n + 1))
                            out1(psA, e, start).then_inc(S("any_y_free"), 1)
                        V.nop().then_inc(S("any_expert_used"), 1)
                    dve.wait_ge(*reached("any_y_free", E1 * ROUNDS + 1))
                with dve.Else():
                    with dve.Fori(0, E1 // RING) as r:
                        for q in range(RING):
                            e = r * RING + q
                            start = dve.value_load(starts[0:1, bass.ds(e, 1), 0:1].rearrange("p a b -> p (a b)"),
                                                   min_val=0, max_val=SLOTS)
                            dve.wait_ge(*reached("l1_used", e + 3))
                            dve.wait_ge(*reached("l1_y_free", e + 2))
                            out1((psA, psB)[q % 2], e, start).then_inc(S("l1_y_free"), 1)
                    dve.wait_ge(*reached("l1_y_free", E1 + 2))
                V.nop().then_inc(S("yT_ready"), 1)
                V.nop().then_inc(S("l1_experts_done"), 1)
                for g in (1, 3):
                    dve.wait_ge(*reached("ys_turned", g + 1))
                    V.tensor_copy(xs[:, 2 * g:2 * g + 2, :].rearrange("p t (m d) -> p (t m) d", m=2), psB[0:P, 0:4, 0:128])\
                        .then_inc(S("ys_dve"), 1)
                dve.wait_ge(*reached("ys_act", 3))
                dve.wait_ge(*reached("ys_dve", 2))
                V.nop().then_inc(S("ys_ready"), 1)
                dve.wait_ge(*reached("l1_tokens_back", 32 * NT))
                for k in range(2):
                    for j in range(NT):
                        ins = V.scalar_tensor_tensor(out=x[:, j, :], in0=yg1[:, k * NT + j, :], scalar=gsel[:, j, k:k + 1],
                                                     in1=x[:, j, :], op0=ALU.mult, op1=ALU.add)
                    step(ins)
            if stages >= 5:
                normalise("l2g", x, xln, "l2g_xln")
                turned("l2g")
                ones("l2a", 4)
                attention("l2a", 4, write_head("l2a"))
                dve.wait_ge(*reached("l2a_out", 4))
                dve.wait_ge(*reached("l2_rows_loaded", 48))
                step(add_row(gat, gat, l2_bias))
                normalise("l2n", gat, gat, "l2n_xln")
                dve.wait_ge(*reached("l2n_xln", 1))
                step(V.tensor_tensor(gat, gat, l2_gamma.unsqueeze(1).to_broadcast([P, NT, D]), ALU.mult))
                step(add_row(x[:], x[:], l2_beta))
                step(V.tensor_tensor(x[:], x[:], gat, ALU.add))

            def dense(tag, two):
                normalise(tag, x, xln, tag + "_xln")
                turned(tag)
                dve.wait_ge(*reached(tag + "_logits", 1))
                step(V.tensor_copy(lg8, psC[0:P, 0:NT * 8].rearrange("p (j e) -> p j e", e=8)))
                top(tag, lg8)
                V.tensor_tensor(lg8, lg8, mx8[:, :, 0:1].to_broadcast([P, NT, 8]), ALU.subtract).then_inc(S(tag + "_shift"), 1)
                if two:
                    onehot(t8, 0, 8)
                    step(onehot(wgt, 1, 8))
                    step(V.tensor_tensor(t8, t8, wgt, ALU.add))
                    step(V.tensor_tensor(x[:], x[:], xln[:], ALU.add))
                dve.wait_ge(*reached(tag + "_exp", 1))
                step(V.tensor_reduce(zz[:, :, 0], ex8, AX, ALU.add))
                step(V.reciprocal(zz[:, :, 0], zz[:, :, 0]))
                ins = V.tensor_tensor(wgt, ex8, zz[:, :, 0:1].to_broadcast([P, NT, 8]), ALU.mult)
                if two:
                    step(ins)
                    step(V.tensor_tensor(wgt, wgt, t8, ALU.mult))
                    step(V.tensor_reduce(zz[:, :, 0], wgt, AX, ALU.add))
                    step(V.tensor_scalar(zz[:, :, 0], zz[:, :, 0], 1e-12, None, ALU.max))
                    step(V.reciprocal(zz[:, :, 0], zz[:, :, 0]))
                    ins = V.tensor_tensor(wgt, wgt, zz[:, :, 0:1].to_broadcast([P, NT, 8]), ALU.mult)
                ins.then_inc(S(tag + "_w"), 1)
                bias_rows(tag, lambda j, ps: V.tensor_tensor(x[:, j, :], ps, x[:, j, :], ALU.add))
                dve.wait_ge(*reached(tag + "_bias_out", NT))
                V.nop().then_inc(S(tag + "_y_free"), 2)
                with dve.Fori(0, E2 // 2) as r:
                    for q in range(2):
                        for j in range(NT):
                            n = (2 * r + q) * NT + j
                            dve.wait_ge(*reached(tag + "_y", n + 1))
                            dve.wait_ge(*reached(tag + "_y_free", n + 1))
                            V.scalar_tensor_tensor(out=x[:, j, :], in0=(psC, psD)[(q * NT + j) % 2][0:P, 0:D],
                                                   scalar=wgt[:, j, bass.ds(2 * r + q, 1)], in1=x[:, j, :],
                                                   op0=ALU.mult, op1=ALU.add).then_inc(S(tag + "_y_free"), 1)
                dve.wait_ge(*reached(tag + "_y_free", E2 * NT + 2))

            if stages >= 6:
                dense("l2f", False)
            if stages >= 7:
                normalise("l3g", x, xln, "l3g_xln")
                turned("l3g")
                for j in range(NT):
                    dve.wait_ge(*reached("l3_agg", j + 1))
                    V.scalar_tensor_tensor(out=x[:, j, :], in0=(psC, psD)[j % 2][0:P, 0:D], scalar=0.0, in1=x[:, j, :],
                                           op0=ALU.max, op1=ALU.add).then_inc(S("l3_out"), 1)
                dve.wait_ge(*reached("l3_out", NT))
            if stages >= 8:
                dense("l3f", True)
            V.nop().then_inc(S("x_final"), 1)


NAMES = ["x", "src", "dst", "edge_weight"] + ["L0_gnn_" + n for n in (
    "W1", "att_src1", "att_dst1", "b1", "W2", "att_src2", "att_dst2", "b2")] + ["L0_ffn_" + n for n in (
    "gate_w", "gate_b", "w1", "b1", "w2", "b2")] + ["L1_gnn_" + n for n in ("W_gcn", "b_gcn", "W_out", "b_out")] + [
    "L1_ffn_" + n for n in ("Wr", "br", "W1", "b1", "W2", "b2")] + ["L2_gnn_" + n for n in (
    "W", "att_src", "att_dst", "bias", "gamma", "beta")] + ["L2_ffn_" + n for n in (
    "Wr", "br", "W1", "b1", "g1", "be1", "m1", "v1", "W2", "b2", "g2", "be2", "m2", "v2", "Wo", "bo")] + [
    "L3_gnn_weight"] + ["L3_ffn_" + n for n in ("router_w", "w1", "b1", "w2", "b2")]


def kernel(**inputs):
    import numpy as np
    import concourse.bacc as bacc
    from concourse.bass_utils import run_bass_kernel_spmd

    nc = bacc.Bacc("TRN2", target_bir_lowering=False, num_devices=1)
    arrays, aps = {}, {}
    for name in NAMES:
        v = np.ascontiguousarray(inputs[name])
        arrays["in_" + name] = v
        aps[name] = nc.dram_tensor("in_" + name, v.shape, mybir.dt.from_np(v.dtype), kind="ExternalInput").ap()
    out = nc.dram_tensor("out_x", (N, D), F32, kind="ExternalOutput").ap()
    build(nc, aps, out)
    r = run_bass_kernel_spmd(nc, [arrays], core_ids=[0])
    return r.results[0]["out_x"]
```

```python
from contextlib import ExitStack

import concourse.bass as bass
from concourse import mybir

F32 = mybir.dt.float32
I32 = mybir.dt.int32
U32 = mybir.dt.uint32
BF16 = mybir.dt.bfloat16
F16 = mybir.dt.float16
ALU = mybir.AluOpType
ACT = mybir.ActivationFunctionType
AX = mybir.AxisListType.X

N, D, E = 625, 256, 20625
P, NT = 125, 5
KD = D // 128
EPP = E // P
CH = 10
CHE = CH * P
CHA = 5
NCHUNK = E // (CHA * P)
WB = 32
NBLK = (N + WB - 1) // WB
NPAD = NBLK * WB
HN = (N + 1) // 2
LN_EPS, BN_EPS, SLOPE = 1e-5, 1e-3, 0.2
NEG = -1e30
E0, F0, CAP = 8, 1024, 98
E1, F1 = 64, 512
SLOTS = 2 * N
WIN = 96
ROUNDS = (N + WIN - 1) // WIN
E2 = 8
CHUNK = 2048
RING = 8
DENSE = {"l2f": (("L2_ffn_W1", "L2_ffn_W2", "L2_ffn_Wo"), (0, 1, 4, 5)),
         "l3f": (("L3_ffn_w1", "L3_ffn_w2"), (2, 3, 6, 7))}
FLT_MAX = 3.4028235e38
PROJ = 10
PARAMS = 26


TAGS = ("l0g", "l0a", "l0m", "l0b", "l0f", "l1g", "l1f", "l2g", "l2a", "l2n", "l2f", "l3g", "l3f")
NORMS = ("l0g", "l0f", "l1g", "l1f", "l2g", "l2n", "l2f", "l3g", "l3f")
TURNS = ("l0g", "l0m", "l0f", "l1g", "l1f", "l2g", "l2f", "l3g", "l3f")
ATTS = ("l0a", "l0b", "l2a")
HEADS = {"l0a": 4, "l0b": 1, "l2a": 4}
RECURRING = {k: (NORMS, 1) for k in ("var", "rstd")} | {"xln": (NORMS, NT)}
RECURRING |= {k: (TURNS, 1) for k in ("turned0", "turned1", "xT0", "xT1")}
RECURRING |= {k: (ATTS, NT) for k in ("proj", "hs", "al")}
RECURRING |= {"ones": (ATTS, 1)}
RECURRING |= {k: (ATTS, HEADS) for k in ("bc", "rows", "r1", "r2")}
RECURRING |= {k: (ATTS, {t: n * NT for t, n in HEADS.items()}) for k in ("masked", "u", "v", "max", "p")}
RECURRING |= {"agg": (ATTS, {"l0a": 4 * NT, "l0b": NT + 1, "l2a": 4 * NT}), "out": (ATTS, {"l0a": 4, "l0b": NT, "l2a": 4})}
RECURRING |= {"logits": (("l0f", "l1f", "l2f", "l3f"), 1), "onehot": (("l0f", "l1f"), 1)}
RECURRING |= {k: (("l0f", "l2f", "l3f"), 1) for k in ("wturned", "wT")}
RECURRING |= {k: (("l0f", "l2f", "l3f"), NT) for k in ("bias", "bias_out")}
RECURRING |= {k: (("l2f", "l3f"), 1) for k in ("shift", "exp", "w")}
RECURRING |= {"hidden": (("l2f", "l3f"), {"l2f": 2 * KD * E2, "l3f": KD * E2})}
RECURRING |= {"act": (("l2f", "l3f"), {"l2f": 2 * KD * E2 + 2, "l3f": KD * E2 + 2})}
RECURRING |= {"y": (("l2f", "l3f"), NT * E2), "y_free": (("l2f", "l3f"), NT * E2 + 2)}

ONCE = {
    "dve_stage": ("pack_ready", "base_ready", "l0a_folded", "flag_ready", "graph_ready", "at_ready", "bn_var_ready",
                  "row_added", "l0a_done", "l0b_folded", "params_used", "zrow_ready", "shift0_ready", "slots0_ready",
                  "bn_ready", "bufT1", "deg_ready",
                  "ndst_row_ready", "gcn_scaled", "shift1_ready", "cntcol_ready",
                  "slots1_first", "slots1_ready", "flag2_ready", "yT_ready", "l1_experts_done"),
    "pe_stage": ("base_sum", "total_sum", "params_acc", "l0_ranks", "bufs_turned0", "bufs_turned1", "indeg_sum",
                 "ndst_turned", "gcn_agg", "l1_ranks", "l1_offsets"),
    "act_stage": ("params_turned", "exp0_ready", "bufT0", "gcn_hT", "exp1_ready"),
    "pool_stage": ("iota_ready", "consts_ready", "bn_pow_ready", "norms_ready"),
}
STAGE_OF = {name: (sem, n) for sem, names in ONCE.items() for n, name in enumerate(names)}


class Steps:

    def __init__(self, sem):
        self.sem, self.n = sem, 0

    def done(self, ins):
        ins.then_inc(self.sem, 1)
        self.n += 1

    def wait(self, eng):
        eng.wait_ge(self.sem, self.n)


def build(nc, a, out):
    with ExitStack() as ctx:
        def sb(name, shape, dt=F32):
            return ctx.enter_context(nc.sbuf_tensor(name, shape, dt))

        def pb(name, shape, dt=F32):
            return ctx.enter_context(nc.psum_tensor(name, shape, dt))

        sems = {}

        def S(name):
            if name[:3] in TAGS and name[4:] in RECURRING:
                name = "each_" + name[4:]
            elif name in STAGE_OF:
                name = STAGE_OF[name][0]
            if name not in sems:
                sems[name] = ctx.enter_context(nc.semaphore(name))
            return sems[name]

        def reached(name, count):
            tag, kind = name[:3], name[4:]
            if tag in TAGS and kind in RECURRING:
                order, per = RECURRING[kind]
                for t in order[:order.index(tag)]:
                    count = count + (per[t] if isinstance(per, dict) else per)
            elif name in STAGE_OF:
                count = count + STAGE_OF[name][1]
            return S(name), count

        edges_d = nc.dram_tensor("edges_d", (E, 5), F32, kind="Internal").ap()
        buf_d = nc.dram_tensor("buf_d", (E0 * CAP + N, D), F32, kind="Internal").ap()
        ybuf_d = nc.dram_tensor("ybuf_d", (E0 * CAP, D), F32, kind="Internal").ap()
        xs_d = nc.dram_tensor("xs_d", (SLOTS, D), F32, kind="Internal").ap()
        ys_d = nc.dram_tensor("ys_d", (SLOTS, D), F32, kind="Internal").ap()

        x = sb("x", [P, NT, D])
        xln = sb("xln", [P, NT, D])
        xT = sb("xT", [128, KD, N])
        ct = sb("ct", [P, NT, NPAD])
        wt = sb("wt", [P, NT, NPAD])
        at = sb("at", [P, NT, NPAD])
        negm = sb("negm", [P, NT, N])
        ring = sb("ring", [128, RING * CHUNK])
        work = sb("work", [128, 12100])
        hs = sb("hs", [P, NT, 260])
        small = sb("small", [128, 1910])

        class Carver:
            def __init__(self, tile):
                self.tile, self.at = tile, 0

            def __call__(self, shape, dt=F32, parts=128):
                n = 1
                for s in shape:
                    n *= s
                words = (n + 1) // 2 if dt in (BF16, F16) else n
                v = self.tile[0:parts, self.at:self.at + words]
                self.at += words
                assert self.at <= self.tile.shape[1], self.at
                if dt != F32:
                    v = v.bitcast(dt)[:, 0:n]
                if len(shape) == 2:
                    v = v.rearrange("p (a b) -> p a b", a=shape[0])
                elif len(shape) == 3:
                    v = v.rearrange("p (a b c) -> p a b c", a=shape[0], b=shape[1])
                return v

        sm = Carver(small)
        ident = sb("ident", [128, 128])
        iota_i = sb("iota_i", [128, NPAD], I32)
        iota_f = sb("iota_f", [128, NPAD])
        iota_h = iota_i[:, 0:NPAD // 2].bitcast(F16)
        sel = sb("sel", [128, 2 * WB])
        tri_b = sm([P], BF16, P)
        tri_f = sm([P], F32, P)
        ones_bf = sm([P], BF16, P)
        strict = sm([E1], F32, E1)
        ones_f = sm([128], F32)
        half_neg = sm([D])
        w_l0a = sb("w_l0a", [128, KD, D + 8])
        w_l0b = sb("w_l0b", [128, KD, D + 2])
        w_l2 = sb("w_l2", [128, KD, D + 8])
        w_l3 = w_l0a[:, :, 0:D]
        w_gcn = sb("w_gcn", [128, KD, 64])
        w_out = sb("w_out", [64, D])
        gate0 = sb("gate0", [128, KD, E0])
        gate1 = sb("gate1", [128, KD, E1])
        gate2 = sb("gate2", [128, KD, E2])
        gate3 = sb("gate3", [128, KD, E2])
        rbias = sb("rbias", [P, E0 + E1 + E2])
        b1_l0a = sb("b1_l0a", [128, KD])
        b_gcn = sb("b_gcn", [64, 1])
        b2_l0b = sb("b2_l0b", [P, D])
        b_out = b2_l0b
        b1T0 = sb("b1T0", [128, F0 // 128, E0])
        b1T1 = sb("b1T1", [128, F1 // 128, E1])
        b2T1 = sb("b2T1", [128, KD, E1])
        bnT = sb("bnT", [128, 10, KD, E2])
        b1T3 = sb("b1T3", [128, KD, E2])
        brow = sb("brow", [E2, D])

        psA = pb("psA", [128, 8, 128])
        psB = pb("psB", [128, 8, 128])
        psC = pb("psC", [128, 512])
        psD = pb("psD", [128, 512])
        psEF = pb("psEF", [128, 8, 128])
        psE, psF = (psEF[:, 4 * i:4 * i + 4].rearrange("p a b -> p (a b)") for i in range(2))

        st6 = sm([NT, 6], F32, P)
        mv = sm([NT, 2], F32, P)
        vare = sm([NT], F32, P)
        rstd = sm([NT], F32, P)
        al = sm([NT, 8], F32, P)
        al2 = sm([NT, 4], F32, P)
        mx = sm([NT, 4], F32, P)
        zz = sm([NT, 4], F32, P)
        r1 = sm([NT, 4], F32, P)
        r2 = sm([NT, 4], F32, P)
        rden = sm([NT], F32, P)
        outdeg = sm([NT], F32, P)
        nsrc = sm([NT], F32, P)
        ndst = sm([NT], F32, P)
        cnt = sm([NBLK], F32, P)
        basef = sm([NBLK], F32, 1)
        base_i = sm([NBLK], I32, 1)
        flagf = sm([4], F32, 1)
        flag_i = sm([2], I32, 1)
        flag2_i = sm([2], I32, 1)
        scol = sm([NT, 3], F32, P)
        mx8 = sm([NT, 8], F32, P)
        ix8 = sm([NT, 8], U32, P)
        ixf = sm([NT, 2], F32, P)
        wgt = sm([NT, 8], F32, P)
        wgT = sm([N], F32, 8)
        gsel = sm([NT, 2], F32, P)
        sloti = sm([NT, 4], I32, P)
        tokid = sm([NT], F32, P)
        tok_i = sm([NT], I32, P)
        cntcol = sm([1], F32, E1)

        wk = Carver(work)
        ohs = [wk([CH, 2 * HN], BF16, P) for _ in range(2)]
        ohd = [wk([CH, 4, WB], BF16, P) for _ in range(2)]
        accs = [wk([2, HN]) for _ in range(2)]
        ebt = [wk([CH, 5], F32, P) for _ in range(2)]
        rk = Carver(ring)
        src_i = rk([EPP], I32, P)
        dst_i = rk([EPP], I32, P)
        ew = rk([EPP], F32, P)
        res = rk([EPP], F32, P)
        bf_part = rk([EPP + 1], BF16, P)
        pack = rk([EPP, 5], F32, P)
        dst_h = rk([EPP + 1], F16, P)
        junk_e = rk([EPP + 1], F16, P)
        b1r0 = rk([F0], F32, E0)
        b1r1 = rk([F1], F32, E1)
        b2r1 = rk([D], F32, E1)
        bnp = [rk([D], F32, E2) for _ in range(10)]
        b1r3 = rk([D], F32, E2)
        rw3 = rk([D], F32, E2)
        attv = [rk([D]) for _ in range(6)]
        attm = rk([KD, D])
        wk = Carver(work)
        u = [wk([NT, N], F32, P) for _ in range(2)]
        v = wk([NT, N], F32, P)
        gat = wk([NT, D], F32, P)
        l2_bias = wk([D], F32, P)
        l2_gamma = wk([D], F32, P)
        l2_beta = wk([D], F32, P)
        wk = Carver(work)
        bufs = wk([E0, D], F32, CAP)
        bufT = wk([KD, E0 * CAP])
        h0 = [wk([F0 // 128, CAP]), work[:, 0:F0 // 128 * CAP].rearrange("p (f c) -> p f c", f=F0 // 128)]
        ysb = wk([E0, D], F32, CAP)
        yg0 = wk([NT, D], F32, P)
        nan_m = wk([NT, D], I32, P)
        clip = wk([NT, D], F32, P)
        bound = work[0:P, 0:NT * D].rearrange("p (a b) -> p a b", a=NT)
        inf_m = work[0:P, NT * D:2 * NT * D].bitcast(I32).rearrange("p (a b) -> p a b", a=NT)
        oh0 = wk([NT, E0], F32, P)
        ohb0 = wk([NT, E0], BF16, P)
        t0 = wk([NT, E0], F32, P)
        zrow = wk([D], F32, P)
        assert wk.at <= 11400
        wk = Carver(work)
        xs = wk([2 * NT, D], F32, P)
        xsT = wk([KD, SLOTS + WIN])
        yT = wk([KD, SLOTS + WIN])
        yg1 = xsT[0:P].rearrange("p k n -> p (k n)")[:, 0:2 * NT * D].rearrange("p (t d) -> p t d", d=D)
        h1 = [wk([F1 // 128, WIN]) for _ in range(2)]
        oh1 = wk([2 * NT, E1], F32, P)
        ohb1 = wk([NT, E1], BF16, P)
        pos1 = wk([NT, E1], F32, P)
        t1 = wk([NT, E1], F32, P)
        lg = wk([NT, E1], F32, P)
        offb = wk([E1], F32, P)
        cntb = wk([E1], F32, P)
        starts_f = wk([E1, ROUNDS], F32, 1)
        starts = wk([E1, ROUNDS], I32, 1)
        wk = Carver(work)
        h1d = [wk([KD, N]) for _ in range(2)]
        h2d = [wk([KD, N]) for _ in range(2)]
        lg8 = sm([NT, 8], F32, P)
        ex8 = sm([NT, 8], F32, P)
        t8 = sm([NT, 8], F32, P)
        ndst_row = work[0:64, 11400:11400 + N]
        scaled = work[0:64, 0:N]
        hT = work[0:64, N:2 * N]

        unused = [xln[:].rearrange("p t d -> p (t d)")[:, i * N:(i + 1) * N] for i in range(2)]

        def cols(ap):
            return ap.rearrange("p (j q) -> p j q", q=P)

        def halves(ps):
            return ps[:].rearrange("p a b -> p (a b)").rearrange("p (h n) -> p h n", h=2)[:, :, 0:HN]

        def hidden0(f):
            return (psA, psB)[f // 4][:, f // 2 % 2 * 4 + f % 2, 0:CAP]

        def hidden1_ps(f):
            return (psC, psD, psE, psF)[f][:, 0:WIN]

        def slot(s):
            return ring[:, s * CHUNK:(s + 1) * CHUNK]

        tokens_by_tile = "(j p) d -> p j d"
        last_out = psA[0:P].rearrange("p a b -> p (a b)")[:, 0:D + 1]

        def kpn(w):
            return w.rearrange("(k p) n -> p k n", p=128)

        block = ctx.enter_context(nc.Block())

        @block.sync
        def _(sp):
            sp.dma_start(dst_i, a["dst"].rearrange("(p t) -> p t", t=EPP)).then_inc(S("dst_loaded"), 16)
            sp.dma_start(src_i, a["src"].rearrange("(p t) -> p t", t=EPP)).then_inc(S("edges_loaded"), 16)
            sp.dma_start(ew, a["edge_weight"].rearrange("(p t) -> p t", t=EPP)).then_inc(S("edges_loaded"), 16)
            sp.dma_start(x[:], a["x"].rearrange(tokens_by_tile, p=P)).then_inc(S("x_loaded"), 16)

            sp.wait_ge(*reached("pack_ready", 1))
            sp.dma_start(edges_d.rearrange("(p t) k -> p (t k)", t=EPP), pack.rearrange("p t k -> p (t k)"))\
                .then_inc(S("edges_packed"), 16)
            sp.wait_ge(*reached("edges_packed", 16))
            sp.wait_ge(*reached("base_ready", 1))

            def edge_run(start, n):
                return edges_d[bass.ds(start, n * P), :].rearrange("(p t) k -> p (t k)", t=n)

            def load_run(b, q):
                base = sp.value_load(base_i[0:1, bass.ds(b, 1)], min_val=0, max_val=E - CHE)
                sp.dma_start(ebt[q].rearrange("p t k -> p (t k)"), edge_run(base, CH))\
                    .then_inc(S(f"edge_run_loaded{q}"), 16)

            for q in range(2):
                load_run(q, q)

            small_loads = [0]

            def load(dst, src, **kw):
                sp.dma_start(dst, src, **kw).then_inc(S("params_loaded"), 16)
                small_loads[0] += 1

            load(b1r0, a["L0_ffn_b1"])
            load(b1r1, a["L1_ffn_b1"])
            load(b2r1, a["L1_ffn_b2"])
            for i, name in enumerate(["b1", "g1", "be1", "m1", "v1", "b2", "g2", "be2", "m2", "v2"]):
                load(bnp[i], a["L2_ffn_" + name])
            load(b1r3, a["L3_ffn_b1"])
            load(rw3, a["L3_ffn_router_w"])

            def next_run(i, q):
                sp.wait_ge(*reached("ohs_ready", 2 * i + q - 1))
                sp.wait_ge(*reached("kinds_ready", 2 * i + q - 1))
                load_run(2 * i + q, q)

            for q in range(2):
                next_run(1, q)
            load(w_gcn[:], kpn(a["L1_gnn_W_gcn"]))
            load(w_out[:], a["L1_gnn_W_out"])
            load(gate0[:], kpn(a["L0_ffn_gate_w"]))
            load(gate1[:], kpn(a["L1_ffn_Wr"]))
            load(gate2[:], kpn(a["L2_ffn_Wr"]))
            load(rbias[:, 0:E0], a["L0_ffn_gate_b"].partition_broadcast(P))
            load(rbias[:, E0:E0 + E1], a["L1_ffn_br"].partition_broadcast(P))
            load(rbias[:, E0 + E1:], a["L2_ffn_br"].partition_broadcast(P))
            load(b_gcn[:], a["L1_gnn_b_gcn"].rearrange("(p a) -> p a", a=1))
            load(b2_l0b[:], a["L0_gnn_b2"].partition_broadcast(P))
            load(brow[:], a["L0_ffn_b2"])
            assert small_loads[0] == PARAMS
            with sp.Fori(2, NBLK // 2) as i:
                for q in range(2):
                    next_run(i, q)

            sp.wait_ge(*reached("flag_ready", 1))
            missed = sp.value_load(flag_i[0:1, 0:1], min_val=0, max_val=1)
            with sp.If(missed == 1):
                with sp.Fori(0, NBLK) as b:
                    with sp.Fori(0, NCHUNK) as c:
                        sp.wait_ge(*reached("all_added", b * NCHUNK + c + 1))
                        sp.dma_start(ebt[0][:, 0:CHA].rearrange("p t k -> p (t k)"), edge_run(c * (CHA * P), CHA))\
                            .then_inc(S("all_loaded"), 16)
            with sp.Else():
                sp.nop()
            sp.nop()

            sp.wait_ge(*reached("params_used", 1))
            sp.wait_ge(*reached("params_acc", 1))

            def load_l0(c):
                e, half = c // 2, c % 2
                s = c % RING
                src = (a["L0_ffn_w2"] if half else a["L0_ffn_w1"])[e]
                sp.dma_start(slot(s).rearrange("p (k n) -> p k n", k=8 if half else KD), kpn(src))\
                    .then_inc(S(f"l0_weights{s}"), 16)

            for c in range(RING):
                load_l0(c)

            sp.wait_ge(*reached("l0a_proj", NT))
            sp.dma_start(w_l3, kpn(a["L3_gnn_weight"])).then_inc(S("w_l3_loaded"), 16)
            sp.wait_ge(*reached("zrow_ready", 1))
            for e in range(E0):
                sp.dma_start(buf_d[e * CAP:(e + 1) * CAP, :], zrow[0:CAP]).then_inc(S("buf_zeroed"), 16)
            sp.wait_ge(*reached("tokens_sent0", 16 * NT))
            sp.dma_start(bufs, buf_d[0:E0 * CAP, :].rearrange("(e c) d -> c e d", e=E0))\
                .then_inc(S("bufs_loaded"), 16)

            def store_y(e):
                sp.wait_ge(*reached("l0_y_free", e + 3))
                sp.dma_start(ybuf_d[e * CAP:(e + 1) * CAP, :], ysb[:, e, :]).then_inc(S("ybuf_stored"), 16)

            for c in range(RING, 2 * RING):
                e = (c - RING) // 2
                if c % 2:
                    sp.wait_ge(*reached("l0_y", e + 1))
                    store_y(e)
                else:
                    sp.wait_ge(*reached("l0_hidden", (e + 1) * (F0 // 256)))
                load_l0(c)

            def load_l1(e, s):
                sp.dma_start(slot(s)[:, 0:CHUNK // 2].rearrange("p (k n) -> p k n", k=KD),
                             kpn(a["L1_ffn_W1"][e] if isinstance(e, int) else
                                 a["L1_ffn_W1"][bass.ds(e, 1)].rearrange("a k n -> (a k) n")))\
                    .then_inc(S(f"l1_weights{s}"), 16)
                sp.dma_start(slot(s)[:, CHUNK // 2:].rearrange("p (k n) -> p k n", k=F1 // 128),
                             kpn(a["L1_ffn_W2"][e] if isinstance(e, int) else
                                 a["L1_ffn_W2"][bass.ds(e, 1)].rearrange("a k n -> (a k) n")))\
                    .then_inc(S(f"l1_weights{s}"), 16)

            for s in range(RING):
                e = (RING + s) // 2
                if s % 2:
                    sp.wait_ge(*reached("l0_y", e + 1))
                    store_y(e)
                elif s < 4:
                    sp.wait_ge(*reached("l0_hidden", (e + 1) * (F0 // 256)))
                if s < 4:
                    load_l1(s, s)
            sp.wait_ge(*reached("l0_tokens_back", 16 * NT))
            for s in range(4, RING):
                load_l1(s, s)
            sp.wait_ge(*reached("row_added", 1))
            sp.dma_start(b_out[:], a["L1_gnn_b_out"].partition_broadcast(P)).then_inc(S("b_out_loaded"), 16)
            sp.wait_ge(*reached("l0f_bias", NT))
            sp.dma_start(brow[:], a["L2_ffn_bo"]).then_inc(S("l2f_brow_loaded"), 16)
            sp.wait_ge(*reached("tokens_sent1", 32 * NT))
            sp.dma_start(xs, xs_d.rearrange("(t p) d -> p t d", p=P)).then_inc(S("xs_loaded"), 16)
            sp.wait_ge(*reached("flag2_ready", 1))
            full = sp.value_load(flag2_i[0:1, 0:1], min_val=0, max_val=1)
            with sp.If(full == 1):
                for s in range(RING):
                    sp.wait_ge(*reached(f"l1_weights{s}", 32))
                with sp.Fori(0, E1) as e:
                    sp.wait_ge(*reached("any_expert_used", e + 1))
                    w1 = a["L1_ffn_W1"][bass.ds(e, 1)].rearrange("a k n -> (a k) n")
                    w2 = a["L1_ffn_W2"][bass.ds(e, 1)].rearrange("a k n -> (a k) n")
                    sp.dma_start(slot(0)[:, 0:CHUNK // 2].rearrange("p (k n) -> p k n", k=KD), kpn(w1))\
                        .then_inc(S("any_expert_loaded"), 16)
                    sp.dma_start(slot(0)[:, CHUNK // 2:].rearrange("p (k n) -> p k n", k=F1 // 128), kpn(w2))\
                        .then_inc(S("any_expert_loaded"), 16)
            with sp.Else():
                with sp.Fori(1, E1 // RING) as r:
                    for s in range(RING):
                        sp.wait_ge(*reached("l1_used", (r - 1) * RING + s + 3))
                        load_l1(r * RING + s, s)
            sp.nop()
            for g in range(NT):
                sp.wait_ge(*reached("ys_dve" if g % 2 else "ys_act", g // 2 + 1))
                sp.dma_start(ys_d[2 * g * P:2 * (g + 1) * P, :].rearrange("(t p) d -> p t d", p=P),
                             xs[:, 2 * g:2 * g + 2, :]).then_inc(S("ys_stored"), 16)
            sp.wait_ge(*reached("l1_tokens_back0", 16 * NT))
            sp.wait_ge(*reached("l1_tokens_back1", 16 * NT))
            sp.dma_start(l2_bias, a["L2_gnn_bias"].partition_broadcast(P)).then_inc(S("l2_rows_loaded"), 16)
            sp.dma_start(l2_gamma, a["L2_gnn_gamma"].partition_broadcast(P)).then_inc(S("l2_rows_loaded"), 16)
            sp.dma_start(l2_beta, a["L2_gnn_beta"].partition_broadcast(P)).then_inc(S("l2_rows_loaded"), 16)

            def load_dense(tag, e, i):
                names, slots = DENSE[tag]
                for n, name in enumerate(names):
                    w = a[name][e] if isinstance(e, int) else a[name][bass.ds(e, 1)].rearrange("a k n -> (a k) n")
                    sp.dma_start(slot(slots[i])[:, n * KD * D:(n + 1) * KD * D].rearrange("p (k n) -> p k n", k=KD), kpn(w))\
                        .then_inc(S(f"{tag}_weights{i}"), 16)

            sp.wait_ge(*reached("l1_experts_done", 1))
            for tag in ("l2f", "l3f"):
                for i in range(4):
                    load_dense(tag, i, i)
            for tag in ("l2f", "l3f"):
                if tag == "l3f":
                    sp.wait_ge(*reached("l2f_bias", NT))
                    sp.dma_start(brow[:], a["L3_ffn_b2"]).then_inc(S("l3f_brow_loaded"), 16)
                for i in range(4):
                    sp.wait_ge(*reached(tag + "_y", (i + 1) * NT))
                    load_dense(tag, 4 + i, i)

            for j in range(NT):
                sp.wait_ge(*reached("l3f_bias_out", j + 1))
                sp.dma_start(out[j * P:(j + 1) * P, :], x[:, j, :]).then_inc(S("out_stored"), 16)
            sp.wait_ge(*reached("out_stored", 16 * NT))

        @block.gpsimd
        def _(pool):
            st = Steps(S("pool_steps"))
            nc.gpsimd.iota(iota_i[:], [[1, NPAD]], base=0, channel_multiplier=0).then_inc(S("iota_ready"), 1)
            st.done(nc.gpsimd.memset(ident[:], 0.0))
            st.done(nc.gpsimd.memset(sel[:], 0.0))
            st.done(nc.gpsimd.memset(tri_f, 1.0))
            st.done(nc.gpsimd.memset(strict, 1.0))
            st.done(nc.gpsimd.memset(ones_f, 1.0))
            st.done(nc.gpsimd.memset(half_neg, -0.5))
            st.done(nc.gpsimd.memset(ones_bf, 1.0))
            st.wait(pool)

            def diag(t, base, n, step=1, op=ALU.not_equal, fill=1.0, cm=1):
                st.done(nc.gpsimd.affine_select(out=t, in_=t, compare_op=op, fill=fill, base=base,
                                                pattern=[[step, n]], channel_multiplier=cm))

            diag(ident[:], 0, 128, -1)
            diag(sel[:, 0:WB], 0, WB, -1)
            for k in range(1, 4):
                diag(sel[:, WB:], -k * WB, WB, -1)
                st.wait(pool)
            diag(tri_f, 0, P, 1, ALU.is_ge, 0.0, -1)
            diag(strict, -1, E1, 1, ALU.is_ge, 0.0, -1)
            st.wait(pool)
            nc.gpsimd.iota(tok_i, [[P, NT]], base=0, channel_multiplier=1).then_inc(S("consts_ready"), 1)

            def power(tag):
                pool.wait_ge(*reached(tag + "_var", 1))
                nc.gpsimd.tensor_tensor(rstd, vare, half_neg[0:P, 0:NT], ALU.pow).then_inc(S(tag + "_rstd"), 1)

            power("l0g")

            def kinds(s, n):
                d = ohd[s][:, 0:n]
                return nc.gpsimd.tensor_tensor(
                    d[:, :, 1:4, :], d[:, :, 0:1, :].to_broadcast([P, n, 3, WB]),
                    ebt[s][:, 0:n, 2:5].unsqueeze(3).to_broadcast([P, n, 3, WB]), ALU.mult)

            with pool.Fori(0, NBLK // 2) as i:
                for q in range(2):
                    pool.wait_ge(*reached("ohd_ready", 2 * i + q + 1))
                    kinds(q, CH).then_inc(S("kinds_ready"), 1)
            pool.wait_ge(*reached("flag_ready", 1))
            missed = pool.value_load(flag_i[0:1, 0:1], min_val=0, max_val=1)
            with pool.If(missed == 1):
                with pool.Fori(0, NBLK) as b:
                    with pool.Fori(0, NCHUNK) as c:
                        pool.wait_ge(*reached("all_ohd", b * NCHUNK + c + 1))
                        kinds(0, CHA).then_inc(S("all_kinds"), 1)
            with pool.Else():
                pool.nop()
            pool.nop()

            pool.wait_ge(*reached("bn_var_ready", 1))
            hn = half_neg[:, 0:KD * E2].rearrange("p (f e) -> p f e", e=E2)
            nc.gpsimd.tensor_tensor(bnT[:, 4], bnT[:, 4], hn, ALU.pow)
            nc.gpsimd.tensor_tensor(bnT[:, 9], bnT[:, 9], hn, ALU.pow).then_inc(S("bn_pow_ready"), 1)
            power("l0f")
            pool.wait_ge(*reached("slots0_ready", 1))
            pool.wait_ge(*reached("buf_zeroed", 16 * E0))
            for j in range(NT):
                nc.gpsimd.indirect_dma_start(
                    buf_d, bass.IndirectOffsetOnAxis(ap=sloti[:, j, 0:1], axis=0), xln[:, j, :], None)\
                    .then_inc(S("tokens_sent0"), 16)
            pool.wait_ge(*reached("ybuf_stored", 16 * E0))
            for j in range(NT):
                nc.gpsimd.indirect_dma_start(
                    yg0[:, j, :], None, ybuf_d, bass.IndirectOffsetOnAxis(ap=sloti[:, j, 1:2], axis=0))\
                    .then_inc(S("l0_tokens_back"), 16)
            pool.wait_ge(*reached("deg_ready", 1))
            nc.gpsimd.tensor_tensor(nsrc, outdeg, half_neg[0:P, 0:NT], ALU.pow)
            nc.gpsimd.tensor_tensor(ndst, ndst, half_neg[0:P, 0:NT], ALU.pow).then_inc(S("norms_ready"), 1)
            power("l1g")
            power("l1f")
            for k in range(2):
                pool.wait_ge(*reached("slots1_ready" if k else "slots1_first", 1))
                for j in range(NT):
                    nc.gpsimd.indirect_dma_start(
                        xs_d, bass.IndirectOffsetOnAxis(ap=sloti[:, j, k:k + 1], axis=0), xln[:, j, :], None)\
                        .then_inc(S("tokens_sent1"), 16)
            pool.wait_ge(*reached("ys_stored", 16 * NT))
            for k in range(2):
                for j in range(NT):
                    nc.gpsimd.indirect_dma_start(
                        yg1[:, k * NT + j, :], None, ys_d,
                        bass.IndirectOffsetOnAxis(ap=sloti[:, j, k:k + 1], axis=0))\
                        .then_inc(S(f"l1_tokens_back{k}"), 16)
            power("l2g")
            power("l2n")
            power("l2f")
            power("l3g")
            power("l3f")

        @block.scalar
        def _(act):
            def load(dst, src, **kw):
                act.dma_start(dst, src, **kw).then_inc(S("proj_loaded"), 16)

            load(w_l0a[:, :, 0:D], kpn(a["L0_gnn_W1"]))
            load(w_l0b[:, :, 0:D], kpn(a["L0_gnn_W2"]))
            load(w_l2[:, :, 0:D], kpn(a["L2_gnn_W"]))
            for i, name in enumerate(["L0_gnn_att_src1", "L0_gnn_att_dst1", "L0_gnn_att_src2", "L0_gnn_att_dst2",
                                      "L2_gnn_att_src", "L2_gnn_att_dst"]):
                load(attv[i], a[name].rearrange("h c -> (h c)").partition_broadcast(128))
            load(b1_l0a[:], a["L0_gnn_b1"].rearrange("(k p) -> p k", p=128), allow_slow_non_contiguous=True)

            act.nop().then_inc(S("acc_free"), 2)
            act.nop().then_inc(S("counts_free"), 2)

            def evac_acc(s):
                return nc.scalar.activation(accs[s], halves((psA, psB)[s]), ACT.Copy)

            def turned(tag, bias=None):
                act.wait_ge(*reached(tag + "_turned0", 1))
                if bias is None:
                    nc.scalar.activation(cols(xT[:, 0, :]), psA[:, 0:NT, 0:P], ACT.Copy).then_inc(S(tag + "_xT0"), 1)
                else:
                    nc.scalar.activation(cols(xT[:, 0, :]), psA[:, 0:NT, 0:P], ACT.Relu, bias=bias[:, 0:1])\
                        .then_inc(S(tag + "_xT0"), 1)
                    act.wait_ge(*reached(tag + "_turned1", 1))
                    nc.scalar.activation(cols(xT[:, 1, :]), psB[:, 0:NT, 0:P], ACT.Relu, bias=bias[:, 1:2])\
                        .then_inc(S(tag + "_xT1"), 1)

            def projected(tag, heads):
                ch = D // heads
                act.wait_ge(*reached(tag + "_ones", 1))
                for j in range(NT):
                    act.wait_ge(*reached(tag + "_proj", j + 1))
                    nc.scalar.activation(al[:, j, 0:2 * heads], (psC, psD)[j % 2][0:P, D:D + 2 * heads], ACT.Copy)\
                        .then_inc(S(tag + "_al"), 1)
                    nc.scalar.activation(hs[:, j, 0:heads * (ch + 1)].rearrange("p (h c) -> p h c", h=heads)[:, :, 0:ch],
                                         (psC, psD)[j % 2][0:P, 0:D].rearrange("p (h c) -> p h c", h=heads),
                                         ACT.Copy).then_inc(S(tag + "_hs"), 1)

            turned("l0g")

            def counts_out(i, q):
                b = 2 * i + q - 1
                act.wait_ge(*reached("block_ready", b + 1))
                ps = (psC, psD)[(q + 1) % 2][0:P, 0:NT * 2 * WB].rearrange("p (j c) -> p j c", c=2 * WB)
                nc.scalar.activation(ct[:, :, bass.ds(b * WB, WB)], ps[:, :, 0:WB], ACT.Copy)
                nc.scalar.activation(at[:, :, bass.ds(b * WB, WB)], ps[:, :, 0:WB], ACT.Copy,
                                     accum_out=cnt[:, bass.ds(b, 1)])
                nc.scalar.activation(wt[:, :, bass.ds(b * WB, WB)], ps[:, :, WB:], ACT.Copy)\
                    .then_inc(S("counts_free"), 1)

            def acc_out(n, q):
                act.wait_ge(*reached("acc_ready", n + 1))
                evac_acc(q).then_inc(S("acc_free"), 1)

            acc_out(0, 0)
            acc_out(1, 1)
            projected("l0a", 4)
            counts_out(0, 1)
            with act.Fori(1, NBLK // 2) as i:
                for q in range(2):
                    acc_out(2 * i + q, q)
                    counts_out(i, q)
            counts_out(NBLK // 2, 0)
            act.wait_ge(*reached("params_acc", 1))
            nc.scalar.activation(b1T0[:], psA[:, 0, 0:64].rearrange("p (f e) -> p f e", e=E0), ACT.Copy)
            nc.scalar.activation(b1T1[:], psC[:, 0:256].rearrange("p (f e) -> p f e", e=E1), ACT.Copy)
            nc.scalar.activation(b2T1[:], psD[:, 0:128].rearrange("p (f e) -> p f e", e=E1), ACT.Copy)
            nc.scalar.activation(b1T3[:], psF[:, 16:32].rearrange("p (f e) -> p f e", e=E2), ACT.Copy)
            nc.scalar.activation(gate3[:], psF[:, 0:16].rearrange("p (f e) -> p f e", e=E2), ACT.Copy)
            nc.scalar.activation(bnT[:].rearrange("p w f e -> p (w f e)"),
                                 psB[:].rearrange("p a b -> p (a b)")[:, 0:10 * KD * E2], ACT.Copy)\
                .then_inc(S("params_turned"), 1)

            act.wait_ge(*reached("flag_ready", 1))
            missed = act.value_load(flag_i[0:1, 0:1], min_val=0, max_val=1)
            with act.If(missed == 1):
                with act.Fori(0, NBLK) as b:
                    with act.Fori(0, NCHUNK) as c:
                        act.wait_ge(*reached("all_acc", b * NCHUNK + c + 1))
                        evac_acc(0).then_inc(S("all_acc_out"), 1)
            with act.Else():
                act.nop()
            act.nop()

            def attention(tag, heads):
                act.wait_ge(*reached(tag + "_rows", 1))
                for h in range(heads):
                    act.wait_ge(*reached(tag + "_r1", h + 1))
                    for i in range(NT):
                        if h >= 2:
                            act.wait_ge(*reached(tag + "_agg", (h - 2) * NT + i + 1))
                        nc.scalar.activation(cols(u[h % 2][:, i, :]), psA[0:P, 0:NT, 0:P], ACT.Exp,
                                             bias=al[:, i, h:h + 1]).then_inc(S(tag + "_u"), 1)
                    act.wait_ge(*reached(tag + "_r2", h + 1))
                    for i in range(NT):
                        if h >= 1:
                            act.wait_ge(*reached(tag + "_max", (h - 1) * NT + i + 1))
                        nc.scalar.activation(cols(v[:, i, :]), psB[0:P, 0:NT, 0:P], ACT.Exp,
                                             bias=al2[:, i, h:h + 1]).then_inc(S(tag + "_v"), 1)

            attention("l0a", 4)
            turned("l0m", b1_l0a)
            projected("l0b", 1)
            attention("l0b", 1)
            turned("l0f")
            act.wait_ge(*reached("shift0_ready", 1))
            nc.scalar.activation(ex8, lg8, ACT.Exp).then_inc(S("exp0_ready"), 1)
            act.wait_ge(*reached("bufs_turned0", 1))
            nc.scalar.activation(bufT[:, 0, :].rearrange("p (e c) -> p e c", e=E0), psA[:, :, 0:CAP], ACT.Copy)\
                .then_inc(S("bufT0"), 1)
            with act.Fori(0, E0 // 4) as r:
                for q in range(4):
                    e = 4 * r + q
                    for f in range(F0 // 128):
                        act.wait_ge(*reached("l0_hidden", e * (F0 // 256) + f // 2 + 1))
                        if f == 0:
                            act.wait_ge(*reached("l0_y_free", e + 1))
                        nc.scalar.activation(h0[q % 2][:, f, :], hidden0(f), ACT.Relu, bias=b1T0[:, f, bass.ds(e, 1)])\
                            .then_inc(S("l0_relu"), 1)
            turned("l1g")
            for j in range(NT):
                act.wait_ge(*reached("gcn_proj", j + 1))
                if j == 0:
                    act.wait_ge(*reached("norms_ready", 1))
                nc.scalar.activation(hs[:, j, 0:64], (psC, psD)[j % 2][0:P, 0:64], ACT.Copy,
                                     scale=nsrc[:, j:j + 1]).then_inc(S("gcn_hs"), 1)
            act.wait_ge(*reached("gcn_scaled", 1))
            nc.scalar.activation(hT, scaled, ACT.Relu, bias=b_gcn[:, 0:1])\
                .then_inc(S("gcn_hT"), 1)
            turned("l1f")
            act.wait_ge(*reached("shift1_ready", 1))
            nc.scalar.activation(gsel[:, :, 1], gsel[:, :, 0], ACT.Exp).then_inc(S("exp1_ready"), 1)
            for g in range(2):
                act.wait_ge(*reached("xs_turned", 2 * g + 1))
                nc.scalar.activation(xsT[:, 0, g * N:(g + 1) * N].rearrange("p (j q) -> p j q", q=P),
                                     psA[:, 0:NT, 0:P], ACT.Copy).then_inc(S("xsT_act"), 1)
            act.wait_ge(*reached("flag2_ready", 1))
            full = act.value_load(flag2_i[0:1, 0:1], min_val=0, max_val=1)

            def hidden1(f, e, q):
                return nc.scalar.activation(h1[q][:, f, :], hidden1_ps(f), ACT.Relu,
                                            bias=b1T1[:, f, bass.ds(e, 1)])

            nf = F1 // 128
            with act.If(full == 1):
                with act.Fori(0, E1) as e:
                    with act.Fori(0, ROUNDS) as r:
                        for f in range(nf):
                            act.wait_ge(*reached("any_hidden", (e * ROUNDS + r) * nf + f + 1))
                            hidden1(f, e, 0).then_inc(S("any_relu"), 1)
            with act.Else():
                with act.Fori(0, E1 // RING) as r:
                    for q in range(RING):
                        for f in range(nf):
                            act.wait_ge(*reached("l1_hidden", (RING * r + q) * nf + f + 1))
                            if f == 0:
                                act.wait_ge(*reached("l1_used", RING * r + q + 1))
                            hidden1(f, RING * r + q, q % 2).then_inc(S("l1_relu"), 1)
            act.nop()
            for g in (0, 2, 4):
                act.wait_ge(*reached("ys_turned", g + 1))
                nc.scalar.activation(xs[:, 2 * g:2 * g + 2, :].rearrange("p t (m d) -> p (t m) d", m=2),
                                     psA[0:P, 0:4, 0:128], ACT.Copy).then_inc(S("ys_act"), 1)
            turned("l2g")
            projected("l2a", 4)
            attention("l2a", 4)

            def dense(tag, func):
                turned(tag)
                act.wait_ge(*reached(tag + "_shift", 1))
                act.wait_ge(*reached("bn_ready", 1))
                nc.scalar.activation(ex8, lg8, ACT.Exp).then_inc(S(tag + "_exp"), 1)
                layers = 2 if tag == "l2f" else 1
                act.nop().then_inc(S(tag + "_act"), 2)
                with act.Fori(0, 2) as r:
                    for t in range(2):
                        for layer in range(layers):
                            for q in range(2):
                                e = 4 * r + 2 * t + q
                                for m in range(KD):
                                    n = (((2 * r + t) * layers + layer) * 2 + q) * KD + m
                                    act.wait_ge(*reached(tag + "_hidden", n + 1))
                                    o = cols((h1d, h2d)[layer][q][:, m, :])
                                    i_ = (psA, psB)[m][:, 0:NT, 0:P]
                                    if tag == "l2f":
                                        ins = nc.scalar.activation(o, i_, func, bias=bnT[:, 5 * layer + 2, m, bass.ds(e, 1)],
                                                                   scale=bnT[:, 5 * layer + 1, m, bass.ds(e, 1)])
                                    else:
                                        ins = nc.scalar.activation(o, i_, func, bias=b1T3[:, m, bass.ds(e, 1)])
                                    ins.then_inc(S(tag + "_act"), 1)

            dense("l2f", ACT.Relu)
            turned("l3g")
            for j in range(NT):
                act.wait_ge(*reached("l3_proj", j + 1))
                nc.scalar.activation(hs[:, j, 0:D], (psC, psD)[j % 2][0:P, 0:D], ACT.Copy)\
                    .then_inc(S("l3_hs"), 1)
            dense("l3f", ACT.Gelu)

        @block.tensor
        def _(pe):
            pe.wait_ge(*reached("consts_ready", 1))
            pe.wait_ge(*reached("cnt_ready", NBLK - 1))
            nc.tensor.matmul(psE[0:1, 0:NBLK], ones_f[0:P, 0:1], cnt, start=True, stop=True).then_inc(S("base_sum"), 1)
            def turn(tag, src_sem, src, by_tile=True):
                for j in range(NT):
                    if j == 0 or by_tile:
                        pe.wait_ge(*reached(src_sem, j + 1))
                    for k in range(KD):
                        ins = nc.tensor.transpose((psA, psB)[k][:, j, 0:P], src[:, j, k * 128:(k + 1) * 128],
                                                  ident[0:P, 0:P])
                        if j == NT - 1:
                            ins.then_inc(S(f"{tag}_turned{k}"), 1)

            turn("l0g", "l0g_xln", xln)
            def project(tag, xtag, w, width, sem_out, sem_in):
                pe.wait_ge(*reached(xtag + "_xT0", 1))
                pe.wait_ge(*reached(xtag + "_xT1", 1))
                for j in range(NT):
                    if j >= 2:
                        for s_ in sem_in:
                            pe.wait_ge(*reached(s_, j - 1))
                    for k in range(KD):
                        ins = nc.tensor.matmul((psC, psD)[j % 2][0:P, 0:width], xT[:, k, j * P:(j + 1) * P],
                                               w[:, k, 0:width],
                                               start=(k == 0), stop=(k == KD - 1))
                    ins.then_inc(S(sem_out), 1)

            def accumulate(s, n):
                acc = halves((psA, psB)[s])
                for t in range(n):
                    w = ohd[s][:, t].rearrange("p k d -> p (k d)")
                    for h in range(2):
                        ins = nc.tensor.matmul(acc[:, h], w, ohs[s][:, t, h * HN:(h + 1) * HN],
                                               start=(t == 0), stop=(t == n - 1))
                return ins

            def split(s, ps):
                acc = accs[s].rearrange("p h n -> p (h n)")
                for j in range(NT):
                    ins = nc.tensor.matmul(ps[0:P, j * 2 * WB:(j + 1) * 2 * WB], acc[:, j * P:(j + 1) * P], sel[:],
                                           start=True, stop=True)
                return ins

            def gather_block(b, q):
                pe.wait_ge(*reached("kinds_ready", b + 1))
                pe.wait_ge(*reached("ohs_ready", b + 1))
                pe.wait_ge(*reached("acc_free", b + 1))
                accumulate(q, CH).then_inc(S("acc_ready"), 1)

            def split_block(b, q):
                pe.wait_ge(*reached("acc_free", b + 3))
                pe.wait_ge(*reached("counts_free", b + 1))
                split(q, (psC, psD)[q]).then_inc(S("block_ready"), 1)

            pe.wait_ge(*reached("l0g_xT0", 1))
            pe.wait_ge(*reached("l0g_xT1", 1))
            gather_block(0, 0)
            gather_block(1, 1)
            pe.wait_ge(*reached("l0a_folded", 1))
            project("l0a", "l0g", w_l0a, D + 8, "l0a_proj", ["l0a_hs", "l0a_al"])
            pe.wait_ge(*reached("l0a_al", NT))
            pe.wait_ge(*reached("l0a_hs", NT))
            split_block(0, 0)
            with pe.Fori(1, NBLK // 2) as i:
                gather_block(2 * i, 0)
                split_block(2 * i - 1, 1)
                gather_block(2 * i + 1, 1)
                split_block(2 * i, 0)
            split_block(NBLK - 1, 1)

            pe.wait_ge(*reached("counts_free", NBLK + 2))
            nc.tensor.matmul(psE[0:1, 0:NBLK], ones_f[0:P, 0:1], cnt, start=True, stop=True).then_inc(S("total_sum"), 1)
            pe.wait_ge(*reached("params_loaded", 16 * PARAMS))
            pe.wait_ge(*reached("acc_free", NBLK + 2))
            pe.wait_ge(*reached("counts_free", NBLK + 2))
            for f in range(F0 // 128):
                nc.tensor.transpose(psA[:, 0, f * E0:(f + 1) * E0], b1r0[:, f * 128:(f + 1) * 128], ident[0:E0, 0:E0])
            for f in range(F1 // 128):
                nc.tensor.transpose(psC[:, f * E1:(f + 1) * E1], b1r1[:, f * 128:(f + 1) * 128], ident[0:E1, 0:E1])
            for k in range(KD):
                nc.tensor.transpose(psD[:, k * E1:(k + 1) * E1], b2r1[:, k * 128:(k + 1) * 128], ident[0:E1, 0:E1])
                nc.tensor.transpose(psF[:, (KD + k) * E2:(KD + k + 1) * E2], b1r3[:, k * 128:(k + 1) * 128],
                                    ident[0:E2, 0:E2])
                nc.tensor.transpose(psF[:, k * E2:(k + 1) * E2], rw3[:, k * 128:(k + 1) * 128], ident[0:E2, 0:E2])
            for n, t in enumerate(bnp):
                for k in range(KD):
                    c = (n * KD + k) * E2
                    ins = nc.tensor.transpose(psB[:].rearrange("p a b -> p (a b)")[:, c:c + E2],
                                              t[:, k * 128:(k + 1) * 128], ident[0:E2, 0:E2])
            ins.then_inc(S("params_acc"), 1)
            pe.wait_ge(*reached("flag_ready", 1))
            pe.wait_ge(*reached("params_turned", 1))
            missed = pe.value_load(flag_i[0:1, 0:1], min_val=0, max_val=1)
            with pe.If(missed == 1):
                with pe.Fori(0, NBLK) as b:
                    with pe.Fori(0, NCHUNK) as c:
                        n = b * NCHUNK + c
                        pe.wait_ge(*reached("all_kinds", n + 1))
                        pe.wait_ge(*reached("all_ohs", n + 1))
                        accumulate(0, CHA).then_inc(S("all_acc"), 1)
                        pe.wait_ge(*reached("all_acc_out", n + 1))
                        split(0, psC).then_inc(S("all_split"), 1)
            with pe.Else():
                pe.nop()
            pe.nop()

            def row(ps, col):
                for j in range(NT):
                    ins = nc.tensor.transpose(ps[0:P, j, 0:P], col(j).to_broadcast([P, P]), ident[0:P, 0:P])
                return ins

            def attention(tag, heads):
                def sources(h):
                    if h >= 1:
                        pe.wait_ge(*reached(tag + "_masked", h * NT))
                    row(psEF, lambda j: al[:, j, h:h + 1]).then_inc(S(tag + "_bc"), 1)

                def rows(h):
                    pe.wait_ge(*reached(tag + "_rows", h + 1))
                    if h >= 1:
                        pe.wait_ge(*reached(tag + "_u", h * NT))
                    row(psA, lambda j: r1[:, j, h:h + 1]).then_inc(S(tag + "_r1"), 1)
                    if h >= 1:
                        pe.wait_ge(*reached(tag + "_v", h * NT))
                    row(psB, lambda j: r2[:, j, h:h + 1]).then_inc(S(tag + "_r2"), 1)

                pe.wait_ge(*reached(tag + "_al", NT))
                for h in range(min(heads, 2)):
                    sources(h)
                pe.wait_ge(*reached(tag + "_hs", NT))
                rows(0)
                if heads == 1:
                    for i in range(NT):
                        pe.wait_ge(*reached(tag + "_p", i + 1))
                        for j in range(NT - 1):
                            ins = nc.tensor.matmul((psC, psD, psE, psF)[j][0:P, 0:D + 1], u[0][:, i, j * P:(j + 1) * P],
                                                   hs[:, i, 0:D + 1], start=(i == 0), stop=(i == NT - 1))
                        ins.then_inc(S(tag + "_agg"), 1)
                    for i in range(NT):
                        ins = nc.tensor.matmul(last_out, u[0][:, i, (NT - 1) * P:], hs[:, i, 0:D + 1],
                                               start=(i == 0), stop=(i == NT - 1))
                    ins.then_inc(S(tag + "_agg"), 1)
                    return
                for h in range(heads):
                    if h + 2 < heads:
                        sources(h + 2)
                    if h + 1 < heads:
                        rows(h + 1)
                    if h >= 2:
                        pe.wait_ge(*reached(tag + "_out", h - 1))
                    for i in range(NT):
                        pe.wait_ge(*reached(tag + "_p", h * NT + i + 1))
                        for j in range(NT):
                            ins = nc.tensor.matmul((psC, psD)[h % 2][0:P, j * 65:(j + 1) * 65],
                                                   u[h % 2][:, i, j * P:(j + 1) * P], hs[:, i, h * 65:(h + 1) * 65],
                                                   start=(i == 0 and j == 0), stop=(i == NT - 1 and j == NT - 1))
                        ins.then_inc(S(tag + "_agg"), 1)

            pe.wait_ge(*reached("at_ready", 1))
            for j in range(NT):
                if j >= 2:
                    pe.wait_ge(*reached("negm_done", j - 1))
                for i in range(NT):
                    ins = nc.tensor.transpose((psA, psB)[j % 2][0:P, i, 0:P], at[:, i, j * P:(j + 1) * P], ident[0:P, 0:P])
                ins.then_inc(S("at_turned"), 1)
            pe.wait_ge(*reached("negm_done", NT))

            attention("l0a", 4)
            turn("l0m", "l0a_done", gat, False)
            pe.wait_ge(*reached("l0b_folded", 1))
            project("l0b", "l0m", w_l0b, D + 2, "l0b_proj", ["l0b_hs", "l0b_al"])
            attention("l0b", 1)

            def logits(tag, gate, ne):
                pe.wait_ge(*reached(tag + "_xT0", 1))
                pe.wait_ge(*reached(tag + "_xT1", 1))
                for j in range(NT):
                    o = psC[0:P, j * ne:(j + 1) * ne]
                    for k in range(KD):
                        ins = nc.tensor.matmul(o, xT[:, k, j * P:(j + 1) * P], gate[:, k, :], start=(k == 0),
                                               stop=(k == KD - 1))
                ins.then_inc(S(tag + "_logits"), 1)

            def ranks(tag, ohb, ne):
                pe.wait_ge(*reached(tag + "_onehot", 1))
                for j in range(NT):
                    o = psD[0:P, j * ne:(j + 1) * ne]
                    for i in range(j + 1):
                        ins = nc.tensor.matmul(o, tri_b if i == j else ones_bf, ohb[:, i, :], start=(i == 0), stop=(i == j))
                return ins

            def expert_bias(tag, wsem, wsrc, brow):
                pe.wait_ge(*reached(wsem, 1))
                if tag != "l0f":
                    pe.wait_ge(*reached(tag + "_brow_loaded", 16))
                for j in range(NT):
                    ins = nc.tensor.transpose(psEF[0:8, j, 0:P], wsrc[:, j, :], ident[0:P, 0:P])
                ins.then_inc(S(tag + "_wturned"), 1)
                pe.wait_ge(*reached(tag + "_wT", 1))
                for j in range(NT):
                    if j >= 2:
                        pe.wait_ge(*reached(tag + "_bias_out", j - 1))
                    nc.tensor.matmul((psE, psF)[j % 2][0:P, 0:D], wgT[:, j * P:(j + 1) * P], brow[:], start=True, stop=True)\
                        .then_inc(S(tag + "_bias"), 1)

            turn("l0f", "l0f_xln", xln)
            logits("l0f", gate0, E0)
            ranks("l0f", ohb0, E0).then_inc(S("l0_ranks"), 1)
            pe.wait_ge(*reached("slots0_ready", 1))
            expert_bias("l0f", "l0f_onehot", oh0, brow)
            pe.wait_ge(*reached("bufs_loaded", 16))
            for k in range(KD):
                for e in range(E0):
                    ins = nc.tensor.transpose((psA, psB)[k][:, e, 0:CAP], bufs[:, e, k * 128:(k + 1) * 128],
                                              ident[0:CAP, 0:CAP])
                ins.then_inc(S(f"bufs_turned{k}"), 1)
            pe.wait_ge(*reached("bufT0", 1))
            pe.wait_ge(*reached("bufT1", 1))
            nf = F0 // 128

            def hidden_of(r, q):
                e = 4 * r + q
                w1 = slot(2 * q).rearrange("p (k n) -> p k n", k=KD)
                pe.wait_ge(*reached(f"l0_weights{2 * q}", 16 * r + 16))
                for f in range(nf):
                    if f % 2 == 0:
                        pe.wait_ge(*reached("l0_relu", e * nf + f + 2))
                    for k in range(KD):
                        ins = nc.tensor.matmul(hidden0(f), w1[:, k, f * 128:(f + 1) * 128],
                                               bufT[:, k, bass.ds(e * CAP, CAP)], start=(k == 0), stop=(k == KD - 1))
                    if f % 2:
                        ins.then_inc(S("l0_hidden"), 1)

            def out_of(r, q):
                e = 4 * r + q
                w2 = slot(2 * q + 1).rearrange("p (k n) -> p k n", k=nf)
                pe.wait_ge(*reached(f"l0_weights{2 * q + 1}", 16 * r + 16))
                pe.wait_ge(*reached("l0_y_free", e + 1))
                for f in range(nf):
                    pe.wait_ge(*reached("l0_relu", (e + 1) * nf + f + 1))
                    ins = nc.tensor.matmul((psC, psD)[q % 2][0:CAP, 0:D], h0[q % 2][:, f, :], w2[:, f, :],
                                           start=(f == 0), stop=(f == nf - 1))
                ins.then_inc(S("l0_y"), 1)

            hidden_of(0, 0)
            with pe.Fori(0, E0 // 4 - 1) as r:
                for q in range(4):
                    hidden_of(*((r, q + 1) if q < 3 else (r + 1, 0)))
                    out_of(r, q)
            for q in range(4):
                if q < 3:
                    hidden_of(E0 // 4 - 1, q + 1)
                out_of(E0 // 4 - 1, q)
            for j in range(NT):
                for i in range(NT):
                    ins = nc.tensor.matmul(psE[0:P, j:j + 1], ct[:, i, j * P:(j + 1) * P], ones_f[0:P, 0:1],
                                           start=(i == 0), stop=(i == NT - 1))
            ins.then_inc(S("indeg_sum"), 1)
            pe.wait_ge(*reached("norms_ready", 1))
            row(psEF, lambda j: ndst[:, j:j + 1]).then_inc(S("ndst_turned"), 1)
            turn("l1g", "l1g_xln", xln)
            project("gcn", "l1g", w_gcn, 64, "gcn_proj", ["gcn_hs"])
            pe.wait_ge(*reached("gcn_hs", NT))
            for i in range(NT):
                nc.tensor.matmul(psA[0:64, 0:4, 0:P], hs[:, i, 0:64], cols(ct[:, i, 0:4 * P]),
                                 start=(i == 0), stop=(i == NT - 1))
                ins = nc.tensor.matmul(psA[0:64, 4, 0:P], hs[:, i, 0:64], ct[:, i, 4 * P:N],
                                       start=(i == 0), stop=(i == NT - 1))
            ins.then_inc(S("gcn_agg"), 1)
            pe.wait_ge(*reached("gcn_hT", 1))
            for j in range(NT):
                if j >= 2:
                    pe.wait_ge(*reached("gcn_out", j - 1))
                nc.tensor.matmul((psC, psD)[j % 2][0:P, 0:D], hT[:, j * P:(j + 1) * P], w_out[:], start=True, stop=True)\
                    .then_inc(S("gcn_y"), 1)
            turn("l1f", "l1f_xln", xln)
            logits("l1f", gate1, E1)
            ranks("l1f", ohb1, E1)
            for i in range(NT):
                ins = nc.tensor.matmul(psE[0:P, 0:E1], ones_bf, ohb1[:, i, :], start=(i == 0), stop=(i == NT - 1))
            for i in range(NT):
                ins = nc.tensor.matmul(psF[0:E1, 0:1], ohb1[:, i, :], ones_bf[:, 0:1], start=(i == 0), stop=(i == NT - 1))
            ins.then_inc(S("l1_ranks"), 1)
            pe.wait_ge(*reached("cntcol_ready", 1))
            nc.tensor.matmul(psC[0:P, 0:E1], cntcol.to_broadcast([E1, P]), strict, start=True, stop=True)\
                .then_inc(S("l1_offsets"), 1)
            pe.wait_ge(*reached("xs_loaded", 16))
            for g in range(4):
                k, half = g % 2, g // 2
                if half:
                    pe.wait_ge(*reached("xsT_act" if k == 0 else "xsT_dve", 1))
                for j in range(NT):
                    ins = nc.tensor.transpose((psA, psB)[k][:, j, 0:P], xs[:, half * NT + j, k * 128:(k + 1) * 128],
                                              ident[0:P, 0:P])
                ins.then_inc(S("xs_turned"), 1)
            pe.wait_ge(*reached("xsT_act", 2))
            pe.wait_ge(*reached("xsT_dve", 2))
            pe.wait_ge(*reached("flag2_ready", 1))
            full = pe.value_load(flag2_i[0:1, 0:1], min_val=0, max_val=1)
            nf = F1 // 128

            def hidden1(s, f, start):
                w1 = slot(s)[:, 0:CHUNK // 2].rearrange("p (k n) -> p k n", k=KD)
                for k in range(KD):
                    ins = nc.tensor.matmul(hidden1_ps(f), w1[:, k, f * 128:(f + 1) * 128],
                                           xsT[:, k, bass.ds(start, WIN)], start=(k == 0), stop=(k == KD - 1))
                return ins

            def out1(s, ps, h, wait):
                w2 = slot(s)[:, CHUNK // 2:].rearrange("p (k n) -> p k n", k=nf)
                for m in range(KD):
                    for f in range(nf):
                        if m == 0:
                            wait(f)
                        ins = nc.tensor.matmul(ps[:, m, 0:WIN], w2[:, f, m * 128:(m + 1) * 128], h[:, f, :],
                                               start=(f == 0), stop=(f == nf - 1))
                return ins

            with pe.If(full == 1):
                with pe.Fori(0, E1) as e:
                    with pe.Fori(0, ROUNDS) as r:
                        n = e * ROUNDS + r
                        pe.wait_ge(*reached("any_expert_loaded", 32 * e + 32))
                        start = pe.value_load(starts[0:1, bass.ds(e, 1), bass.ds(r, 1)].rearrange("p a b -> p (a b)"),
                                              min_val=0, max_val=SLOTS)
                        for f in range(nf):
                            hidden1(0, f, start).then_inc(S("any_hidden"), 1)
                        pe.wait_ge(*reached("any_y_free", n + 1))
                        out1(0, psA, h1[0], lambda f: pe.wait_ge(*reached("any_relu", n * nf + f + 1))).then_inc(S("any_y"), 1)
            with pe.Else():
                def hidden_of(r, q):
                    e = r * RING + q
                    start = pe.value_load(starts[0:1, bass.ds(e, 1), 0:1].rearrange("p a b -> p (a b)"),
                                          min_val=0, max_val=SLOTS)
                    pe.wait_ge(*reached(f"l1_weights{q}", 32 * r + 32))
                    for f in range(nf):
                        pe.wait_ge(*reached("l1_relu", e * nf + f + 1))
                        hidden1(q, f, start).then_inc(S("l1_hidden"), 1)

                def out_of(r, q):
                    e = r * RING + q
                    pe.wait_ge(*reached("l1_y_free", e + 1))
                    out1(q, (psA, psB)[q % 2], h1[q % 2],
                         lambda f: pe.wait_ge(*reached("l1_relu", (e + 1) * nf + f + 1))).then_inc(S("l1_used"), 1)

                hidden_of(0, 0)
                with pe.Fori(0, E1 // RING - 1) as r:
                    for q in range(RING):
                        hidden_of(*((r, q + 1) if q + 1 < RING else (r + 1, 0)))
                        out_of(r, q)
                for q in range(RING):
                    if q + 1 < RING:
                        hidden_of(E1 // RING - 1, q + 1)
                    out_of(E1 // RING - 1, q)
            pe.nop()
            pe.wait_ge(*reached("yT_ready", 1))
            for g in range(5):
                if g >= 2:
                    pe.wait_ge(*reached("ys_dve" if g % 2 else "ys_act", g // 2))
                for t in range(2):
                    for m in range(KD):
                        c = (2 * g + t) * P
                        ins = nc.tensor.transpose((psA, psB)[g % 2][0:P, t * KD + m, :], yT[:, m, c:c + P], ident[:])
                ins.then_inc(S("ys_turned"), 1)
            turn("l2g", "l2g_xln", xln)
            project("l2a", "l2g", w_l2, D + 8, "l2a_proj", ["l2a_hs", "l2a_al"])
            attention("l2a", 4)

            def dense(tag, gate, layers):
                turn(tag, tag + "_xln", xln)
                logits(tag, gate, E2)
                pe.wait_ge(*reached(tag + "_y_free", 2))
                slots = DENSE[tag][1]
                with pe.Fori(0, 2) as r:
                    for t in range(2):
                        p = 2 * r + t
                        for q in range(2):
                            pe.wait_ge(*reached(f"{tag}_weights{2 * t + q}", 16 * (layers + 1) * (r + 1)))
                        for layer in range(layers):
                            for q in range(2):
                                w = slot(slots[2 * t + q])[:, layer * KD * D:(layer + 1) * KD * D]\
                                    .rearrange("p (k n) -> p k n", k=KD)
                                src = xT if layer == 0 else h1d[q]
                                n = (p * layers + layer) * 2 + q
                                if layer:
                                    pe.wait_ge(*reached(tag + "_act", (p * layers * 2 + q + 1) * KD + 2))
                                for m in range(KD):
                                    ps = (psA, psB)[m]
                                    pe.wait_ge(*reached(tag + "_act", n * KD + m + 1))
                                    for k in range(KD):
                                        wk_ = w[:, k, m * 128:(m + 1) * 128]
                                        nc.tensor.matmul(ps[:, 0:4, 0:P], wk_, cols(src[:, k, 0:4 * P]),
                                                         start=(k == 0), stop=(k == KD - 1))
                                        ins = nc.tensor.matmul(ps[:, 4, 0:P], wk_, src[:, k, 4 * P:N],
                                                               start=(k == 0), stop=(k == KD - 1))
                                    ins.then_inc(S(tag + "_hidden"), 1)
                        for q in range(2):
                            hsrc = (h1d, h2d)[layers - 1][q]
                            w = slot(slots[2 * t + q])[:, layers * KD * D:(layers + 1) * KD * D]\
                                .rearrange("p (k n) -> p k n", k=KD)
                            pe.wait_ge(*reached(tag + "_act", ((p * layers + layers - 1) * 2 + q + 1) * KD + 2))
                            for j in range(NT):
                                pe.wait_ge(*reached(tag + "_y_free", (2 * p + q) * NT + j + 1))
                                for k in range(KD):
                                    ins = nc.tensor.matmul(((psC, psD)[(q * NT + j) % 2])[0:P, 0:D],
                                                           hsrc[:, k, j * P:(j + 1) * P], w[:, k, :],
                                                           start=(k == 0), stop=(k == KD - 1))
                                ins.then_inc(S(tag + "_y"), 1)
                expert_bias(tag, tag + "_w", wgt, brow)

            dense("l2f", gate2, 2)
            turn("l3g", "l3g_xln", xln)
            pe.wait_ge(*reached("w_l3_loaded", 16))
            project("l3", "l3g", w_l3, D, "l3_proj", ["l3_hs"])
            pe.wait_ge(*reached("l3_hs", NT))
            for j in range(NT):
                if j >= 2:
                    pe.wait_ge(*reached("l3_out", j - 1))
                for i in range(NT):
                    ins = nc.tensor.matmul((psC, psD)[j % 2][0:P, 0:D], wt[:, i, j * P:(j + 1) * P], hs[:, i, 0:D],
                                           start=(i == 0), stop=(i == NT - 1))
                ins.then_inc(S("l3_agg"), 1)
            dense("l3f", gate3, 1)

        @block.vector
        def _(dve):
            V = nc.vector
            st = Steps(S("dve_steps"))

            def step(ins):
                st.done(ins)
                st.wait(dve)

            V.nop().then_inc(S("all_added"), 1)
            dve.wait_ge(*reached("dst_loaded", 16))
            V.memset(cnt, 0.0)
            V.tensor_copy(pack[:, :, 1], dst_i)
            step(V.tensor_copy(dst_h[:, 0:EPP], dst_i))
            for b in range(1, NBLK):
                ins = V.tensor_scalar(junk_e[:, 0:EPP], dst_h[:, 0:EPP], float(b * WB), 0.0, ALU.is_lt,
                                      ALU.add, accum_out=cnt[:, b:b + 1])
                ins.then_inc(S("cnt_ready"), 1)
                dve.wait_ge(*reached("cnt_ready", b))
            dve.wait_ge(*reached("edges_loaded", 32))
            V.tensor_copy(pack[:, :, 0], src_i)
            step(V.tensor_copy(bf_part[:, 0:EPP], ew))
            step(V.tensor_copy(pack[:, :, 2], bf_part[:, 0:EPP]))
            step(V.tensor_tensor(res, ew, pack[:, :, 2], ALU.subtract))
            step(V.tensor_copy(bf_part[:, 0:EPP], res))
            step(V.tensor_copy(pack[:, :, 3], bf_part[:, 0:EPP]))
            V.tensor_tensor(pack[:, :, 4], res, pack[:, :, 3], ALU.subtract).then_inc(S("pack_ready"), 1)
            dve.wait_ge(*reached("base_sum", 1))
            step(V.tensor_scalar(basef, psE[0:1, 0:NBLK], float(E - CHE), None, ALU.min))
            V.tensor_copy(base_i, basef).then_inc(S("base_ready"), 1)
            dve.wait_ge(*reached("iota_ready", 1))
            step(V.tensor_copy(iota_f[:], iota_i[:]))
            V.tensor_copy(iota_h, iota_f[:])
            dve.wait_ge(*reached("consts_ready", 1))
            V.tensor_copy(tri_b, tri_f)
            step(V.tensor_copy(tokid, tok_i))
            def stats(j, src):
                return V.bn_stats(st6[:, j, :], src[:, j, :])

            def normalise(tag, src, dst, sem, stats_made=False):
                if not stats_made:
                    for j in range(NT):
                        ins = stats(j, src)
                    step(ins)
                for j in range(NT):
                    ins = V.bn_aggr(mv[:, j, :], st6[:, j, :])
                step(ins)
                V.tensor_scalar(vare, mv[:, :, 1], LN_EPS, None, ALU.add).then_inc(S(tag + "_var"), 1)
                dve.wait_ge(*reached(tag + "_rstd", 1))
                for j in range(NT):
                    V.tensor_scalar(dst[:, j, :], src[:, j, :], mv[:, j, 0:1], rstd[:, j:j + 1],
                                    ALU.subtract, ALU.mult).then_inc(S(sem), 1)

            def turned(tag):
                dve.wait_ge(*reached(tag + "_turned1", 1))
                V.tensor_copy(cols(xT[:, 1, :]), psB[:, 0:NT, 0:P]).then_inc(S(tag + "_xT1"), 1)

            dve.wait_ge(*reached("x_loaded", 16))
            normalise("l0g", x, xln, "l0g_xln")
            def ones(tag, heads):
                ch = D // heads
                V.memset(hs[:, :, 0:heads * (ch + 1)].rearrange("p j (h c) -> p j h c", h=heads)[:, :, :, ch:ch + 1], 1.0)\
                    .then_inc(S(tag + "_ones"), 1)


            def fold(w, heads, v0):
                for n in range(2):
                    step(V.tensor_tensor(attm, w[:, :, 0:D], attv[v0 + n].unsqueeze(1).to_broadcast([128, KD, D]), ALU.mult))
                    step(V.tensor_reduce(w[:, :, D + n * heads:D + (n + 1) * heads],
                                         attm.rearrange("p k (h c) -> p k h c", h=heads), AX, ALU.add))

            turned("l0g")

            def onehots(s, b, n, sem_d, sem_s):
                e = ebt[s][:, 0:n]
                V.tensor_tensor(ohd[s][:, 0:n, 0, :], iota_f[0:P, bass.ds(b * WB, WB)].unsqueeze(1).to_broadcast([P, n, WB]),
                                e[:, :, 1:2].to_broadcast([P, n, WB]), ALU.is_equal).then_inc(S(sem_d), 1)
                for t in range(n):
                    ins = V.tensor_scalar(ohs[s][:, t, 0:2 * HN], iota_h[0:P, 0:2 * HN], e[:, t, 0:1], None, ALU.is_equal)
                ins.then_inc(S(sem_s), 1)

            def block_onehots(i, q, first):
                b = 2 * i + q
                dve.wait_ge(*reached(f"edge_run_loaded{q}", 16 * i + 16))
                if not first:
                    dve.wait_ge(*reached("acc_ready", b - 1))
                onehots(q, b, CH, "ohd_ready", "ohs_ready")

            block_onehots(0, 0, True)
            block_onehots(0, 1, True)
            dve.wait_ge(*reached("proj_loaded", 16 * PROJ))
            fold(w_l0a, 4, 0)
            V.nop().then_inc(S("l0a_folded"), 1)
            ones("l0a", 4)
            with dve.Fori(1, NBLK // 2) as i:
                for q in range(2):
                    block_onehots(i, q, False)
            dve.wait_ge(*reached("total_sum", 1))
            step(V.tensor_reduce(flagf[:, 0:1], psE[0:1, 0:NBLK], AX, ALU.add))
            step(V.tensor_scalar(flagf[:, 1:2], flagf[:, 0:1], float(E), None, ALU.not_equal))
            V.tensor_copy(flag_i[:, 0:1], flagf[:, 1:2]).then_inc(S("flag_ready"), 1)
            dve.wait_ge(*reached("flag_ready", 1))
            missed = dve.value_load(flag_i[0:1, 0:1], min_val=0, max_val=1)
            with dve.If(missed == 1):
                V.memset(ct[:], 0.0)
                V.memset(wt[:], 0.0).then_inc(S("all_zeroed"), 1)
                dve.wait_ge(*reached("all_zeroed", 1))
                with dve.Fori(0, NBLK) as b:
                    with dve.Fori(0, NCHUNK) as c:
                        n = b * NCHUNK + c
                        dve.wait_ge(*reached("all_loaded", 16 * n + 16))
                        onehots(0, b, CHA, "all_ohd", "all_ohs")
                        dve.wait_ge(*reached("all_split", n + 1))
                        dve.wait_ge(*reached("all_added", n + 1))
                        ps = psC[0:P, 0:NT * 2 * WB].rearrange("p (j c) -> p j c", c=2 * WB)
                        cb, wb = ct[:, :, bass.ds(b * WB, WB)], wt[:, :, bass.ds(b * WB, WB)]
                        V.tensor_tensor(cb, ps[:, :, 0:WB], cb, ALU.add)
                        V.tensor_tensor(wb, ps[:, :, WB:], wb, ALU.add).then_inc(S("all_added"), 1)
                dve.wait_ge(*reached("all_added", NBLK * NCHUNK + 1))
                V.tensor_copy(at[:], ct[:]).then_inc(S("all_zeroed"), 1)
                dve.wait_ge(*reached("all_zeroed", 2))
            with dve.Else():
                V.nop()
            V.nop().then_inc(S("graph_ready"), 1)
            for j in range(NT):
                ins = V.tensor_tensor(at[:, j, j * P:(j + 1) * P], ct[:, j, j * P:(j + 1) * P], ident[0:P, 0:P], ALU.add)
            ins.then_inc(S("at_ready"), 1)
            dve.wait_ge(*reached("params_turned", 1))
            V.tensor_scalar(bnT[:, 4], bnT[:, 4], BN_EPS, None, ALU.add)
            V.tensor_scalar(bnT[:, 9], bnT[:, 9], BN_EPS, None, ALU.add).then_inc(S("bn_var_ready"), 1)
            for j in range(NT):
                dve.wait_ge(*reached("at_turned", j + 1))
                V.tensor_scalar(cols(negm[:, j, :]), (psA, psB)[j % 2][0:P, 0:NT, 0:P], 0.5, NEG, ALU.is_lt, ALU.mult)\
                    .then_inc(S("negm_done"), 1)

            def attention(tag, heads, write, between=None):
                ald = al[:, :, heads:2 * heads]

                def maxima(h):
                    dve.wait_ge(*reached(tag + "_bc", h + 1))
                    for j in range(NT):
                        n = h * NT + j
                        if n >= 2:
                            dve.wait_ge(*reached(tag + "_masked", n - 1))
                        V.tensor_tensor_reduce(out=cols(unused[j % 2]), in0=psEF[0:P, 0:NT, 0:P],
                                               in1=cols(negm[:, j, :]), scale=1.0, scalar=NEG, op0=ALU.add,
                                               op1=ALU.max, accum_out=mx[:, j, h:h + 1]).then_inc(S(tag + "_masked"), 1)
                    if h == 0:
                        dve.wait_ge(*reached(tag + "_al", NT))
                        V.tensor_scalar(al2[:, :, 0:heads], al[:, :, 0:heads], SLOPE, None, ALU.mult)
                    dve.wait_ge(*reached(tag + "_masked", (h + 1) * NT))
                    z, m, d = zz[:, :, h], mx[:, :, h], ald[:, :, h]
                    step(V.tensor_tensor(z, m, d, ALU.add))
                    step(V.scalar_tensor_tensor(out=m, in0=z, scalar=SLOPE, in1=z, op0=ALU.mult, op1=ALU.max))
                    V.tensor_tensor(r1[:, :, h], d, m, ALU.subtract)
                    V.scalar_tensor_tensor(out=r2[:, :, h], in0=d, scalar=SLOPE, in1=m, op0=ALU.mult, op1=ALU.subtract)\
                        .then_inc(S(tag + "_rows"), 1)

                for h in range(min(heads, 2)):
                    maxima(h)
                if between is not None:
                    between()

                def larger(h, i):
                    dve.wait_ge(*reached(tag + "_v", h * NT + i + 1))
                    V.tensor_tensor(u[h % 2][:, i, :], u[h % 2][:, i, :], v[:, i, :], ALU.max).then_inc(S(tag + "_max"), 1)

                for h in range(heads):
                    dve.wait_ge(*reached(tag + "_u", (h + 1) * NT))
                    larger(h, 0)
                    for i in range(NT):
                        if i + 1 < NT:
                            larger(h, i + 1)
                        dve.wait_ge(*reached(tag + "_max", h * NT + i + 1))
                        V.scalar_tensor_tensor(out=u[h % 2][:, i, :], in0=u[h % 2][:, i, :], scalar=1.0, in1=at[:, i, 0:N],
                                               op0=ALU.min, op1=ALU.mult).then_inc(S(tag + "_p"), 1)
                    if h >= 1:
                        write(h - 1)
                    if h + 2 < heads:
                        maxima(h + 2)
                write(heads - 1)

            def write_head(tag):
                def write(h):
                    dve.wait_ge(*reached(tag + "_agg", (h + 1) * NT))
                    if h >= 1:
                        dve.wait_ge(*reached(tag + "_out", h))
                    ps = (psC, psD)[h % 2][0:P, 0:NT * 65].rearrange("p (j c) -> p j c", c=65)
                    if tag == "l2a":
                        step(V.tensor_scalar(rden, ps[:, :, 64], 1e-16, None, ALU.add))
                        step(V.reciprocal(rden, rden))
                        for j in range(NT):
                            ins = V.scalar_tensor_tensor(out=gat[:, j, h * 64:(h + 1) * 64], in0=ps[:, j, 0:64],
                                                         scalar=rden[:, j:j + 1], in1=l2_bias[:, h * 64:(h + 1) * 64],
                                                         op0=ALU.mult, op1=ALU.add)
                        ins.then_inc(S(tag + "_out"), 1)
                        return
                    step(V.reciprocal(rden, ps[:, :, 64]))
                    V.tensor_tensor(gat[:, :, h * 64:(h + 1) * 64], ps[:, :, 0:64],
                                    rden.unsqueeze(2).to_broadcast([P, NT, 64]), ALU.mult).then_inc(S(tag + "_out"), 1)
                return write

            def write_l0b(h):
                for j in range(NT):
                    dve.wait_ge(*reached("l0b_agg", NT if j < NT - 1 else NT + 1))
                    ps = (psC, psD, psE, psF, last_out)[j]
                    step(V.reciprocal(rden[:, j:j + 1], ps[0:P, D:D + 1]))
                    V.scalar_tensor_tensor(out=x[:, j, :], in0=ps[0:P, 0:D], scalar=rden[:, j:j + 1], in1=x[:, j, :],
                                           op0=ALU.mult, op1=ALU.add).then_inc(S("l0b_out"), 1)
                    dve.wait_ge(*reached("l0b_out", j + 1))
                    ins = stats(j, x)
                step(ins)

            def add_row(dst, src, rowv):
                return V.tensor_tensor(dst, src, rowv.unsqueeze(1).to_broadcast([P, NT, D]), ALU.add)

            add_row(x[:], x[:], b2_l0b[:]).then_inc(S("row_added"), 1)
            dve.wait_ge(*reached("row_added", 1))
            attention("l0a", 4, write_head("l0a"))
            dve.wait_ge(*reached("l0a_out", 4))
            V.nop().then_inc(S("l0a_done"), 1)
            fold(w_l0b, 1, 2)
            V.nop().then_inc(S("l0b_folded"), 1)
            ones("l0b", 1)

            def between():
                fold(w_l2, 4, 4)
                V.nop().then_inc(S("params_used"), 1)
                step(V.tensor_reduce(outdeg, ct[:], AX, ALU.add))

            attention("l0b", 1, write_l0b, between)
            dve.wait_ge(*reached("l0b_out", NT))
            V.memset(zrow, 0.0).then_inc(S("zrow_ready"), 1)

            def top(tag, lgt):
                for j in range(NT):
                    ins = V.max(mx8[:, j, :], lgt[:, j, :])
                step(ins)
                indices(lgt)

            def indices(lgt):
                for j in range(NT):
                    ins = V.max_index(ix8[:, j, :], mx8[:, j, :], lgt[:, j, :])
                step(ins)
                step(V.tensor_copy(ixf, ix8[:, :, 0:2]))

            def onehot(dst, col, ne):
                return V.tensor_tensor(dst, iota_f[0:P, 0:ne].unsqueeze(1).to_broadcast([P, NT, ne]),
                                       ixf[:, :, col:col + 1].to_broadcast([P, NT, ne]), ALU.is_equal)

            def bias_rows(tag, each):
                dve.wait_ge(*reached(tag + "_wturned", 1))
                V.tensor_copy(cols(wgT), psEF[0:8, 0:NT, 0:P]).then_inc(S(tag + "_wT"), 1)
                for j in range(NT):
                    dve.wait_ge(*reached(tag + "_bias", j + 1))
                    each(j, (psE, psF)[j % 2][0:P, 0:D]).then_inc(S(tag + "_bias_out"), 1)

            normalise("l0f", x, xln, "l0f_xln", True)
            turned("l0f")
            dve.wait_ge(*reached("l0f_logits", 1))
            step(V.tensor_tensor(lg8, psC[0:P, 0:NT * E0].rearrange("p (j e) -> p j e", e=E0),
                                 rbias[:, 0:E0].unsqueeze(1).to_broadcast([P, NT, E0]), ALU.add))
            top("l0", lg8)
            step(onehot(oh0, 0, E0))
            V.tensor_copy(ohb0, oh0).then_inc(S("l0f_onehot"), 1)
            V.tensor_tensor(lg8, lg8, mx8[:, :, 0:1].to_broadcast([P, NT, E0]), ALU.subtract)\
                .then_inc(S("shift0_ready"), 1)
            dve.wait_ge(*reached("l0_ranks", 1))
            step(V.tensor_tensor(t0, psD[0:P, 0:NT * E0].rearrange("p (j e) -> p j e", e=E0), oh0, ALU.mult))
            step(V.tensor_reduce(scol[:, :, 0], t0, AX, ALU.add))
            step(V.tensor_scalar(scol[:, :, 1], scol[:, :, 0], CAP + 0.5, None, ALU.is_lt))
            step(V.tensor_scalar(scol[:, :, 0], scol[:, :, 0], float(CAP), -1.0, ALU.min, ALU.add))
            step(V.scalar_tensor_tensor(out=scol[:, :, 0], in0=ixf[:, :, 0], scalar=float(CAP), in1=scol[:, :, 0],
                                        op0=ALU.mult, op1=ALU.add))
            step(V.tensor_copy(sloti[:, :, 1], scol[:, :, 0]))
            step(V.scalar_tensor_tensor(out=scol[:, :, 2], in0=tokid, scalar=float(E0 * CAP), in1=scol[:, :, 0],
                                        op0=ALU.add, op1=ALU.subtract))
            step(V.tensor_scalar(zz[:, :, 0], scol[:, :, 1], -1.0, 1.0, ALU.mult, ALU.add))
            step(V.tensor_tensor(scol[:, :, 2], scol[:, :, 2], zz[:, :, 0], ALU.mult))
            step(V.tensor_tensor(scol[:, :, 2], scol[:, :, 2], scol[:, :, 0], ALU.add))
            V.tensor_copy(sloti[:, :, 0], scol[:, :, 2]).then_inc(S("slots0_ready"), 1)
            dve.wait_ge(*reached("exp0_ready", 1))
            step(V.tensor_reduce(zz[:, :, 0], ex8, AX, ALU.add))
            step(V.reciprocal(zz[:, :, 0], zz[:, :, 0]))
            step(V.tensor_tensor(rden, zz[:, :, 0], scol[:, :, 1], ALU.mult))
            bias_rows("l0f", lambda j, ps: V.tensor_scalar(clip[:, j, :], ps, rden[:, j:j + 1], None, ALU.mult))
            dve.wait_ge(*reached("bn_pow_ready", 1))
            for n in (0, 5):
                b_, g_, be_, m_, v_ = (bnT[:, n + i] for i in range(5))
                step(V.tensor_tensor(g_, g_, v_, ALU.mult))
                step(V.tensor_tensor(b_, b_, m_, ALU.subtract))
                step(V.tensor_tensor(b_, b_, g_, ALU.mult))
                step(V.tensor_tensor(be_, be_, b_, ALU.add))
            V.nop().then_inc(S("bn_ready"), 1)
            dve.wait_ge(*reached("bufs_turned1", 1))
            V.tensor_copy(bufT[:, 1, :].rearrange("p (e c) -> p e c", e=E0), psB[:, :, 0:CAP]).then_inc(S("bufT1"), 1)
            V.nop().then_inc(S("l0_y_free"), 2)
            V.nop().then_inc(S("l0_relu"), F0 // 128)
            with dve.Fori(0, 2) as r:
                for q in range(4):
                    e = 4 * r + q
                    dve.wait_ge(*reached("l0_y", e + 1))
                    V.tensor_copy(ysb[:, bass.ds(e, 1), :].rearrange("p a d -> p (a d)"), (psC, psD)[q % 2][0:CAP, 0:D])\
                        .then_inc(S("l0_y_free"), 1)
            dve.wait_ge(*reached("l0_tokens_back", 16 * NT))
            for j in range(NT):
                ins = V.scalar_tensor_tensor(out=yg0[:, j, :], in0=yg0[:, j, :], scalar=rden[:, j:j + 1],
                                             in1=clip[:, j, :], op0=ALU.mult, op1=ALU.add)
            step(ins)
            step(V.tensor_scalar(clip, yg0, 1e4, -1e4, ALU.min, ALU.max))
            step(V.tensor_tensor(nan_m, yg0, yg0, ALU.not_equal))
            step(V.tensor_scalar(bound, yg0, FLT_MAX, -FLT_MAX, ALU.min, ALU.max))
            step(V.tensor_tensor(inf_m, bound, yg0, ALU.not_equal))
            step(V.copy_predicated(yg0, inf_m, clip))
            step(V.copy_predicated(yg0, nan_m, zrow.unsqueeze(1).to_broadcast([P, NT, D])))
            V.tensor_scalar(outdeg, outdeg, 1.0, None, ALU.max)
            dve.wait_ge(*reached("indeg_sum", 1))
            V.tensor_scalar(ndst, psE[0:P, 0:NT], 1.0, None, ALU.max).then_inc(S("deg_ready"), 1)
            step(V.tensor_tensor(x[:], x[:], yg0, ALU.add))
            normalise("l1g", x, xln, "l1g_xln")
            turned("l1g")
            dve.wait_ge(*reached("ndst_turned", 1))
            V.tensor_copy(cols(ndst_row), psEF[0:64, 0:NT, 0:P]).then_inc(S("ndst_row_ready"), 1)
            dve.wait_ge(*reached("b_out_loaded", 16))
            step(add_row(x[:], x[:], b_out[:]))
            dve.wait_ge(*reached("gcn_agg", 1))
            dve.wait_ge(*reached("ndst_row_ready", 1))
            V.tensor_tensor(cols(scaled), psA[0:64, 0:NT, 0:P], cols(ndst_row), ALU.mult).then_inc(S("gcn_scaled"), 1)
            for j in range(NT):
                dve.wait_ge(*reached("gcn_y", j + 1))
                V.tensor_tensor(x[:, j, :], (psC, psD)[j % 2][0:P, 0:D], x[:, j, :], ALU.add).then_inc(S("gcn_out"), 1)
                dve.wait_ge(*reached("gcn_out", j + 1))
                ins = stats(j, x)
            step(ins)
            normalise("l1f", x, xln, "l1f_xln", True)
            turned("l1f")
            dve.wait_ge(*reached("l1f_logits", 1))
            step(V.tensor_tensor(lg, psC[0:P, 0:NT * E1].rearrange("p (j e) -> p j e", e=E1),
                                 rbias[:, E0:E0 + E1].unsqueeze(1).to_broadcast([P, NT, E1]), ALU.add))
            top("l1", lg)
            V.tensor_tensor(gsel[:, :, 0], mx8[:, :, 1], mx8[:, :, 0], ALU.subtract).then_inc(S("shift1_ready"), 1)
            onehot(oh1[:, 0:NT, :], 0, E1)
            step(onehot(oh1[:, NT:, :], 1, E1))
            V.tensor_tensor(ohb1, oh1[:, 0:NT, :], oh1[:, NT:, :], ALU.add).then_inc(S("l1f_onehot"), 1)
            dve.wait_ge(*reached("l1_ranks", 1))
            V.tensor_copy(cntcol, psF[0:E1, 0:1]).then_inc(S("cntcol_ready"), 1)
            V.tensor_copy(pos1, psD[0:P, 0:NT * E1].rearrange("p (j e) -> p j e", e=E1))
            V.tensor_copy(cntb, psE[0:P, 0:E1])
            dve.wait_ge(*reached("l1_offsets", 1))
            step(V.tensor_copy(offb, psC[0:P, 0:E1]))
            step(V.tensor_tensor(pos1, pos1, offb.unsqueeze(1).to_broadcast([P, NT, E1]), ALU.add))
            for k in range(2):
                step(V.tensor_tensor(t1, pos1, oh1[:, k * NT:(k + 1) * NT, :], ALU.mult))
                step(V.tensor_reduce(scol[:, :, k], t1, AX, ALU.add))
                step(V.tensor_scalar(scol[:, :, k], scol[:, :, k], -1.0, None, ALU.add))
                ins = V.tensor_copy(sloti[:, :, k], scol[:, :, k])
                if k == 0:
                    ins.then_inc(S("slots1_first"), 1)
            ins.then_inc(S("slots1_ready"), 1)
            dve.wait_ge(*reached("exp1_ready", 1))
            step(V.tensor_scalar(gsel[:, :, 0], gsel[:, :, 1], 1.0, None, ALU.add))
            step(V.reciprocal(gsel[:, :, 0], gsel[:, :, 0]))
            step(V.tensor_tensor(gsel[:, :, 1], gsel[:, :, 1], gsel[:, :, 0], ALU.mult))
            for r in range(ROUNDS):
                ins = V.scalar_tensor_tensor(out=starts_f[:, :, r], in0=cntb[0:1, :], scalar=float(r * WIN),
                                             in1=offb[0:1, :], op0=ALU.min, op1=ALU.add)
            step(V.tensor_reduce(flagf[:, 2:3], cntb[0:1, :], AX, ALU.max))
            step(V.tensor_scalar(flagf[:, 3:4], flagf[:, 2:3], WIN + 0.5, None, ALU.is_gt))
            V.tensor_copy(starts, starts_f)
            V.memset(xsT[:, :, SLOTS:], 0.0)
            V.tensor_copy(flag2_i[:, 0:1], flagf[:, 3:4]).then_inc(S("flag2_ready"), 1)
            for g in range(2):
                dve.wait_ge(*reached("xs_turned", 2 * g + 2))
                V.tensor_copy(xsT[:, 1, g * N:(g + 1) * N].rearrange("p (j q) -> p j q", q=P), psB[:, 0:NT, 0:P])\
                    .then_inc(S("xsT_dve"), 1)
            dve.wait_ge(*reached("flag2_ready", 1))
            full = dve.value_load(flag2_i[0:1, 0:1], min_val=0, max_val=1)

            def out1(ps, e, start):
                for m in range(KD):
                    ins = V.tensor_scalar(yT[:, m, bass.ds(start, WIN)], ps[:, m, 0:WIN], b2T1[:, m, bass.ds(e, 1)], None,
                                          ALU.add)
                return ins

            V.nop().then_inc(S("l1_y_free"), 2)
            V.nop().then_inc(S("l1_used"), 2)
            V.nop().then_inc(S("l1_relu"), F1 // 128)
            V.nop().then_inc(S("any_y_free"), 1)
            V.nop().then_inc(S("any_expert_used"), 1)
            with dve.If(full == 1):
                with dve.Fori(0, E1) as e:
                    with dve.Fori(0, ROUNDS) as r:
                        n = e * ROUNDS + r
                        start = dve.value_load(starts[0:1, bass.ds(e, 1), bass.ds(r, 1)].rearrange("p a b -> p (a b)"),
                                               min_val=0, max_val=SLOTS)
                        dve.wait_ge(*reached("any_y", n + 1))
                        dve.wait_ge(*reached("any_y_free", n + 1))
                        out1(psA, e, start).then_inc(S("any_y_free"), 1)
                    V.nop().then_inc(S("any_expert_used"), 1)
                dve.wait_ge(*reached("any_y_free", E1 * ROUNDS + 1))
            with dve.Else():
                with dve.Fori(0, E1 // RING) as r:
                    for q in range(RING):
                        e = r * RING + q
                        start = dve.value_load(starts[0:1, bass.ds(e, 1), 0:1].rearrange("p a b -> p (a b)"),
                                               min_val=0, max_val=SLOTS)
                        dve.wait_ge(*reached("l1_used", e + 3))
                        dve.wait_ge(*reached("l1_y_free", e + 2))
                        out1((psA, psB)[q % 2], e, start).then_inc(S("l1_y_free"), 1)
                dve.wait_ge(*reached("l1_y_free", E1 + 2))
            V.nop().then_inc(S("yT_ready"), 1)
            V.nop().then_inc(S("l1_experts_done"), 1)
            for g in (1, 3):
                dve.wait_ge(*reached("ys_turned", g + 1))
                V.tensor_copy(xs[:, 2 * g:2 * g + 2, :].rearrange("p t (m d) -> p (t m) d", m=2), psB[0:P, 0:4, 0:128])\
                    .then_inc(S("ys_dve"), 1)
            for k in range(2):
                dve.wait_ge(*reached(f"l1_tokens_back{k}", 16 * NT))
                for j in range(NT):
                    ins = V.scalar_tensor_tensor(out=x[:, j, :], in0=yg1[:, k * NT + j, :], scalar=gsel[:, j, k:k + 1],
                                                 in1=x[:, j, :], op0=ALU.mult, op1=ALU.add)
                step(ins)
            normalise("l2g", x, xln, "l2g_xln")
            turned("l2g")
            ones("l2a", 4)

            def offset():
                dve.wait_ge(*reached("l2_rows_loaded", 48))
                step(add_row(x[:], x[:], l2_beta))

            attention("l2a", 4, write_head("l2a"), offset)
            dve.wait_ge(*reached("l2a_out", 4))
            normalise("l2n", gat, gat, "l2n_xln")
            dve.wait_ge(*reached("l2n_xln", NT))
            step(V.tensor_tensor(gat, gat, l2_gamma.unsqueeze(1).to_broadcast([P, NT, D]), ALU.mult))
            step(V.tensor_tensor(x[:], x[:], gat, ALU.add))

            def dense(tag, two):
                normalise(tag, x, xln, tag + "_xln", two)
                turned(tag)
                dve.wait_ge(*reached(tag + "_logits", 1))
                lps = psC[0:P, 0:NT * 8].rearrange("p (j e) -> p j e", e=8)
                if tag == "l2f":
                    step(V.tensor_tensor(lg8, lps, rbias[:, E0 + E1:].unsqueeze(1).to_broadcast([P, NT, E2]), ALU.add))
                else:
                    step(V.tensor_copy(lg8, lps))
                V.nop().then_inc(S(tag + "_y_free"), 2)
                for j in range(NT):
                    ins = V.max(mx8[:, j, :], lg8[:, j, :])
                step(ins)
                if two:
                    indices(lg8)
                V.tensor_tensor(lg8, lg8, mx8[:, :, 0:1].to_broadcast([P, NT, 8]), ALU.subtract).then_inc(S(tag + "_shift"), 1)
                if two:
                    onehot(t8, 0, 8)
                    step(onehot(wgt, 1, 8))
                    step(V.tensor_tensor(t8, t8, wgt, ALU.add))
                    step(V.tensor_tensor(x[:], x[:], xln[:], ALU.add))
                dve.wait_ge(*reached(tag + "_exp", 1))
                step(V.tensor_reduce(zz[:, :, 0], ex8, AX, ALU.add))
                step(V.reciprocal(zz[:, :, 0], zz[:, :, 0]))
                ins = V.tensor_tensor(wgt, ex8, zz[:, :, 0:1].to_broadcast([P, NT, 8]), ALU.mult)
                if two:
                    step(ins)
                    step(V.tensor_tensor(wgt, wgt, t8, ALU.mult))
                    step(V.tensor_reduce(zz[:, :, 0], wgt, AX, ALU.add))
                    step(V.tensor_scalar(zz[:, :, 0], zz[:, :, 0], 1e-12, None, ALU.max))
                    step(V.reciprocal(zz[:, :, 0], zz[:, :, 0]))
                    ins = V.tensor_tensor(wgt, wgt, zz[:, :, 0:1].to_broadcast([P, NT, 8]), ALU.mult)
                ins.then_inc(S(tag + "_w"), 1)
                dve.wait_ge(*reached(tag + "_w", 1))
                with dve.Fori(0, E2 // 2) as r:
                    for q in range(2):
                        for j in range(NT):
                            n = (2 * r + q) * NT + j
                            dve.wait_ge(*reached(tag + "_y", n + 1))
                            dve.wait_ge(*reached(tag + "_y_free", n + 1))
                            V.scalar_tensor_tensor(out=x[:, j, :], in0=(psC, psD)[(q * NT + j) % 2][0:P, 0:D],
                                                   scalar=wgt[:, j, bass.ds(2 * r + q, 1)], in1=x[:, j, :],
                                                   op0=ALU.mult, op1=ALU.add).then_inc(S(tag + "_y_free"), 1)
                dve.wait_ge(*reached(tag + "_y_free", E2 * NT + 2))
                bias_rows(tag, lambda j, ps: V.tensor_tensor(x[:, j, :], ps, x[:, j, :], ALU.add))
                dve.wait_ge(*reached(tag + "_bias_out", NT))

            dense("l2f", False)
            normalise("l3g", x, xln, "l3g_xln")
            turned("l3g")
            for j in range(NT):
                dve.wait_ge(*reached("l3_agg", j + 1))
                V.scalar_tensor_tensor(out=x[:, j, :], in0=(psC, psD)[j % 2][0:P, 0:D], scalar=0.0, in1=x[:, j, :],
                                       op0=ALU.max, op1=ALU.add).then_inc(S("l3_out"), 1)
                dve.wait_ge(*reached("l3_out", j + 1))
                ins = stats(j, x)
            step(ins)
            dense("l3f", True)


NAMES = ["x", "src", "dst", "edge_weight"] + ["L0_gnn_" + n for n in (
    "W1", "att_src1", "att_dst1", "b1", "W2", "att_src2", "att_dst2", "b2")] + ["L0_ffn_" + n for n in (
    "gate_w", "gate_b", "w1", "b1", "w2", "b2")] + ["L1_gnn_" + n for n in ("W_gcn", "b_gcn", "W_out", "b_out")] + [
    "L1_ffn_" + n for n in ("Wr", "br", "W1", "b1", "W2", "b2")] + ["L2_gnn_" + n for n in (
    "W", "att_src", "att_dst", "bias", "gamma", "beta")] + ["L2_ffn_" + n for n in (
    "Wr", "br", "W1", "b1", "g1", "be1", "m1", "v1", "W2", "b2", "g2", "be2", "m2", "v2", "Wo", "bo")] + [
    "L3_gnn_weight"] + ["L3_ffn_" + n for n in ("router_w", "w1", "b1", "w2", "b2")]


def kernel(**inputs):
    import numpy as np
    import concourse.bacc as bacc
    from concourse.bass_utils import run_bass_kernel_spmd

    nc = bacc.Bacc("TRN2", target_bir_lowering=False, num_devices=1)
    arrays, aps = {}, {}
    for name in NAMES:
        v = np.ascontiguousarray(inputs[name])
        arrays["in_" + name] = v
        aps[name] = nc.dram_tensor("in_" + name, v.shape, mybir.dt.from_np(v.dtype), kind="ExternalInput").ap()
    out = nc.dram_tensor("out_x", (N, D), F32, kind="ExternalOutput").ap()
    build(nc, aps, out)
    r = run_bass_kernel_spmd(nc, [arrays], core_ids=[0])
    return r.results[0]["out_x"]
```
